# Optimizing a Trainium2 kernel written in Bass

```python
import numpy as np
import jax
import jax.numpy as jnp

def _softmax(x, axis=-1):
    return jax.nn.softmax(x, axis=axis)

def _gelu(x):
    return jax.nn.gelu(x, approximate=True)

def _silu(x):
    return jax.nn.silu(x)

def _sigmoid(x):
    return jax.nn.sigmoid(x)

def _layernorm(x, axis=-1, eps=1e-05):
    m = jnp.mean(x, axis=axis, keepdims=True)
    v = jnp.var(x, axis=axis, keepdims=True)
    return (x - m) / jnp.sqrt(v + eps)

def _scatter_add(tgt, idx, src, axis=0):
    return tgt.at[idx].add(src)

def _segment_sum(src, seg, n):
    return jax.ops.segment_sum(src, seg, n)
kernel_name = 'mk_decoder_postln_d1_seqx_r8_0b9aef'

def setup_inputs(seed: int=0):
    np.random.seed(seed)
    _w = jnp.asarray

    def _rec_inputs():
        import jax
        import jax.numpy as jnp
        _rk = jax.random.key(seed)
        x = 7.22e-05 + 1 * jax.random.normal(jax.random.fold_in(_rk, 1), (16, 256, 128), jnp.float32)
        _lenS = 256 - jax.random.randint(jax.random.fold_in(_rk, 7), (16,), 0, max(1, 256 // 4) + 1, jnp.int32)
        _lenS2 = 1601 - jax.random.randint(jax.random.fold_in(_rk, 8), (16,), 0, max(1, 1601 // 4) + 1, jnp.int32)
        _ctx_1024P = jax.random.normal(jax.random.fold_in(_rk, 11), (16, 16, 128), jnp.float32)
        _ctx_1024c = jax.random.dirichlet(jax.random.fold_in(_rk, 511), 0.3 * jnp.ones((16,), jnp.float32), (16, 1601))
        _ctx_1024t = jnp.einsum('bsk,bkd->bsd', _ctx_1024c, _ctx_1024P)
        _ctx_1024t = _ctx_1024t * jax.lax.rsqrt(jnp.mean(jnp.square(_ctx_1024t)) + 1e-12) * 0.953939
        ctx_1024 = 4.13588e-05 + 0.999923 * (_ctx_1024t + 0.3 * jax.random.normal(jax.random.fold_in(_rk, 611), (16, 1601, 128), jnp.float32))
        return (x, ctx_1024)
    x, ctx_1024 = _rec_inputs()

    def _L0_attn_setup():
        import jax, jax.numpy as jnp
        import numpy as np
        D_MODEL = 128

        def bitlinear(x, weight):
            scale = jnp.clip(jnp.mean(jnp.abs(weight), axis=1, keepdims=True), 1e-05, None)
            w_q = jnp.clip(jnp.round(weight / scale), -1.0, 1.0)
            w = weight + jax.lax.stop_gradient(w_q * scale - weight)
            return x @ w.T

        def rmsnorm(x, w, eps=1e-06):
            return x * jax.lax.rsqrt(jnp.mean(x * x, axis=-1, keepdims=True) + eps) * w
        key = jax.random.key(seed)
        ks = jax.random.split(key, 6)
        D = D_MODEL
        std = np.sqrt(2.0 / D)
        return {'x': jax.random.normal(ks[0], (4, 512, D), dtype=jnp.float32), 'Wr': jax.random.normal(ks[1], (D, D), dtype=jnp.float32) * std, 'Wk': jax.random.normal(ks[2], (D, D), dtype=jnp.float32) * std, 'Wv': jax.random.normal(ks[3], (D, D), dtype=jnp.float32) * std, 'Wo': jax.random.normal(ks[4], (D, D), dtype=jnp.float32) * std, 'decay': jnp.ones((D,), dtype=jnp.float32) * 0.99, 'ln_w': jnp.ones((D,), dtype=jnp.float32)}
    _L0_attn_all = _L0_attn_setup()
    _L0_attn_in = {k: v for k, v in _L0_attn_all.items() if k in ('Wr', 'Wk', 'Wv', 'Wo', 'decay', 'ln_w')}
    del _L0_attn_all

    def _L0_xattn_setup():
        import jax, jax.numpy as jnp
        import numpy as np
        B, LQ, LK = (4, 256, 256)
        DIM = 128
        H, D = (16, 64)
        AD = H * D
        SCALE = 1.0 / np.sqrt(D).astype(np.float32)
        key = jax.random.key(seed)
        ks = jax.random.split(key, 12)
        init = lambda k, shape, fan_in: jax.random.normal(k, shape, jnp.float32) / np.sqrt(fan_in).astype(np.float32)
        return {'x': jax.random.normal(ks[0], (B, LQ, DIM), jnp.float32), 'embeds': jax.random.normal(ks[1], (B, LK, DIM), jnp.float32), 'Wq': init(ks[2], (DIM, AD), DIM), 'bq': jnp.zeros((AD,), jnp.float32), 'Wk': init(ks[3], (DIM, AD), DIM), 'bk': jnp.zeros((AD,), jnp.float32), 'Wv': init(ks[4], (DIM, AD), DIM), 'bv': jnp.zeros((AD,), jnp.float32), 'Wo': init(ks[5], (AD, DIM), AD), 'bo': jnp.zeros((DIM,), jnp.float32)}
    _L0_xattn_all = _L0_xattn_setup()
    _L0_xattn_in = {k: v for k, v in _L0_xattn_all.items() if k in ('Wq', 'bq', 'Wk', 'bk', 'Wv', 'bv', 'Wo', 'bo')}
    del _L0_xattn_all

    def _L0_ffn_setup():
        import math
        import jax, jax.numpy as jnp
        import numpy as np
        B, S, D, F, E = (8, 256, 128, 512, 8)
        CAPACITY_FACTOR = 1.0
        key = jax.random.key(seed)
        k1, k2, k3, k4 = jax.random.split(key, 4)
        x = jax.random.normal(k1, (B, S, D), dtype=jnp.float32)
        Wr = jax.random.normal(k2, (D, E), dtype=jnp.float32) * (1.0 / math.sqrt(D))
        W1 = jax.random.normal(k3, (E, D, F), dtype=jnp.float32) * (1.0 / math.sqrt(D))
        W2 = jax.random.normal(k4, (E, F, D), dtype=jnp.float32) * (1.0 / math.sqrt(F))
        return {'x': x, 'Wr': Wr, 'W1': W1, 'W2': W2}
    _L0_ffn_all = _L0_ffn_setup()
    _L0_ffn_in = {k: v for k, v in _L0_ffn_all.items() if k in ('Wr', 'W1', 'W2')}
    del _L0_ffn_all
    return {'x': x, 'ctx_1024': ctx_1024, 'L0_attn_Wr': _L0_attn_in['Wr'], 'L0_attn_Wk': _L0_attn_in['Wk'], 'L0_attn_Wv': _L0_attn_in['Wv'], 'L0_attn_Wo': _L0_attn_in['Wo'], 'L0_attn_decay': _L0_attn_in['decay'], 'L0_attn_ln_w': _L0_attn_in['ln_w'], 'L0_xattn_Wq': _L0_xattn_in['Wq'], 'L0_xattn_bq': _L0_xattn_in['bq'], 'L0_xattn_Wk': _L0_xattn_in['Wk'], 'L0_xattn_bk': _L0_xattn_in['bk'], 'L0_xattn_Wv': _L0_xattn_in['Wv'], 'L0_xattn_bv': _L0_xattn_in['bv'], 'L0_xattn_Wo': _L0_xattn_in['Wo'], 'L0_xattn_bo': _L0_xattn_in['bo'], 'L0_ffn_Wr': _L0_ffn_in['Wr'], 'L0_ffn_W1': _L0_ffn_in['W1'], 'L0_ffn_W2': _L0_ffn_in['W2']}

def reference(x, ctx_1024, L0_attn_Wr, L0_attn_Wk, L0_attn_Wv, L0_attn_Wo, L0_attn_decay, L0_attn_ln_w, L0_xattn_Wq, L0_xattn_bq, L0_xattn_Wk, L0_xattn_bk, L0_xattn_Wv, L0_xattn_bv, L0_xattn_Wo, L0_xattn_bo, L0_ffn_Wr, L0_ffn_W1, L0_ffn_W2):
    import jax
    import jax.numpy as jnp

    def _L0_attn_ref(x, Wr, Wk, Wv, Wo, decay, ln_w):
        import jax, jax.numpy as jnp
        import numpy as np
        D_MODEL = 128

        def bitlinear(x, weight):
            scale = jnp.clip(jnp.mean(jnp.abs(weight), axis=1, keepdims=True), 1e-05, None)
            w_q = jnp.clip(jnp.round(weight / scale), -1.0, 1.0)
            w = weight + jax.lax.stop_gradient(w_q * scale - weight)
            return x @ w.T

        def rmsnorm(x, w, eps=1e-06):
            return x * jax.lax.rsqrt(jnp.mean(x * x, axis=-1, keepdims=True) + eps) * w
        B, T, D = x.shape
        r = jax.nn.sigmoid(bitlinear(x, Wr))
        k = bitlinear(x, Wk)
        v = bitlinear(x, Wv)
        dec = jax.nn.sigmoid(decay)
        kv = k * v
        positions = jnp.arange(T, dtype=x.dtype)
        log_decay = jnp.log(jnp.clip(dec, 1e-07, None))
        scale = jnp.exp(positions[:, None] * log_decay[None, :])
        scaled = kv / jnp.clip(scale, 1e-10, None)[None]
        cum = jnp.cumsum(scaled, axis=1)
        state = cum * scale[None]
        return bitlinear(rmsnorm(r * state, ln_w), Wo)

    def _L0_xattn_ref(x, embeds, Wq, bq, Wk, bk, Wv, bv, Wo, bo):
        import jax, jax.numpy as jnp
        import numpy as np
        B, LQ, LK = (4, 256, 256)
        DIM = 128
        H, D = (16, 64)
        AD = H * D
        SCALE = 1.0 / np.sqrt(D).astype(np.float32)
        b, lq, _ = x.shape
        lk = embeds.shape[1]
        q = (x @ Wq + bq).reshape(b, lq, H, D)
        k = (embeds @ Wk + bk).reshape(b, lk, H, D)
        v = (embeds @ Wv + bv).reshape(b, lk, H, D)
        scores = jnp.einsum('bqhd,bkhd->bhqk', q, k) * SCALE
        attn = jax.nn.softmax(scores, axis=-1)
        ctx = jnp.einsum('bhqk,bkhd->bqhd', attn, v).reshape(b, lq, AD)
        return ctx @ Wo + bo

    def _L0_ffn_ref(x, Wr, W1, W2):
        import math
        import jax, jax.numpy as jnp
        import numpy as np
        B, S, D, F, E = (8, 256, 128, 512, 8)
        CAPACITY_FACTOR = 1.0
        b, s, d = x.shape
        t = b * s
        cap = max(math.ceil(t * CAPACITY_FACTOR / E), 1)
        xf = x.reshape(t, d)
        probs = jax.nn.softmax(xf.astype(jnp.float32) @ Wr, axis=-1)
        eidx = jnp.argmax(probs, axis=-1)
        p_tok = jnp.take_along_axis(probs, eidx[:, None], axis=1)[:, 0]
        onehot = jax.nn.one_hot(eidx, E, dtype=jnp.int32)
        rank_all = jnp.cumsum(onehot, axis=0) - onehot
        rank = jnp.take_along_axis(rank_all, eidx[:, None], axis=1)[:, 0]
        keep = rank < cap
        slot = jnp.where(keep, rank, cap)
        dispatch = jnp.zeros((E, cap + 1), dtype=jnp.int32).at[eidx, slot].set(jnp.arange(t, dtype=jnp.int32))
        valid = jnp.zeros((E, cap + 1), dtype=bool).at[eidx, slot].set(keep)
        dispatch = dispatch[:, :cap]
        valid = valid[:, :cap]
        xe = xf[dispatch]
        h = jnp.maximum(jnp.einsum('ecd,edf->ecf', xe, W1), 0.0)
        ye = jnp.einsum('ecf,efd->ecd', h, W2)
        pe = p_tok[dispatch]
        ye = ye * (pe * valid.astype(ye.dtype))[:, :, None]
        y = jnp.zeros((t, d), dtype=x.dtype).at[dispatch.reshape(-1)].add(ye.reshape(E * cap, d).astype(x.dtype))
        return y.reshape(b, s, d)
    x = _layernorm(x + _L0_attn_ref(x, L0_attn_Wr, L0_attn_Wk, L0_attn_Wv, L0_attn_Wo, L0_attn_decay, L0_attn_ln_w), axis=-1)
    x = _layernorm(x + _L0_xattn_ref(x, ctx_1024, L0_xattn_Wq, L0_xattn_bq, L0_xattn_Wk, L0_xattn_bk, L0_xattn_Wv, L0_xattn_bv, L0_xattn_Wo, L0_xattn_bo), axis=-1)
    x = _layernorm(x + _L0_ffn_ref(x, L0_ffn_Wr, L0_ffn_W1, L0_ffn_W2), axis=-1)
    return x

_drawn_inputs = setup_inputs


def setup_inputs(seed=0):
    import zlib

    import numpy as np

    out = dict(_drawn_inputs(seed))
    spreads = {'L0_attn_decay': (0.9900000095367432, 0.2),
     'L0_attn_ln_w': (1.0, 0.2),
     'L0_xattn_bq': (0.0, 0.1),
     'L0_xattn_bk': (0.0, 0.1),
     'L0_xattn_bv': (0.0, 0.1),
     'L0_xattn_bo': (0.0, 0.1)}
    factors = {}
    for name, (base, spread) in spreads.items():
        noise = np.random.default_rng([zlib.crc32(name.encode()), seed]).standard_normal(out[name].shape)
        drawn = base * np.exp(spread * noise) if base else spread * noise
        out[name] = jnp.asarray(drawn.astype(out[name].dtype))
    for name, factor in factors.items():
        out[name] = (out[name] * factor).astype(out[name].dtype)
    return out
```

```python
from contextlib import ExitStack

import concourse.bass as bass
from concourse import mybir

P = 128
F32 = mybir.dt.float32
F32R = mybir.dt.float32r
I32 = mybir.dt.int32
ALU = mybir.AluOpType
ACT = mybir.ActivationFunctionType
AX = mybir.AxisListType


HELD = 1


class Chain:

    def __init__(self, eng, sem):
        self.eng, self.sem, self.base, self.steps = eng, sem, 0, 0

    def __call__(self, instruction):
        instruction.then_inc(self.sem, 1)
        self.steps += 1
        self.eng.wait_ge(self.sem, self.base + self.steps)

    def enter(self, turn, per_turn):
        self.start = self.base + self.steps
        self.base, self.steps, self.per_turn = self.start + turn * per_turn, 0, per_turn

    def leave(self, turns):
        assert self.steps == self.per_turn, (self.steps, self.per_turn)
        self.base, self.steps = self.start + turns * self.per_turn, 0


def decoder_layer(nc, x, ctx, Wr, Wk, Wv, Wo, decay, ln_w, xWq, xbq, xWk, xbk, xWv, xbv, xWo, xbo,
                  fWr, fW1, fW2, out):
    B, T, D = x.shape
    KEYS = ctx.shape[1]
    AD = xWq.shape[1]
    DH = 64
    H = AD // DH
    NJ = H // 2
    QT = T // P
    KT = -(-KEYS // P)
    KREM = KEYS - (KT - 1) * P
    NT = B * QT
    E = fWr.shape[1]
    F = fW1.shape[2]
    FC = F // P
    CAP = max(-(-B * T // E), 1)
    ST = CAP // P
    SLOTS = E * CAP
    AB = B // 2
    ATILES = 2 * QT
    AN = 2 * T
    SCALE = DH ** -0.5
    NG = NT // 4
    assert D == P and QT == 2 and H == 16 and CAP % P == 0 and B % 2 == 0 and ATILES == 4
    CH = (KEYS - 1) // 4
    assert 4 * CH + 1 == KEYS and CH % 2 == 0
    KEY0 = [0, CH, 2 * CH, 3 * CH]
    WID = [CH, CH, CH + 2, CH + 2]
    KPAD = KEYS + 1

    xe_dram = nc.dram_tensor("slots_in", [SLOTS, D], F32, kind="Internal").ap()
    ye_dram = nc.dram_tensor("slots_out", [SLOTS + 1, D], F32, kind="Internal").ap()

    with ExitStack() as stack:
        def sb(name, shape, dt=F32):
            return stack.enter_context(nc.sbuf_tensor(name, shape, dt))

        def sem(name):
            return stack.enter_context(nc.semaphore(name))

        ps = stack.enter_context(nc.psum_tensor("ps", [P, 8, 512], F32))

        ident = sb("ident", [P, P])
        ones = sb("ones", [P, P])
        tri = sb("tri", [P, P])
        iota8 = sb("iota8", [P, NT, E])
        minus_half = sb("minus_half", [P, 4])
        w_rows = sb("w_rows", [P, 4, P])
        w_tmp = sb("w_tmp", [P, 4, P])
        w_tern = sb("w_tern", [P, 4, P])
        w_T = sb("w_T", [P, 4, P])
        w_sum = sb("w_sum", [P, 4])
        w_scale = sb("w_scale", [P, 4])
        w_half = sb("w_half", [P, 4])
        w_nhalf = sb("w_nhalf", [P, 4])
        decay_c = sb("decay_c", [P, 1])
        dec = sb("dec", [P, 4])
        lnw_c = sb("lnw_c", [P, 1])
        scale_t = sb("scale_t", [P, 2, T])
        inv_scale = sb("inv_scale", [P, 2, T])
        half_scale = sb("half_scale", [P, 2, T])
        carry = sb("carry", [P, 2, T])
        wq_rows = sb("wq_rows", [P, AD])
        wk_rows = sb("wk_rows", [P, AD])
        wv_rows = sb("wv_rows", [P, AD])
        wo_rows = sb("wo_rows", [P, NJ, P])
        wq_T = sb("wq_T", [P, NJ, P])
        wk_T = sb("wk_T", [P, 2, NJ, P])
        bq_c = sb("bq_c", [P, NJ])
        bk_c = sb("bk_c", [P, NJ])
        bv_c = sb("bv_c", [P, NJ])
        bk_m = sb("bk_m", [P, NJ, 2])
        bo_b = sb("bo_b", [P, P])
        bo_all = sb("bo_all", [P, P])
        m_tab = sb("m_tab", [P, H, P])
        qb_tab = sb("qb_tab", [P, H])
        kb_tab = sb("kb_tab", [P, H])
        kb_const = sb("kb_const", [P, H])
        fwr_sb = sb("fwr_sb", [P, E])
        zeros = sb("zeros", [P, P])

        x_all = sb("x_all", [P, NT, P])
        x1T_all = sb("x1T_all", [P, B * T])
        r_all = sb("r_all", [P, NT, H])

        prob_T = sb("prob_T", [P, 2, KT, T])
        region = prob_T[:, :, :, :].rearrange("p h k t -> p (h k t)")
        xT, th, ksb, y, ysq, t2 = (region[:, n * AN:(n + 1) * AN] for n in range(6))
        t1 = region[:, NT * P:NT * P + AN] if NT * P > 6 * AN else region[:, 6 * AN:7 * AN]

        xs = sb("xs", [P, 4, P])
        hrow = sb("hrow", [P, 4, P])
        x1s = sb("x1s", [P, 4, P])
        x1Ts = sb("x1Ts", [P, AN])
        ms = sb("ms", [P, 4])
        rms = sb("rms", [P, 4])
        stats = sb("stats", [P, 4, 6])
        mv = sb("mv", [P, 4, 2])
        ve = sb("ve", [P, 4])
        rstd = sb("rstd", [P, 4])
        pad = sb("pad", [P, 1])

        ctx_raw = sb("ctx_raw", [P, KT, P])
        ctx_f = sb("ctx_f", [P, KEYS])
        ctx_hi = sb("ctx_hi", [P, KPAD], F32R)
        ctx_lo = sb("ctx_lo", [P, KPAD], F32R)
        x1T_cur = sb("x1T_cur", [P, T])
        m_cur = sb("m_cur", [P, 2, P])
        qb_cur = sb("qb_cur", [P, 2])
        q_hi = sb("q_hi", [P, 2, T], F32R)
        q_lo = sb("q_lo", [P, 2, T], F32R)
        r_cur = sb("r_cur", [P, QT, 2])
        prob = sb("prob", [P, 2, KT * P])
        v_pair = sb("v_pair", [P, KT, P])
        mx = sb("mx", [P, 2, 2])
        nmx = sb("nmx", [P, 2])
        nbias = sb("nbias", [P, 2])
        esum = sb("esum", [P, 4, 3])
        den = sb("den", [P, 4])
        rden = sb("rden", [P, 4])
        rspread = sb("rspread", [P, QT, P])
        rdT = sb("rdT", [P, QT, P])
        heads_T = sb("heads_T", [P, NJ, T])

        logit = sb("logit", [P, NT, E])
        lm = sb("lm", [P, NT, E])
        ex = sb("ex", [P, NT, E])
        one_hot = sb("one_hot", [P, NT, E])
        rk = sb("rk", [P, NT, E])
        tot = sb("tot", [P, E, NT])
        cmask = sb("cmask", [P, E, NT])
        csum = sb("csum", [P, E, NT])
        tmax = sb("tmax", [P, NT])
        tden = sb("tden", [P, NT])
        ptok = sb("ptok", [P, NT])
        vmin = sb("vmin", [P, NT])
        rank = sb("rank", [P, NT])
        keep = sb("keep", [P, NT])
        slot = sb("slot", [P, NT])
        dest = sb("dest", [P, NT], I32)
        w1_sb = sb("w1_sb", [P, 2, F])
        w2_sb = sb("w2_sb", [P, 2, FC, P])
        xe = sb("xe", [P, 2, ST, P])
        spare = prob[:, :, :].rearrange("p u k -> p (u k)")
        xeT = spare[:, 0:2 * CAP].rearrange("p (s c) -> p s c", s=2)
        assert B * T == 2 * FC * CAP
        hT = x1T_all[:, :].rearrange("p (s f c) -> p s f c", s=2, f=FC)
        ye = spare[:, 2 * CAP:4 * CAP].rearrange("p (s t n) -> p s t n", s=2, n=P)
        y_all = region[:, 0:NT * P].rearrange(
            "p (n d) -> p n d", n=NT)

        weights_in = sem("weights_in")
        consts_ready = sem("consts_ready")
        masks_ready = sem("masks_ready")
        slots_zeroed = sem("slots_zeroed")
        tern_ready = sem("tern_ready")
        decay_exp = sem("decay_exp")
        setup_tr = sem("setup_tr")
        setup_ev_act = sem("setup_ev_act")
        setup_ev_dve = sem("setup_ev_dve")
        setup_mm = sem("setup_mm")
        tables_act = sem("tables_act")
        tables_dve = sem("tables_dve")
        dve_own = sem("dve_own")
        pool_own = sem("pool_own")
        a_x = sem("a_x")
        a_xs_free = sem("a_xs_free")
        a_xT_ps = sem("a_xT_ps")
        a_xT = sem("a_xT")
        a_rkv = sem("a_rkv")
        a_gate = sem("a_gate")
        a_y = sem("a_y")
        a_ysq = sem("a_ysq")
        a_o = sem("a_o")
        a_var = sem("a_var")
        a_pow = sem("a_pow")
        a_x1 = sem("a_x1")
        a_x1_kept = sem("a_x1_kept")
        a_x1T_ps = sem("a_x1T_ps")
        a_x1T = sem("a_x1T")
        a_x1T_kept = sem("a_x1T_kept")
        a_r_ps = sem("a_r_ps")
        a_r = sem("a_r")
        ctx_in = sem("ctx_in")
        ctx_tr = sem("ctx_tr")
        ctx_hi_ok = sem("ctx_hi_ok")
        ctx_f_ok = sem("ctx_f_ok")
        ctx_lo_ok = sem("ctx_lo_ok")
        x1T_staged = sem("x1T_staged")
        m_staged = sem("m_staged")
        q_ps = sem("q_ps")
        q_hi_ok = sem("q_hi_ok")
        q_lo_ok = sem("q_lo_ok")
        scores = sem("scores")
        row_max = sem("row_max")
        exp_low = sem("exp_low")
        exp_high = sem("exp_high")
        ring_full = sem("ring_full")
        ring_act = sem("ring_act")
        ring_dve = sem("ring_dve")
        rden_ok = sem("rden_ok")
        pv_ok = sem("pv_ok")
        rdT_ok = sem("rdT_ok")
        norm_ok = sem("norm_ok")
        y_ps = sem("y_ps")
        y_read = sem("y_read")
        b_var = sem("b_var")
        b_pow = sem("b_pow")
        x2_ok = sem("x2_ok")
        c_staged = sem("c_staged")
        c_tr = sem("c_tr")
        c_xT = sem("c_xT")
        c_logit = sem("c_logit")
        c_logit_kept = sem("c_logit_kept")
        c_lm = sem("c_lm")
        c_exp = sem("c_exp")
        c_hot = sem("c_hot")
        c_rank_ps = sem("c_rank_ps")
        c_dest = sem("c_dest")
        c_scatter = sem("c_scatter")
        f_in = [sem(f"f_in{i}") for i in range(2)]
        f_tr = sem("f_tr")
        f_xT = sem("f_xT")
        f_h = sem("f_h")
        f_relu = sem("f_relu")
        f_y = sem("f_y")
        f_y_sb = sem("f_y_sb")
        f_out = sem("f_out")
        c_gather = sem("c_gather")
        g_var = sem("g_var")
        g_pow = sem("g_pow")
        g_ready = sem("g_ready")
        g_out = sem("g_out")

        V_TILES = [list(range(4 * c, min(4 * c + 4, KT))) for c in range(-(-KT // 4))]
        NC = len(V_TILES)
        assert NC == 4
        CHUNKS = ([("v", 0, 0), ("v", 0, 1)] + [("t", 0, c) for c in range(NC)] +
                  [("v", 0, 2), ("v", 0, 3)] + [("t", u, c) for u in (1, 2, 3) for c in range(NC)])
        OWNER = {}
        for i, (kind, u, c) in enumerate(CHUNKS):
            OWNER[i] = "act" if (kind == "v" and c == 0) or (kind == "t" and c in (0, 2)) else "dve"
        NRING = len(CHUNKS)
        RING_ACT = sum(OWNER[i] == "act" for i in range(NRING))
        RING_DVE = NRING - RING_ACT
        AT = {key: i for i, key in enumerate(CHUNKS)}

        def emptied(i):
            n = sum(OWNER[k] == "act" for k in range(i + 1))
            return n, i + 1 - n

        N_LOADS = 18
        C_IN = ctx.rearrange("b k d -> (b k) d")

        block = stack.enter_context(nc.Block())

        @block.sync
        def _(sp):
            for held in (f_out, g_out,):
                sp.sem_inc(held, HELD)
            def load(dst, src):
                sp.dma_start(dst, src).then_inc(weights_in, 16)

            for m, w in enumerate((Wr, Wk, Wv, Wo)):
                load(w_rows[:, m, :], w)
            load(decay_c[:, :], decay.rearrange("(d a) -> d a", a=1))
            load(lnw_c[:, :], ln_w.rearrange("(d a) -> d a", a=1))
            load(wq_rows[:, :], xWq)
            load(wk_rows[:, :], xWk)
            load(wv_rows[:, :], xWv)
            load(wo_rows[:, :, :], xWo.rearrange("(j p) n -> p j n", p=P))
            with nc.allow_non_contiguous_dma(reason="biases laid over the partitions, 4 KB each"):
                load(bq_c[:, :], xbq.rearrange("(j p) -> p j", p=P))
                load(bk_c[:, :], xbk.rearrange("(j p) -> p j", p=P))
                load(bv_c[:, :], xbv.rearrange("(j p) -> p j", p=P))
            load(bo_b[:, :], xbo.rearrange("(a n) -> a n", a=1).broadcast_to([P, P]))
            load(fwr_sb[:, :], fWr)
            sp.wait_ge(consts_ready, 1)
            for s in range(SLOTS // P):
                sp.dma_start(xe_dram[s * P:(s + 1) * P, :], zeros[:, :]).then_inc(slots_zeroed, 16)
            sp.dma_start(ye_dram[SLOTS:SLOTS + 1, :], zeros[0:1, :]).then_inc(slots_zeroed, 16)
            with sp.Fori(0, AB) as i:
                sp.wait_ge(a_xs_free, i + HELD)
                sp.dma_start(xs[:, :, :], x[bass.ds(i * 2, 2)].rearrange(
                    "b (t p) d -> p (b t) d", p=P)).then_inc(a_x, 16)
            with sp.Fori(0, B) as b:
                sp.wait_ge(ctx_tr, b * NC + HELD)
                rows = C_IN[bass.ds(b * KEYS, KEYS)]
                sp.dma_start(ctx_raw[:, 0:KT - 1, :], C_IN[bass.ds(b * KEYS, (KT - 1) * P)].rearrange(
                    "(t p) d -> p t d", p=P)).then_inc(ctx_in, 16)
                sp.dma_start(ctx_raw[0:KREM, KT - 1, :],
                             C_IN[bass.ds(b * KEYS + (KT - 1) * P, KREM)]).then_inc(ctx_in, 16)
            sp.wait_ge(c_scatter, 16 * NT)
            with sp.Fori(0, E // 2) as i:
                for s in range(2):
                    sp.wait_ge(f_y, i * 2 + HELD)
                    sp.dma_start(xe[:, s, :, :], xe_dram[bass.ds(i * (2 * CAP) + s * CAP, CAP)].rearrange(
                        "(t p) d -> p t d", p=P)).then_inc(f_in[s], 16)
                    sp.dma_start(w1_sb[:, s, :], fW1[bass.ds(i * 2 + s, 1)].rearrange(
                        "o d f -> (o d) f")).then_inc(f_in[s], 16)
                    sp.dma_start(w2_sb[:, s, :, :], fW2[bass.ds(i * 2 + s, 1)].rearrange(
                        "o (c p) d -> p (o c) d", p=P)).then_inc(f_in[s], 16)
                for s in range(2):
                    sp.wait_ge(f_y_sb, i * 2 + s + 1 + HELD)
                    sp.dma_start(ye_dram[bass.ds(i * (2 * CAP) + s * CAP, CAP)].rearrange(
                        "(t p) d -> p t d", p=P), ye[:, s, :, :]).then_inc(f_out, 16)
            with sp.Fori(0, NG) as g:
                sp.wait_ge(g_ready, g + 1)
                sp.dma_start(out[bass.ds(g * 2, 2)].rearrange("b (t p) d -> p (b t) d", p=P),
                             x1s[:, :, :]).then_inc(g_out, 16)
            sp.wait_ge(g_out, 16 * NG + HELD)

        @block.gpsimd
        def _(pool):
            for held in (a_x1_kept,):
                pool.sem_inc(held, HELD)
            own = Chain(pool, pool_own)
            nc.gpsimd.memset(zeros[:, :], 0.0).then_inc(consts_ready, 1)
            own(nc.gpsimd.memset(ident[:, :], 0.0))
            nc.gpsimd.affine_select(out=ident[:, :], in_=ident[:, :], compare_op=ALU.not_equal, fill=1.0,
                                    base=0, pattern=[[-1, P]], channel_multiplier=1).then_inc(masks_ready, 1)
            own(nc.gpsimd.memset(tri[:, :], 0.0))
            nc.gpsimd.affine_select(out=tri[:, :], in_=tri[:, :], compare_op=ALU.is_ge, fill=1.0,
                                    base=0, pattern=[[-1, P]], channel_multiplier=1).then_inc(masks_ready, 1)
            nc.gpsimd.memset(ones[:, :], 1.0).then_inc(masks_ready, 1)
            nc.gpsimd.memset(minus_half[:, :], -0.5).then_inc(masks_ready, 1)
            nc.gpsimd.iota(iota8[:, :, :], pattern=[[0, NT], [1, E]], base=0, channel_multiplier=0,
                           allow_small_or_imprecise_dtypes=True).then_inc(masks_ready, 1)
            own(nc.gpsimd.memset(v_pair[:, KT - 1, :], 0.0))
            own(nc.gpsimd.memset(prob[:, 0, :], 0.0))
            nc.gpsimd.memset(prob[:, 1, :], 0.0).then_inc(masks_ready, 1)
            pool.wait_ge(masks_ready, 4)

            def power(dst, src, ready, count, done):
                pool.wait_ge(ready, count)
                nc.gpsimd.tensor_tensor(dst, src, minus_half[:, 0:src.shape[-1]], ALU.pow).then_inc(done, 1)

            with pool.Fori(0, AB) as i:
                power(rms[:, :], ms[:, :], a_var, i * 2 + 1, a_pow)
                power(rstd[:, :], ve[:, :], a_var, i * 2 + 2, a_pow)
                pool.wait_ge(a_x1, i + 1)
                nc.gpsimd.tensor_copy(x_all[:, bass.ds(i * 4, 4), :], x1s[:, :, :]).then_inc(a_x1_kept, 1)

            def stage_tokens(b):
                pool.wait_ge(q_ps, b * NJ + HELD)
                nc.gpsimd.tensor_copy(x1T_cur[:, :], x1T_all[:, bass.ds(b * T, T)]).then_inc(x1T_staged, 1)

            def stage_pair(pair, j):
                pool.wait_ge(consts_ready, 1)
                pool.wait_ge(q_ps, pair + HELD)
                pool.wait_ge(q_hi_ok, pair + HELD)
                pool.wait_ge(q_lo_ok, pair + HELD)
                nc.gpsimd.tensor_copy(m_cur[:, :, :], m_tab[:, bass.ds(j * 2, 2), :]).then_inc(m_staged, 1)
                nc.gpsimd.tensor_copy(qb_cur[:, :], qb_tab[:, bass.ds(j * 2, 2)]).then_inc(m_staged, 1)

            pool.wait_ge(a_x1T_kept, AB + HELD)
            stage_tokens(0)
            with pool.Fori(0, NJ) as j:
                stage_pair(j, j)
            with pool.Fori(1, B) as b:
                stage_tokens(b)
                stage_pair(b * NJ, 0)
                power(rstd[:, 0:QT], ve[:, 0:QT], b_var, b, b_pow)
                with pool.Fori(1, NJ) as j:
                    stage_pair(b * NJ + j, j)
            stage_pair(B * NJ, 0)
            power(rstd[:, 0:QT], ve[:, 0:QT], b_var, B, b_pow)

            with pool.Fori(0, NG) as g:
                pool.wait_ge(x2_ok, B)
                pool.wait_ge(c_tr, g + HELD)
                nc.gpsimd.tensor_copy(hrow[:, :, :], x_all[:, bass.ds(g * 4, 4), :]).then_inc(c_staged, 1)

            pool.wait_ge(slots_zeroed, 16 * (SLOTS // P + 1))
            pool.wait_ge(c_dest, 1)
            for t in range(NT):
                nc.gpsimd.indirect_dma_start(
                    xe_dram[:, :], bass.IndirectOffsetOnAxis(ap=dest[:, t:t + 1], axis=0), x_all[:, t, :], None,
                    bounds_check=SLOTS - 1, oob_is_err=False).then_inc(c_scatter, 16)
            pool.wait_ge(f_out, 16 * E + HELD)
            for t in range(NT):
                nc.gpsimd.indirect_dma_start(
                    y_all[:, t, :], None, ye_dram[:, :], bass.IndirectOffsetOnAxis(ap=dest[:, t:t + 1], axis=0),
                    bounds_check=SLOTS, oob_is_err=False).then_inc(c_gather, 16)
            with pool.Fori(0, NG) as g:
                power(rstd[:, :], ve[:, :], g_var, g + 1, g_pow)

        @block.scalar
        def _(act):
            for held in (q_hi_ok, a_x1T_kept, ring_act, exp_low, exp_high, f_relu,):
                act.sem_inc(held, HELD)
            copy = nc.scalar.copy
            act.wait_ge(weights_in, 16 * 15)
            nc.scalar.activation(dec[:, 0:1], decay_c[:, :], ACT.Exp, scale=-1.0).then_inc(decay_exp, 1)
            act.wait_ge(setup_tr, 1)
            copy(w_T[:, 0:3, :], ps[:, 0, 0:3 * P].rearrange("p (m n) -> p m n", m=3)).then_inc(setup_ev_act, 1)
            act.wait_ge(setup_tr, 2)
            copy(wq_T[:, :, :], ps[:, 1:3, :].rearrange("p a (b n) -> p (a b) n", n=P)).then_inc(setup_ev_act, 1)
            act.wait_ge(setup_mm, 1)
            nc.scalar.mul(m_tab[:, :, :], ps[:, 0:4, :].rearrange("p a (b n) -> p (a b) n", n=P), SCALE)\
                .then_inc(tables_act, 1)

            with act.Fori(0, AB) as i:
                act.wait_ge(a_xT_ps, i + 1)
                copy(xT[:, :], ps[:, 0, :]).then_inc(a_xT, 1)
                act.wait_ge(a_rkv, i * 3 + 1)
                nc.scalar.activation(th[:, :], ps[:, 1, :], ACT.Tanh, scale=0.5).then_inc(a_gate, 1)
                act.wait_ge(a_rkv, i * 3 + 2)
                copy(ksb[:, :], ps[:, 2, :]).then_inc(a_gate, 1)
                act.wait_ge(a_y, i + 1)
                nc.scalar.activation(ysq[:, :], y[:, :], ACT.Square).then_inc(a_ysq, 1)
                act.wait_ge(a_x1T_ps, i + 1 + HELD)
                copy(x1Ts[:, :], ps[:, 6, :]).then_inc(a_x1T, 1)
                copy(x1T_all[:, bass.ds(i * AN, AN)], ps[:, 6, :]).then_inc(a_x1T_kept, 1)

            def query_high(n_pairs):
                act.wait_ge(q_ps, n_pairs + HELD)
                nc.scalar.activation(q_hi[:, 0, :], ps[:, 7, 0:T], ACT.Identity, bias=qb_cur[:, 0:1])
                nc.scalar.activation(q_hi[:, 1, :], ps[:, 7, T:2 * T], ACT.Identity, bias=qb_cur[:, 1:2])\
                    .then_inc(q_hi_ok, 1)

            act.wait_ge(m_staged, 2)
            query_high(1)
            with act.Fori(0, B) as b:
                for c, tiles in enumerate(V_TILES):
                    n = sum(P if k < KT - 1 else KREM for k in tiles)
                    k0 = tiles[0] * P
                    act.wait_ge(ctx_tr, b * NC + c + 1 + HELD)
                    copy(ctx_hi[:, k0:k0 + n], ps[:, 4 + c % 2, 0:n]).then_inc(ctx_hi_ok, 1)
                    copy(ctx_f[:, k0:k0 + n], ps[:, 4 + c % 2, 0:n]).then_inc(ctx_f_ok, 1)
                with act.Fori(0, NJ) as j:
                    pair = b * NJ + j

                    def ring(key):
                        i = AT[key]
                        if OWNER[i] != "act":
                            return
                        kind, u, c = key
                        act.wait_ge(ring_full, pair * NRING + i + 1)
                        src = ps[:, 4 + i % 2, :].rearrange("p (k n) -> p k n", n=P)
                        tiles = V_TILES[c]
                        if kind == "v":
                            copy(v_pair[:, tiles[0]:tiles[-1] + 1, :], src[:, 0:len(tiles), :])\
                                .then_inc(ring_act, 1)
                        else:
                            copy(prob_T[:, u % 2, tiles[0]:tiles[-1] + 1, u // 2 * P:u // 2 * P + P],
                                 src[:, 0:len(tiles), :]).then_inc(ring_act, 1)

                    def exps(u):
                        act.wait_ge(row_max, pair * 4 + u + 1)
                        bias = nbias[:, u % 2:u % 2 + 1]
                        nc.scalar.activation(prob[:, u % 2, 0:2 * CH].rearrange("p (a k) -> p a k", a=2),
                                             ps[:, 0:2, 0:CH], ACT.Exp, bias=bias,
                                             accum_out=esum[:, u, 0:1]).then_inc(exp_low, 1)
                        nc.scalar.activation(prob[:, u % 2, 2 * CH:3 * CH + 1], ps[:, 2, 0:CH + 1], ACT.Exp,
                                             bias=bias, accum_out=esum[:, u, 1:2]).then_inc(exp_high, 1)
                        nc.scalar.activation(prob[:, u % 2, 3 * CH + 1:KEYS], ps[:, 3, 1:CH + 1], ACT.Exp,
                                             bias=bias, accum_out=esum[:, u, 2:3]).then_inc(exp_high, 1)

                    def spread(qt):
                        act.wait_ge(pv_ok, pair * 2 + qt + 1)
                        copy(rdT[:, qt, :], ps[:, 6 + qt, P:2 * P]).then_inc(rdT_ok, 1)

                    ring(("v", 0, 0))
                    exps(0)
                    for c in range(NC):
                        ring(("t", 0, c))
                    exps(1)
                    for c in range(NC):
                        ring(("t", 1, c))
                    exps(2)
                    for c in range(NC):
                        ring(("t", 2, c))
                    exps(3)
                    act.wait_ge(scores, pair * 8 + 8)
                    act.wait_ge(m_staged, pair * 2 + 4)
                    query_high(pair + 2)
                    spread(0)
                    for c in range(NC):
                        ring(("t", 3, c))
                    spread(1)

            with act.Fori(0, NG) as g:
                act.wait_ge(c_tr, g + 1 + HELD)
                copy(x1Ts[:, :], ps[:, 0, :]).then_inc(c_xT, 1)
            act.wait_ge(c_lm, 1)
            nc.scalar.activation(ex[:, :, :], lm[:, :, :], ACT.Exp).then_inc(c_exp, 1)
            with act.Fori(0, E // 2) as i:
                for s in range(2):
                    act.wait_ge(f_tr, i * 2 + s + 1)
                    copy(xeT[:, s, :], ps[:, 0 + s, 0:CAP]).then_inc(f_xT, 1)
                    for f in range(FC):
                        act.wait_ge(f_h, i * (2 * FC) + s * FC + f + 1)
                        nc.scalar.activation(hT[:, s, f, :], ps[:, 2 + f, 0:CAP], ACT.Relu).then_inc(f_relu, 1)

        @block.vector
        def _(dve):
            for held in (a_xs_free, q_lo_ok, ring_dve, norm_ok, y_read, c_logit_kept, f_y_sb, a_r,):
                dve.sem_inc(held, HELD)
            own = Chain(dve, dve_own)
            v = nc.vector
            dve.wait_ge(weights_in, 16 * 15)
            own(v.tensor_reduce(w_sum[:, :], w_rows[:, :, :], AX.X, ALU.add, apply_absolute_value=True))
            own(v.tensor_scalar(w_scale[:, :], w_sum[:, :], 1.0 / D, 1e-5, ALU.mult, ALU.max))
            own(v.tensor_scalar(w_half[:, :], w_scale[:, :], 0.5, None, ALU.mult))
            own(v.tensor_scalar(w_nhalf[:, :], w_scale[:, :], -0.5, None, ALU.mult))
            for m in range(4):
                own(v.tensor_scalar(w_tmp[:, m, :], w_rows[:, m, :], w_half[:, m:m + 1], None, ALU.is_gt))
                own(v.scalar_tensor_tensor(w_tern[:, m, :], w_rows[:, m, :], w_nhalf[:, m:m + 1],
                                           w_tmp[:, m, :], ALU.is_lt, ALU.subtract))
                own(v.scalar_tensor_tensor(w_tmp[:, m, :], w_tern[:, m, :], w_scale[:, m:m + 1],
                                           w_rows[:, m, :], ALU.mult, ALU.add))
                v.tensor_tensor(w_tern[:, m, :], w_rows[:, m, :], w_tmp[:, m, :], ALU.subtract)\
                    .then_inc(tern_ready, 1)
            dve.wait_ge(decay_exp, 1)
            own(v.tensor_scalar(dec[:, 1:2], dec[:, 0:1], 1.0, None, ALU.add))
            own(v.reciprocal(dec[:, 2:3], dec[:, 1:2]))
            own(v.tensor_scalar(dec[:, 3:4], dec[:, 2:3], 1e-7, None, ALU.max))
            own(v.memset(carry[:, :, :], 0.0))
            own(v.memset(scale_t[:, :, 0:1], 1.0))
            own(v.tensor_tensor_scan(scale_t[:, 0, 1:T], dec[:, 3:4].broadcast_to([P, T - 1]), carry[:, 0, 1:T],
                                     1.0, ALU.mult, ALU.add))
            own(v.tensor_copy(scale_t[:, 1, :], scale_t[:, 0, :]))
            own(v.tensor_scalar(half_scale[:, :, :], scale_t[:, :, :], 0.5, None, ALU.mult))
            own(v.tensor_scalar(inv_scale[:, :, :], scale_t[:, :, :], 1e-10, None, ALU.max))
            own(v.reciprocal(scale_t[:, :, :], inv_scale[:, :, :]))
            own(v.tensor_copy(inv_scale[:, :, :], scale_t[:, :, :]))
            own(v.memset(carry[:, :, 1:T], 1.0))
            own(v.memset(wk_T[64:P, 0, :, :], 0.0))
            own(v.memset(wk_T[0:64, 1, :, :], 0.0))
            own(v.memset(bk_m[:, :, :], 0.0))
            own(v.memset(ctx_hi[:, KEYS:KPAD].bitcast(F32), 0.0))
            own(v.memset(ctx_lo[:, KEYS:KPAD].bitcast(F32), 0.0))
            own(v.tensor_copy(bk_m[0:64, :, 0], bk_c[0:64, :]))
            own(v.tensor_copy(bk_m[64:P, :, 1], bk_c[64:P, :]))
            dve.wait_ge(setup_tr, 1)
            dve.wait_ge(setup_ev_act, 1)
            v.tensor_scalar(w_T[:, 3, :], ps[:, 0, 3 * P:4 * P], lnw_c[:, :], None, ALU.mult)\
                .then_inc(setup_ev_dve, 1)
            dve.wait_ge(setup_tr, 3)
            v.tensor_copy(wk_T[0:64, 0, :, :], ps[0:64, 3:5, :].rearrange("p a (b n) -> p (a b) n", n=P))\
                .then_inc(setup_ev_dve, 1)
            v.tensor_copy(wk_T[64:P, 1, :, :], ps[64:P, 3:5, :].rearrange("p a (b n) -> p (a b) n", n=P))\
                .then_inc(setup_ev_dve, 1)
            dve.wait_ge(setup_mm, 2)
            v.tensor_scalar(qb_tab[:, :], ps[:, 5, 0:H], SCALE, None, ALU.mult).then_inc(tables_dve, 1)
            v.tensor_scalar(kb_tab[:, :], ps[:, 5, H:2 * H], SCALE, None, ALU.mult).then_inc(tables_dve, 1)
            v.tensor_scalar(kb_const[:, :], ps[:, 5, 2 * H:3 * H], SCALE, None, ALU.mult).then_inc(tables_dve, 1)
            v.tensor_tensor(bo_all[:, :], ps[:, 6, 0:P], bo_b[:, :], ALU.add).then_inc(tables_dve, 1)
            dve.wait_ge(tables_dve, 4)

            def carry_wait():
                v.memset(pad[:, :], 0.0)

            def moments(tiles):
                for t in range(tiles):
                    last = v.bn_stats(stats[:, t, :], hrow[:, t, :])
                own(last)
                carry_wait()
                for t in range(tiles):
                    last = v.bn_aggr(mv[:, t, :], stats[:, t, :])
                own(last)

            flat = lambda a: a[:, :, :].rearrange("p b t -> p (b t)")
            with dve.Fori(0, AB) as i:
                own.enter(i, 3 + 2)
                dve.wait_ge(a_gate, i * 2 + 2)
                dve.wait_ge(a_rkv, i * 3 + 3)
                own(v.tensor_tensor(t1[:, :], ksb[:, :], ps[:, 3, :], ALU.mult))
                own(v.tensor_tensor(t2[:, :], t1[:, :], flat(inv_scale), ALU.mult))
                own(v.tensor_tensor_scan(t1[:, :], flat(carry), t2[:, :], 0.0, ALU.mult, ALU.add))
                v.tensor_tensor(t2[:, :], t1[:, :], flat(half_scale), ALU.mult).then_inc(a_r, 1)
                dve.wait_ge(a_r, i * 3 + 1 + HELD)
                v.scalar_tensor_tensor(y[:, :], th[:, :], 1.0, t2[:, :], ALU.add, ALU.mult).then_inc(a_y, 1)
                dve.wait_ge(a_o, i * 2 + 2)
                v.tensor_scalar(ms[:, :], ps[:, 5, 0:4], 1.0 / D, 1e-6, ALU.mult, ALU.add).then_inc(a_var, 1)
                dve.wait_ge(a_pow, i * 2 + 1)
                for t in range(4):
                    last = v.scalar_tensor_tensor(hrow[:, t, :], ps[:, 4, t * P:t * P + P], rms[:, t:t + 1],
                                                  xs[:, t, :], ALU.mult, ALU.add)
                last.then_inc(a_xs_free, 1)
                dve.wait_ge(a_xs_free, i + 1 + HELD)
                moments(4)
                v.tensor_scalar(ve[:, :], mv[:, :, 1], 1e-5, None, ALU.add).then_inc(a_var, 1)
                dve.wait_ge(a_pow, i * 2 + 2)
                dve.wait_ge(a_x1_kept, i + HELD)
                dve.wait_ge(a_x1T_ps, i + HELD)
                for t in range(4):
                    last = v.tensor_scalar(x1s[:, t, :], hrow[:, t, :], mv[:, t, 0:1], rstd[:, t:t + 1],
                                           ALU.subtract, ALU.mult)
                    last.then_inc(a_x1, 1) if t == 3 else last.then_inc(a_r, 1) if t == 0 else None
                dve.wait_ge(a_r_ps, i + 1)
                v.tensor_tensor(r_all[:, bass.ds(i * 4, 4), :],
                                ps[:, 7, 0:4 * H].rearrange("p (t h) -> p t h", h=H),
                                kb_const[:, None, :].broadcast_to([P, 4, H]), ALU.add).then_inc(a_r, 1)
            own.leave(AB)
            dve.wait_ge(a_r, AB * 3 + HELD)

            def query_low(n_pairs):
                dve.wait_ge(q_hi_ok, n_pairs + HELD)
                for h in range(2):
                    last = v.scalar_tensor_tensor(q_lo[:, h, :], ps[:, 7, h * T:h * T + T], qb_cur[:, h:h + 1],
                                                  q_hi[:, h, :].bitcast(F32), ALU.add, ALU.subtract)
                last.then_inc(q_lo_ok, 1)

            dve.wait_ge(m_staged, 2)
            query_low(1)
            PAIR_STEPS = 1 + 4 * 2 + 2 * 2
            with dve.Fori(0, B) as b:
                for c, tiles in enumerate(V_TILES):
                    n = sum(P if k < KT - 1 else KREM for k in tiles)
                    k0 = tiles[0] * P
                    dve.wait_ge(ctx_f_ok, b * NC + c + 1)
                    v.tensor_tensor(ctx_lo[:, k0:k0 + n], ctx_f[:, k0:k0 + n],
                                    ctx_hi[:, k0:k0 + n].bitcast(F32), ALU.subtract).then_inc(ctx_lo_ok, 1)
                start = own.base + own.steps
                EPI = 1 + 2 + 1
                with dve.Fori(0, NJ) as j:
                    pair = b * NJ + j
                    own.base, own.steps = start + b * (NJ * PAIR_STEPS + EPI) + j * PAIR_STEPS, 0

                    def ring(key):
                        i = AT[key]
                        if OWNER[i] != "dve":
                            return
                        kind, u, c = key
                        dve.wait_ge(ring_full, pair * NRING + i + 1)
                        src = ps[:, 4 + i % 2, :].rearrange("p (k n) -> p k n", n=P)
                        tiles = V_TILES[c]
                        if kind == "v":
                            rows = KREM if tiles[-1] == KT - 1 else P
                            v.tensor_copy(v_pair[0:rows, tiles[0]:tiles[-1] + 1, :],
                                          src[0:rows, 0:len(tiles), :]).then_inc(ring_dve, 1)
                        else:
                            v.tensor_copy(prob_T[:, u % 2, tiles[0]:tiles[-1] + 1, u // 2 * P:u // 2 * P + P],
                                          src[:, 0:len(tiles), :]).then_inc(ring_dve, 1)

                    def maxima(u):
                        s = u % 2
                        dve.wait_ge(scores, pair * 8 + 2 * u + 1)
                        v.tensor_reduce(mx[:, s, 0:1], ps[:, 0:2, 0:CH], AX.XY, ALU.max)
                        dve.wait_ge(scores, pair * 8 + 2 * u + 2)
                        own(v.tensor_reduce(mx[:, s, 1:2], ps[:, 2:4, 0:CH + 1], AX.XY, ALU.max))
                        own(v.tensor_reduce(nmx[:, s:s + 1], mx[:, s, :], AX.X, ALU.max, negate=True))
                        r = r_cur[:, u // 2, u % 2:u % 2 + 1]
                        v.scalar_tensor_tensor(nbias[:, s:s + 1], nmx[:, s:s + 1], r, r, ALU.subtract,
                                               ALU.add).then_inc(row_max, 1)

                    def row_sums(qt):
                        dve.wait_ge(exp_high, pair * 8 + 4 * qt + 4 + HELD)
                        own(v.tensor_reduce(den[:, 2 * qt:2 * qt + 2], esum[:, 2 * qt:2 * qt + 2, :], AX.X, ALU.add))
                        own(v.reciprocal(rden[:, 2 * qt:2 * qt + 2], den[:, 2 * qt:2 * qt + 2]))
                        v.tensor_copy(rspread[:, qt, :].rearrange("p (h d) -> p h d", h=2),
                                      rden[:, 2 * qt:2 * qt + 2, None].broadcast_to([P, 2, DH])).then_inc(rden_ok, 1)

                    def normalise(qt):
                        dve.wait_ge(rdT_ok, pair * 2 + qt + 1)
                        v.tensor_tensor(heads_T[:, bass.ds(j, 1), qt * P:qt * P + P],
                                        ps[:, 6 + qt, 0:P].rearrange("p (a n) -> p a n", a=1),
                                        rdT[:, qt:qt + 1, :], ALU.mult).then_inc(norm_ok, 1)

                    own(v.tensor_copy(r_cur[:, :, :], r_all[:, bass.ds(b * QT, QT), bass.ds(j * 2, 2)]))
                    maxima(0)
                    ring(("v", 0, 1))
                    maxima(1)
                    for c in range(NC):
                        ring(("t", 0, c))
                    ring(("v", 0, 2))
                    ring(("v", 0, 3))
                    maxima(2)
                    row_sums(0)
                    for c in range(NC):
                        ring(("t", 1, c))
                    maxima(3)
                    for c in range(NC):
                        ring(("t", 2, c))
                    query_low(pair + 2)
                    normalise(0)
                    for c in range(NC):
                        ring(("t", 3, c))
                    row_sums(1)
                    normalise(1)
                assert own.steps == PAIR_STEPS, own.steps
                own.base, own.steps = start + b * (NJ * PAIR_STEPS + EPI) + NJ * PAIR_STEPS, 0
                dve.wait_ge(y_ps, b + 1)
                dve.wait_ge(a_x1_kept, AB + HELD)
                own(v.tensor_tensor(hrow[:, 0:QT, :], ps[:, 6, 0:QT * P].rearrange("p (t n) -> p t n", n=P),
                                    bo_all[:, None, :].broadcast_to([P, QT, P]), ALU.add))
                v.tensor_tensor(hrow[:, 0:QT, :], hrow[:, 0:QT, :], x_all[:, bass.ds(b * QT, QT), :], ALU.add)\
                    .then_inc(y_read, 1)
                dve.wait_ge(y_read, b + 1 + HELD)
                moments(QT)
                v.tensor_scalar(ve[:, 0:QT], mv[:, 0:QT, 1], 1e-5, None, ALU.add).then_inc(b_var, 1)
                dve.wait_ge(b_pow, b + 1)
                for qt in range(QT):
                    last = v.tensor_scalar(hrow[:, qt, :], hrow[:, qt, :], mv[:, qt, 0:1], rstd[:, qt:qt + 1],
                                           ALU.subtract, ALU.mult)
                own(last)
                carry_wait()
                v.tensor_copy(x_all[:, bass.ds(b * QT, QT), :], hrow[:, 0:QT, :]).then_inc(x2_ok, 1)
                assert own.steps == EPI, own.steps
            own.base, own.steps = start + B * (NJ * PAIR_STEPS + EPI), 0
            dve.wait_ge(x2_ok, B)

            with dve.Fori(0, NG) as g:
                dve.wait_ge(c_logit, g + 1)
                carry_wait()
                v.tensor_copy(logit[:, bass.ds(g * 4, 4), :],
                              ps[:, 1, 0:4 * E].rearrange("p (t e) -> p t e", e=E)).then_inc(c_logit_kept, 1)
            dve.wait_ge(c_logit_kept, NG + HELD)
            over = lambda a: a[:, :, None].broadcast_to([P, NT, E])
            own(v.tensor_reduce(tmax[:, :], logit[:, :, :], AX.X, ALU.max))
            v.tensor_tensor(lm[:, :, :], logit[:, :, :], over(tmax), ALU.subtract).then_inc(c_lm, 1)
            dve.wait_ge(c_lm, 1)
            own(v.tensor_scalar(rk[:, :, :], lm[:, :, :], 0.0, None, ALU.is_ge))
            own(v.scalar_tensor_tensor(one_hot[:, :, :].rearrange("p t e -> p (t e)"),
                                       rk[:, :, :].rearrange("p t e -> p (t e)"), -float(E),
                                       iota8[:, :, :].rearrange("p t e -> p (t e)"), ALU.mult, ALU.add))
            own(v.tensor_reduce(vmin[:, :], one_hot[:, :, :], AX.X, ALU.min))
            v.tensor_tensor(rk[:, :, :], one_hot[:, :, :], over(vmin), ALU.is_equal).then_inc(c_hot, 1)
            dve.wait_ge(c_exp, 1)
            own(v.tensor_reduce(tden[:, :], ex[:, :, :], AX.X, ALU.add))
            own(v.reciprocal(ptok[:, :], tden[:, :]))
            own(v.memset(cmask[:, :, :], 1.0))
            own(v.memset(cmask[:, :, 0:1], 0.0))
            dve.wait_ge(c_rank_ps, 2)
            own(v.tensor_copy(tot[:, :, :], ps[:, 1, 0:NT * E].rearrange("p (t e) -> p e t", e=E)))
            own(v.tensor_tensor_scan(csum[:, :, :].rearrange("p e t -> p (e t)"),
                                     cmask[:, :, :].rearrange("p e t -> p (e t)"),
                                     tot[:, :, :].rearrange("p e t -> p (e t)"), 0.0, ALU.mult, ALU.add))
            own(v.tensor_tensor(cmask[:, :, :], csum[:, :, :], tot[:, :, :], ALU.subtract))
            own(v.tensor_tensor(lm[:, :, :], ps[:, 0, 0:NT * E].rearrange("p (t e) -> p t e", e=E),
                                cmask[:, :, :].rearrange("p e t -> p t e"), ALU.add))
            own(v.tensor_tensor(ex[:, :, :], lm[:, :, :], rk[:, :, :], ALU.mult))
            own(v.tensor_reduce(rank[:, :], ex[:, :, :], AX.X, ALU.add))
            own(v.tensor_scalar(keep[:, :], rank[:, :], float(CAP), None, ALU.is_lt))
            own(v.scalar_tensor_tensor(slot[:, :], vmin[:, :], float(CAP), rank[:, :], ALU.mult, ALU.add))
            own(v.tensor_scalar(tmax[:, :], slot[:, :], float(E * CAP - SLOTS), None, ALU.add))
            own(v.tensor_tensor(slot[:, :], tmax[:, :], keep[:, :], ALU.mult))
            own(v.tensor_tensor(tden[:, :], ptok[:, :], keep[:, :], ALU.mult))
            v.tensor_scalar(dest[:, :], slot[:, :], float(SLOTS), None, ALU.add).then_inc(c_dest, 1)

            with dve.Fori(0, E // 2) as i:
                for s in range(2):
                    dve.wait_ge(f_y, i * 2 + s + 1 + HELD)
                    dve.wait_ge(f_out, i * 32 + HELD)
                    v.tensor_copy(ye[:, s, :, :], ps[:, 6 + s, 0:ST * P].rearrange("p (t n) -> p t n", n=P))\
                        .then_inc(f_y_sb, 1)

            dve.wait_ge(c_gather, 16 * NT)
            with dve.Fori(0, NG) as g:
                own.enter(g, 1 + 1 + 2)
                for t in range(4):
                    last = (v.tensor_scalar(t1[:, t * P:t * P + P],
                                        y_all[:, bass.ds(g * 4 + t, 1), :].rearrange("p a n -> p (a n)"),
                                        tden[:, bass.ds(g * 4 + t, 1)], None, ALU.mult))
                own(last)
                own(v.tensor_tensor(hrow[:, :, :], t1[:, :].rearrange("p (t n) -> p t n", n=P),
                                    x_all[:, bass.ds(g * 4, 4), :], ALU.add))
                moments(4)
                v.tensor_scalar(ve[:, :], mv[:, :, 1], 1e-5, None, ALU.add).then_inc(g_var, 1)
                dve.wait_ge(g_pow, g + 1)
                dve.wait_ge(g_out, g * 16 + HELD)
                for t in range(4):
                    last = v.tensor_scalar(x1s[:, t, :], hrow[:, t, :], mv[:, t, 0:1], rstd[:, t:t + 1],
                                           ALU.subtract, ALU.mult)
                last.then_inc(g_ready, 1)
            own.leave(NG)

        @block.tensor
        def _(pe):
            for held in (ctx_tr, f_y, q_ps, c_tr, a_x1T_ps,):
                pe.sem_inc(held, HELD)
            mm = nc.tensor.matmul
            tr = nc.tensor.transpose
            pe.wait_ge(masks_ready, 6)
            pe.wait_ge(weights_in, 16 * 15)
            pe.wait_ge(tern_ready, 4)
            for m in range(4):
                last = tr(ps[:, 0, m * P:m * P + P], w_tern[:, m, :], ident[:, :])
            last.then_inc(setup_tr, 1)
            for j in range(NJ):
                last = tr(ps[:, 1 + j // 4, j % 4 * P:j % 4 * P + P], wq_rows[:, j * P:j * P + P], ident[:, :])
            last.then_inc(setup_tr, 1)
            for j in range(NJ):
                last = tr(ps[:, 3 + j // 4, j % 4 * P:j % 4 * P + P], wk_rows[:, j * P:j * P + P], ident[:, :])
            last.then_inc(setup_tr, 1)
            pe.wait_ge(setup_ev_act, 2)
            pe.wait_ge(setup_ev_dve, 3)
            for h in range(H):
                last = mm(ps[:, h // 4, h % 4 * P:h % 4 * P + P], wq_T[:, h // 2, :], wk_T[:, h % 2, h // 2, :],
                          start=True, stop=True)
            last.then_inc(setup_mm, 1)
            for h in range(H):
                mm(ps[:, 5, h:h + 1], wk_T[:, h % 2, h // 2, :], bq_c[:, h // 2:h // 2 + 1], start=True, stop=True)
            for j in range(NJ):
                mm(ps[:, 5, H + 2 * j:H + 2 * j + 2], wq_T[:, j, :], bk_m[:, j, :], start=True, stop=True)
            for j in range(NJ):
                mm(ps[:, 5, 2 * H + 2 * j:2 * H + 2 * j + 2], bq_c[:, j:j + 1].broadcast_to([P, P]), bk_m[:, j, :],
                   start=True, stop=True)
            for j in range(NJ):
                last = mm(ps[:, 6, 0:P], bv_c[:, j:j + 1].broadcast_to([P, P]), wo_rows[:, j, :],
                          start=(j == 0), stop=(j == NJ - 1))
            last.then_inc(setup_mm, 1)
            pe.wait_ge(tables_act, 1)
            pe.wait_ge(tables_dve, 4)

            with pe.Fori(0, AB) as i:
                pe.wait_ge(a_x, i * 16 + 16)
                for t in range(4):
                    last = tr(ps[:, 0, t * P:t * P + P], xs[:, t, :], ident[:, :])
                last.then_inc(a_xT_ps, 1)
                pe.wait_ge(a_xT, i + 1)
                for m in range(3):
                    mm(ps[:, 1 + m, :], w_T[:, m, :], xT[:, :], start=True, stop=True).then_inc(a_rkv, 1)
                pe.wait_ge(a_y, i + 1)
                for t in range(4):
                    last = mm(ps[:, 4, t * P:t * P + P], y[:, t * P:t * P + P], w_T[:, 3, :], start=True, stop=True)
                last.then_inc(a_o, 1)
                pe.wait_ge(a_ysq, i + 1)
                for t in range(4):
                    last = mm(ps[:, 5, t:t + 1], ysq[:, t * P:t * P + P], ones[:, 0:1], start=True, stop=True)
                last.then_inc(a_o, 1)
                pe.wait_ge(a_x1, i + 1)
                pe.wait_ge(a_x1T_kept, i + HELD)
                for t in range(4):
                    last = tr(ps[:, 6, t * P:t * P + P], x1s[:, t, :], ident[:, :])
                last.then_inc(a_x1T_ps, 1)
                pe.wait_ge(a_x1T, i + 1)
                pe.wait_ge(a_r, i * 3 + HELD)
                for t in range(4):
                    last = mm(ps[:, 7, t * H:t * H + H], x1Ts[:, t * P:t * P + P], kb_tab[:, :], start=True, stop=True)
                last.then_inc(a_r_ps, 1)
            pe.wait_ge(a_r, AB * 3 + HELD)
            pe.wait_ge(a_x1T_kept, AB + HELD)

            def queries():
                for h in range(2):
                    last = mm(ps[:, 7, h * T:h * T + T], m_cur[:, h, :], x1T_cur[:, :], start=True, stop=True)
                last.then_inc(q_ps, 1)

            pe.wait_ge(x1T_staged, 1)
            pe.wait_ge(m_staged, 2)
            queries()
            with pe.Fori(0, B) as b:
                pe.wait_ge(ctx_in, b * 32 + 32)
                pe.wait_ge(ring_act, b * (NJ * RING_ACT) + HELD)
                pe.wait_ge(ring_dve, b * (NJ * RING_DVE) + HELD)
                for c, tiles in enumerate(V_TILES):
                    if c >= 2:
                        pe.wait_ge(ctx_f_ok, b * NC + c - 1)
                    for n, k in enumerate(tiles):
                        rows = P if k < KT - 1 else KREM
                        last = tr(ps[:, 4 + c % 2, n * P:n * P + rows], ctx_raw[0:rows, k, :],
                                  ident[0:rows, 0:rows])
                    last.then_inc(ctx_tr, 1)
                with pe.Fori(0, NJ) as j:
                    pair = b * NJ + j

                    def unit_scores(u):
                        h, q0 = u % 2, u // 2 * P
                        for half in range(2):
                            if half == 0:
                                pe.wait_ge(exp_low, pair * 4 + u + HELD)
                            else:
                                pe.wait_ge(exp_high, pair * 8 + 2 * u + HELD)
                            for c in (2 * half, 2 * half + 1):
                                o = ps[:, c, 0:WID[c]]
                                k0, k1 = KEY0[c], KEY0[c] + WID[c]
                                mm(o, q_hi[:, h, q0:q0 + P], ctx_hi[:, k0:k1], start=True, stop=False)
                                mm(o, q_hi[:, h, q0:q0 + P], ctx_lo[:, k0:k1], start=False, stop=False)
                                last = mm(o, q_lo[:, h, q0:q0 + P], ctx_hi[:, k0:k1], start=False, stop=True)
                            last.then_inc(scores, 1)

                    def ring(key):
                        i = AT[key]
                        kind, u, c = key
                        na, nd = emptied(i - 2) if i >= 2 else emptied(NRING + i - 2)
                        turn = pair * NRING
                        if i >= 2:
                            if OWNER[i - 2] == "act":
                                pe.wait_ge(ring_act, pair * RING_ACT + na + HELD)
                            else:
                                pe.wait_ge(ring_dve, pair * RING_DVE + nd + HELD)
                        else:
                            pe.wait_ge(ring_act, pair * RING_ACT + HELD)
                            pe.wait_ge(ring_dve, pair * RING_DVE + HELD)
                        bank = 4 + i % 2
                        for n, k in enumerate(V_TILES[c]):
                            if kind == "v":
                                rows = P if k < KT - 1 else KREM
                                last = mm(ps[0:rows, bank, n * P:n * P + P], ctx_f[:, k * P:k * P + rows],
                                          wv_rows[:, bass.ds(j * P, P)], start=True, stop=True)
                            else:
                                last = tr(ps[:, bank, n * P:n * P + P], prob[:, u % 2, k * P:k * P + P], ident[:, :])
                        last.then_inc(ring_full, 1)

                    def transposed(u):
                        for c in range(NC):
                            if c == 0:
                                pe.wait_ge(exp_low, pair * 4 + u + 1 + HELD)
                            if c == 1:
                                pe.wait_ge(exp_high, pair * 8 + 2 * u + 2 + HELD)
                            ring(("t", u, c))

                    def values(qt, last_chunk):
                        na, nd = emptied(AT[last_chunk])
                        pe.wait_ge(ring_act, pair * RING_ACT + na + HELD)
                        pe.wait_ge(ring_dve, pair * RING_DVE + nd + HELD)
                        bank = 6 + qt
                        for k in range(KT):
                            for h in range(2):
                                mm(ps[h * DH:h * DH + DH, bank, 0:P], v_pair[:, k, h * DH:h * DH + DH],
                                   prob_T[:, h, k, qt * P:qt * P + P], start=(k == 0), stop=(k == KT - 1))
                        pe.wait_ge(rden_ok, pair * 2 + qt + 1)
                        tr(ps[:, bank, P:2 * P], rspread[:, qt, :], ident[:, :]).then_inc(pv_ok, 1)

                    pe.wait_ge(ctx_f_ok, b * NC + NC)
                    pe.wait_ge(ctx_lo_ok, b * NC + NC)
                    pe.wait_ge(q_lo_ok, pair + 1 + HELD)
                    unit_scores(0)
                    ring(("v", 0, 0))
                    ring(("v", 0, 1))
                    unit_scores(1)
                    transposed(0)
                    ring(("v", 0, 2))
                    ring(("v", 0, 3))
                    unit_scores(2)
                    transposed(1)
                    pe.wait_ge(m_staged, pair * 2 + 4)
                    pe.wait_ge(norm_ok, pair * 2 + HELD)
                    queries()
                    unit_scores(3)
                    transposed(2)
                    pe.wait_ge(y_read, b + HELD)
                    values(0, ("t", 1, NC - 1))
                    transposed(3)
                    pe.wait_ge(q_lo_ok, pair + 2 + HELD)
                    values(1, ("t", 3, NC - 1))
                pe.wait_ge(norm_ok, b * (2 * NJ) + 2 * NJ + HELD)
                for qt in range(QT):
                    for jj in range(NJ):
                        last = mm(ps[:, 6, qt * P:qt * P + P], heads_T[:, jj, qt * P:qt * P + P],
                                  wo_rows[:, jj, :], start=(jj == 0), stop=(jj == NJ - 1))
                last.then_inc(y_ps, 1)
            pe.wait_ge(y_read, B + HELD)
            pe.wait_ge(q_lo_ok, B * NJ + 1 + HELD)

            with pe.Fori(0, NG) as g:
                pe.wait_ge(c_staged, g + 1)
                for t in range(4):
                    last = tr(ps[:, 0, t * P:t * P + P], hrow[:, t, :], ident[:, :])
                last.then_inc(c_tr, 1)
                pe.wait_ge(c_xT, g + 1)
                pe.wait_ge(c_logit_kept, g + HELD)
                for t in range(4):
                    last = mm(ps[:, 1, t * E:t * E + E], x1Ts[:, t * P:t * P + P], fwr_sb[:, :], start=True, stop=True)
                last.then_inc(c_logit, 1)
            pe.wait_ge(c_hot, 1)
            hot = rk[:, :, :].rearrange("p t e -> p (t e)")
            mm(ps[:, 0, 0:NT * E], tri[:, :], hot, start=True, stop=True).then_inc(c_rank_ps, 1)
            mm(ps[:, 1, 0:NT * E], ones[:, :], hot, start=True, stop=True).then_inc(c_rank_ps, 1)
            pe.wait_ge(c_dest, 1)

            with pe.Fori(0, E // 2) as i:
                for s in range(2):
                    pe.wait_ge(f_in[s], i * 48 + 48)
                    for t in range(ST):
                        last = tr(ps[:, s, t * P:t * P + P], xe[:, s, t, :], ident[:, :])
                    last.then_inc(f_tr, 1)
                    pe.wait_ge(f_xT, i * 2 + s + 1)
                    pe.wait_ge(f_relu, i * (2 * FC) + s * FC + HELD)
                    for f in range(FC):
                        mm(ps[:, 2 + f, 0:CAP], w1_sb[:, s, f * P:f * P + P], xeT[:, s, :], start=True, stop=True)\
                            .then_inc(f_h, 1)
                    pe.wait_ge(f_relu, i * (2 * FC) + s * FC + FC + HELD)
                    pe.wait_ge(f_y_sb, i * 2 + HELD)
                    for t in range(ST):
                        for f in range(FC):
                            last = mm(ps[:, 6 + s, t * P:t * P + P], hT[:, s, f, t * P:t * P + P],
                                      w2_sb[:, s, f, :], start=(f == 0), stop=(f == FC - 1))
                    last.then_inc(f_y, 1)


_INS = ['x', 'ctx_1024', 'L0_attn_Wr', 'L0_attn_Wk', 'L0_attn_Wv', 'L0_attn_Wo', 'L0_attn_decay', 'L0_attn_ln_w',
        'L0_xattn_Wq', 'L0_xattn_bq', 'L0_xattn_Wk', 'L0_xattn_bk', 'L0_xattn_Wv', 'L0_xattn_bv', 'L0_xattn_Wo',
        'L0_xattn_bo', 'L0_ffn_Wr', 'L0_ffn_W1', 'L0_ffn_W2']


def kernel(**inputs):
    import numpy as _np
    import concourse.bacc as _bacc
    from concourse import mybir as _mybir
    from concourse.bass_utils import run_bass_kernel_spmd as _run

    nc = _bacc.Bacc("TRN2", target_bir_lowering=False, num_devices=1)
    arrays, args = {}, []
    for name in _INS:
        a = _np.ascontiguousarray(inputs[name])
        arrays[f"in_{name}_dram"] = a
        args.append(nc.dram_tensor(f"in_{name}_dram", a.shape, _mybir.dt.from_np(a.dtype), kind="ExternalInput").ap())
    shape = inputs["x"].shape
    args.append(nc.dram_tensor("out_0_dram", shape, _mybir.dt.float32, kind="ExternalOutput").ap())
    decoder_layer(nc, *args)
    r = _run(nc, [arrays], core_ids=[0])
    return r.results[0]["out_0_dram"]
```

```python
from contextlib import ExitStack

import concourse.bass as bass
from concourse import mybir

P = 128
F32 = mybir.dt.float32
F32R = mybir.dt.float32r
I32 = mybir.dt.int32
ALU = mybir.AluOpType
ACT = mybir.ActivationFunctionType
AX = mybir.AxisListType


HELD = 1
HELD_EXP = 4


class Chain:

    def __init__(self, eng, sem):
        self.eng, self.sem, self.base, self.steps = eng, sem, 0, 0

    def __call__(self, instruction):
        instruction.then_inc(self.sem, 1)
        self.steps += 1
        self.eng.wait_ge(self.sem, self.base + self.steps)

    def enter(self, turn, per_turn):
        self.start = self.base + self.steps
        self.base, self.steps, self.per_turn = self.start + turn * per_turn, 0, per_turn

    def leave(self, turns):
        assert self.steps == self.per_turn, (self.steps, self.per_turn)
        self.base, self.steps = self.start + turns * self.per_turn, 0


def decoder_layer(nc, x, ctx, Wr, Wk, Wv, Wo, decay, ln_w, xWq, xbq, xWk, xbk, xWv, xbv, xWo, xbo,
                  fWr, fW1, fW2, out):
    B, T, D = x.shape
    KEYS = ctx.shape[1]
    AD = xWq.shape[1]
    DH = 64
    H = AD // DH
    NJ = H // 2
    QT = T // P
    KT = -(-KEYS // P)
    KREM = KEYS - (KT - 1) * P
    NT = B * QT
    E = fWr.shape[1]
    F = fW1.shape[2]
    FC = F // P
    CAP = max(-(-B * T // E), 1)
    ST = CAP // P
    SLOTS = E * CAP
    AB = B // 2
    ATILES = 2 * QT
    AN = 2 * T
    SCALE = DH ** -0.5
    NG = NT // 4
    assert D == P and QT == 2 and H == 16 and CAP % P == 0 and B % 2 == 0 and ATILES == 4
    CH = (KEYS - 1) // 4
    assert 4 * CH + 1 == KEYS and CH % 2 == 0
    KEY0 = [0, CH, 2 * CH, 3 * CH]
    WID = [CH, CH, CH + 2, CH + 2]
    KPAD = KEYS + 1
    PART = [0, CH, 2 * CH, 3 * CH + 1, KEYS]

    xe_dram = nc.dram_tensor("slots_in", [SLOTS, D], F32, kind="Internal").ap()
    ye_dram = nc.dram_tensor("slots_out", [SLOTS + 1, D], F32, kind="Internal").ap()

    with ExitStack() as stack:
        def sb(name, shape, dt=F32):
            return stack.enter_context(nc.sbuf_tensor(name, shape, dt))

        def sem(name):
            return stack.enter_context(nc.semaphore(name))

        ps = stack.enter_context(nc.psum_tensor("ps", [P, 8, 512], F32))

        ident = sb("ident", [P, P])
        ones = sb("ones", [P, P])
        tri = sb("tri", [P, P])
        iota8 = sb("iota8", [P, NT, E])
        minus_half = sb("minus_half", [P, 4])
        w_rows = sb("w_rows", [P, 4, P])
        w_tmp = sb("w_tmp", [P, 4, P])
        w_tern = sb("w_tern", [P, 4, P])
        w_T = sb("w_T", [P, 4, P])
        w_sum = sb("w_sum", [P, 4])
        w_scale = sb("w_scale", [P, 4])
        w_half = sb("w_half", [P, 4])
        w_nhalf = sb("w_nhalf", [P, 4])
        decay_c = sb("decay_c", [P, 1])
        dec = sb("dec", [P, 4])
        lnw_c = sb("lnw_c", [P, 1])
        scale_t = sb("scale_t", [P, 2, T])
        inv_scale = sb("inv_scale", [P, 2, T])
        half_scale = sb("half_scale", [P, 2, T])
        carry = sb("carry", [P, 2, T])
        wv_rows = sb("wv_rows", [P, AD])
        wo_rows = sb("wo_rows", [P, NJ, P])
        wq_T = sb("wq_T", [P, NJ, P])
        wk_T = sb("wk_T", [P, 2, NJ, P])
        bq_c = sb("bq_c", [P, NJ])
        bk_c = sb("bk_c", [P, NJ])
        bv_c = sb("bv_c", [P, NJ])
        bk_m = sb("bk_m", [P, NJ, 2])
        bo_b = sb("bo_b", [P, P])
        bo_all = sb("bo_all", [P, P])
        m_tab = sb("m_tab", [P, H, P])
        qb_tab = sb("qb_tab", [P, H])
        kb_tab = sb("kb_tab", [P, H])
        kb_const = sb("kb_const", [P, H])
        fwr_sb = sb("fwr_sb", [P, E])
        zeros = sb("zeros", [P, P])

        x_all = sb("x_all", [P, NT, P])
        x1T_all = sb("x1T_all", [P, B * T])
        r_all = sb("r_all", [P, B * NJ + 1, 2 * QT])

        prob_T = sb("prob_T", [P, 2, KT, T])
        region = prob_T[:, :, :, :].rearrange("p h k t -> p (h k t)")
        xT, th, ksb, y, ysq, t2 = (region[:, n * AN:(n + 1) * AN] for n in range(6))
        t1 = region[:, NT * P:NT * P + AN] if NT * P > 6 * AN else region[:, 6 * AN:7 * AN]

        wq_rows, wk_rows = region[:, 0:AD], region[:, AD:2 * AD]

        xs = sb("xs", [P, 4, P])
        hrow = sb("hrow", [P, 4, P])
        x1s = sb("x1s", [P, 4, P])
        x1Ts = sb("x1Ts", [P, AN])
        ms = sb("ms", [P, 4])
        rms = sb("rms", [P, 4])
        stats = sb("stats", [P, 4, 6])
        mv = sb("mv", [P, 4, 2])
        ve = sb("ve", [P, 4])
        rstd = sb("rstd", [P, 4])
        pad = sb("pad", [P, 1])

        ctx_raw = sb("ctx_raw", [P, KT, P])
        ctx_f = sb("ctx_f", [P, KEYS])
        ctx_hi = sb("ctx_hi", [P, KPAD], F32R)
        ctx_lo = sb("ctx_lo", [P, KPAD], F32R)
        x1T_cur = sb("x1T_cur", [P, T])
        m_cur = sb("m_cur", [P, 2, P])
        qb_cur = sb("qb_cur", [P, 2])
        q_f = sb("q_f", [P, 2, T])
        q_hi = sb("q_hi", [P, 2, T], F32R)
        q_lo = sb("q_lo", [P, 2, T], F32R)
        r_cur = sb("r_cur", [P, 1, 2 * QT])
        prob = sb("prob", [P, 2, KT * P])
        v_pair = sb("v_pair", [P, KT, P])
        mx = sb("mx", [P, 2, 4])
        nmx = sb("nmx", [P, 2])
        nbias = sb("nbias", [P, 2])
        esum = sb("esum", [P, 4, 4])
        den = sb("den", [P, 4])
        rden = sb("rden", [P, 4])
        rspread = sb("rspread", [P, QT, P])
        rdT = sb("rdT", [P, QT, P])
        x2_rows = sb("x2_rows", [P, QT, P])
        heads_T = sb("heads_T", [P, NJ, T])

        logit = sb("logit", [P, NT, E])
        lm = sb("lm", [P, NT, E])
        ex = sb("ex", [P, NT, E])
        one_hot = sb("one_hot", [P, NT, E])
        rk = sb("rk", [P, NT, E])
        tot = sb("tot", [P, E, NT])
        cmask = sb("cmask", [P, E, NT])
        csum = sb("csum", [P, E, NT])
        tmax = sb("tmax", [P, NT])
        tden = sb("tden", [P, NT])
        ptok = sb("ptok", [P, NT])
        vmin = sb("vmin", [P, NT])
        rank = sb("rank", [P, NT])
        keep = sb("keep", [P, NT])
        slot = sb("slot", [P, NT])
        dest = sb("dest", [P, NT], I32)
        w1_sb = sb("w1_sb", [P, 2, F])
        w2_sb = sb("w2_sb", [P, 2, FC, P])
        xe = sb("xe", [P, 2, ST, P])
        spare = prob[:, :, :].rearrange("p u k -> p (u k)")
        xeT = spare[:, 0:2 * CAP].rearrange("p (s c) -> p s c", s=2)
        assert B * T == 2 * FC * CAP
        hT = x1T_all[:, :].rearrange("p (s f c) -> p s f c", s=2, f=FC)
        ye = spare[:, 2 * CAP:4 * CAP].rearrange("p (s t n) -> p s t n", s=2, n=P)
        y_all = region[:, 0:NT * P].rearrange(
            "p (n d) -> p n d", n=NT)

        weights_in = sem("weights_in")
        consts_ready = sem("consts_ready")
        masks_ready = sem("masks_ready")
        slots_zeroed = sem("slots_zeroed")
        tern_ready = sem("tern_ready")
        decay_exp = sem("decay_exp")
        setup_tr = sem("setup_tr")
        setup_ev_act = sem("setup_ev_act")
        setup_ev_dve = sem("setup_ev_dve")
        setup_mm = sem("setup_mm")
        tables_act = sem("tables_act")
        tables_dve = sem("tables_dve")
        dve_own = sem("dve_own")
        pool_own = sem("pool_own")
        a_x = sem("a_x")
        a_xs_free = sem("a_xs_free")
        a_xT_ps = sem("a_xT_ps")
        a_xT = sem("a_xT")
        a_rkv = sem("a_rkv")
        a_gate = sem("a_gate")
        a_y = sem("a_y")
        a_ysq = sem("a_ysq")
        a_o = sem("a_o")
        a_var = sem("a_var")
        a_pow = sem("a_pow")
        a_x1 = sem("a_x1")
        a_x1_kept = sem("a_x1_kept")
        a_x1T_ps = sem("a_x1T_ps")
        a_x1T = sem("a_x1T")
        a_x1T_kept = sem("a_x1T_kept")
        a_r_ps = sem("a_r_ps")
        a_r = sem("a_r")
        ctx_in = sem("ctx_in")
        ctx_tr = sem("ctx_tr")
        ctx_hi_ok = sem("ctx_hi_ok")
        ctx_f_ok = sem("ctx_f_ok")
        ctx_lo_ok = sem("ctx_lo_ok")
        x1T_staged = sem("x1T_staged")
        m_staged = sem("m_staged")
        q_ps = sem("q_ps")
        q_f_ok = sem("q_f_ok")
        q_hi_ok = sem("q_hi_ok")
        q_lo_ok = sem("q_lo_ok")
        scores = sem("scores")
        row_max = sem("row_max")
        exp_ok = sem("exp_ok")
        ring_full = sem("ring_full")
        ring_act = sem("ring_act")
        ring_dve = sem("ring_dve")
        rden_ok = sem("rden_ok")
        pv_ok = sem("pv_ok")
        rdT_ok = sem("rdT_ok")
        norm_ok = sem("norm_ok")
        y_ps = sem("y_ps")
        y_read = sem("y_read")
        b_var = sem("b_var")
        b_pow = sem("b_pow")
        x2_rows_ok = sem("x2_rows_ok")
        x2_ok = sem("x2_ok")
        c_staged = sem("c_staged")
        c_tr = sem("c_tr")
        c_xT = sem("c_xT")
        c_logit = sem("c_logit")
        c_logit_kept = sem("c_logit_kept")
        c_lm = sem("c_lm")
        c_exp = sem("c_exp")
        c_hot = sem("c_hot")
        c_rank_ps = sem("c_rank_ps")
        c_dest = sem("c_dest")
        c_scatter = sem("c_scatter")
        f_in = [sem(f"f_in{i}") for i in range(2)]
        f_tr = sem("f_tr")
        f_xT = sem("f_xT")
        f_h = sem("f_h")
        f_relu = sem("f_relu")
        f_y = sem("f_y")
        f_y_sb = sem("f_y_sb")
        f_out = sem("f_out")
        c_gather = sem("c_gather")
        g_var = sem("g_var")
        g_pow = sem("g_pow")
        g_ready = sem("g_ready")
        g_out = sem("g_out")

        RING = (4, 5, 7)
        NRB = len(RING)
        K_CHUNKS = [list(range(4 * c, min(4 * c + 4, KT))) for c in range(-(-KT // 4))]
        NC = len(K_CHUNKS)
        assert NC == 4
        CHUNKS = ([("v", 0, c) for c in range(NC)] + [("t", 0, c) for c in range(NC - 1)] + [("q", 0, 0)] +
                  [("t", 0, NC - 1)] + [("t", u, c) for u in (1, 2, 3) for c in range(NC)])
        NRING = len(CHUNKS)
        assert NRING % NRB == 0
        AT = {key: i for i, key in enumerate(CHUNKS)}
        BY_ACT = {("v", 0): 1, ("t", 0): 1, ("t", 1): 2, ("t", 2): 2, ("t", 3): 2}
        OWNER = ["query" if kind == "q" else "act" if c < BY_ACT[kind, u] else "dve" for kind, u, c in CHUNKS]
        RING_ACT = OWNER.count("act")
        RING_DVE = OWNER.count("dve")

        RING_FULL = RING_ACT + RING_DVE

        def filled(i):
            return i + 1 - OWNER[:i + 1].count("query")

        QBANK = RING[AT[("q", 0, 0)] % NRB]

        def emptied(i):
            return OWNER[:i + 1].count("act"), OWNER[:i + 1].count("dve")

        C_IN = ctx.rearrange("b k d -> (b k) d")

        block = stack.enter_context(nc.Block())

        @block.sync
        def _(sp):
            for held in (f_out, g_out,):
                sp.sem_inc(held, HELD)
            def load(dst, src):
                sp.dma_start(dst, src).then_inc(weights_in, 16)

            for m, w in enumerate((Wr, Wk, Wv, Wo)):
                load(w_rows[:, m, :], w)
            load(decay_c[:, :], decay.rearrange("(d a) -> d a", a=1))
            load(lnw_c[:, :], ln_w.rearrange("(d a) -> d a", a=1))
            load(wq_rows[:, :], xWq)
            load(wk_rows[:, :], xWk)
            load(wv_rows[:, :], xWv)
            load(wo_rows[:, :, :], xWo.rearrange("(j p) n -> p j n", p=P))
            with nc.allow_non_contiguous_dma(reason="biases laid over the partitions, 4 KB each"):
                load(bq_c[:, :], xbq.rearrange("(j p) -> p j", p=P))
                load(bk_c[:, :], xbk.rearrange("(j p) -> p j", p=P))
                load(bv_c[:, :], xbv.rearrange("(j p) -> p j", p=P))
            load(bo_b[:, :], xbo.rearrange("(a n) -> a n", a=1).broadcast_to([P, P]))
            load(fwr_sb[:, :], fWr)
            sp.wait_ge(consts_ready, 1)
            for s in range(SLOTS // P):
                sp.dma_start(xe_dram[s * P:(s + 1) * P, :], zeros[:, :]).then_inc(slots_zeroed, 16)
            sp.dma_start(ye_dram[SLOTS:SLOTS + 1, :], zeros[0:1, :]).then_inc(slots_zeroed, 16)
            with sp.Fori(0, AB) as i:
                sp.wait_ge(a_xs_free, i + HELD)
                sp.dma_start(xs[:, :, :], x[bass.ds(i * 2, 2)].rearrange(
                    "b (t p) d -> p (b t) d", p=P)).then_inc(a_x, 16)
            def load_context(b):
                sp.dma_start(ctx_raw[:, 0:KT - 1, :], C_IN[bass.ds(b * KEYS, (KT - 1) * P)].rearrange(
                    "(t p) d -> p t d", p=P)).then_inc(ctx_in, 16)
                sp.dma_start(ctx_raw[0:KREM, KT - 1, :],
                             C_IN[bass.ds(b * KEYS + (KT - 1) * P, KREM)]).then_inc(ctx_in, 16)

            load_context(0)
            with sp.Fori(1, B) as b:
                sp.wait_ge(ctx_tr, b * NC + HELD)
                load_context(b)
            sp.wait_ge(ctx_tr, B * NC + HELD)
            load_context(0)
            sp.wait_ge(c_scatter, 16 * NT)
            with sp.Fori(0, E // 2) as i:
                for s in range(2):
                    sp.wait_ge(f_y, i * 2 + HELD)
                    sp.dma_start(xe[:, s, :, :], xe_dram[bass.ds(i * (2 * CAP) + s * CAP, CAP)].rearrange(
                        "(t p) d -> p t d", p=P)).then_inc(f_in[s], 16)
                    sp.dma_start(w1_sb[:, s, :], fW1[bass.ds(i * 2 + s, 1)].rearrange(
                        "o d f -> (o d) f")).then_inc(f_in[s], 16)
                    sp.dma_start(w2_sb[:, s, :, :], fW2[bass.ds(i * 2 + s, 1)].rearrange(
                        "o (c p) d -> p (o c) d", p=P)).then_inc(f_in[s], 16)
                for s in range(2):
                    sp.wait_ge(f_y_sb, i * 2 + s + 1 + HELD)
                    sp.dma_start(ye_dram[bass.ds(i * (2 * CAP) + s * CAP, CAP)].rearrange(
                        "(t p) d -> p t d", p=P), ye[:, s, :, :]).then_inc(f_out, 16)
            with sp.Fori(0, NG) as g:
                sp.wait_ge(g_ready, g + 1)
                sp.dma_start(out[bass.ds(g * 2, 2)].rearrange("b (t p) d -> p (b t) d", p=P),
                             x1s[:, :, :]).then_inc(g_out, 16)
            sp.wait_ge(g_out, 16 * NG + HELD)

        @block.gpsimd
        def _(pool):
            for held in (a_x1_kept, x2_ok,):
                pool.sem_inc(held, HELD)
            own = Chain(pool, pool_own)
            nc.gpsimd.memset(zeros[:, :], 0.0).then_inc(consts_ready, 1)
            own(nc.gpsimd.memset(ident[:, :], 0.0))
            nc.gpsimd.affine_select(out=ident[:, :], in_=ident[:, :], compare_op=ALU.not_equal, fill=1.0,
                                    base=0, pattern=[[-1, P]], channel_multiplier=1).then_inc(masks_ready, 1)
            own(nc.gpsimd.memset(tri[:, :], 0.0))
            nc.gpsimd.affine_select(out=tri[:, :], in_=tri[:, :], compare_op=ALU.is_ge, fill=1.0,
                                    base=0, pattern=[[-1, P]], channel_multiplier=1).then_inc(masks_ready, 1)
            nc.gpsimd.memset(ones[:, :], 1.0).then_inc(masks_ready, 1)
            nc.gpsimd.memset(minus_half[:, :], -0.5).then_inc(masks_ready, 1)
            nc.gpsimd.iota(iota8[:, :, :], pattern=[[0, NT], [1, E]], base=0, channel_multiplier=0,
                           allow_small_or_imprecise_dtypes=True).then_inc(masks_ready, 1)
            own(nc.gpsimd.memset(v_pair[:, KT - 1, :], 0.0))
            own(nc.gpsimd.memset(prob[:, 0, :], 0.0))
            nc.gpsimd.memset(prob[:, 1, :], 0.0).then_inc(masks_ready, 1)
            pool.wait_ge(masks_ready, 4)

            def power(dst, src, ready, count, done):
                pool.wait_ge(ready, count)
                nc.gpsimd.tensor_tensor(dst, src, minus_half[:, 0:src.shape[-1]], ALU.pow).then_inc(done, 1)

            with pool.Fori(0, AB) as i:
                power(rms[:, :], ms[:, :], a_var, i * 2 + 1, a_pow)
                power(rstd[:, :], ve[:, :], a_var, i * 2 + 2, a_pow)
                pool.wait_ge(a_x1, i + 1)
                nc.gpsimd.tensor_copy(x_all[:, bass.ds(i * 4, 4), :], x1s[:, :, :]).then_inc(a_x1_kept, 1)

            def stage_tokens(b):
                pool.wait_ge(q_ps, b * NJ + HELD)
                nc.gpsimd.tensor_copy(x1T_cur[:, :], x1T_all[:, bass.ds(b * T, T)]).then_inc(x1T_staged, 1)

            def stage_pair(pair, j):
                pool.wait_ge(consts_ready, 1)
                pool.wait_ge(q_ps, pair + HELD)
                pool.wait_ge(q_f_ok, pair + HELD)
                nc.gpsimd.tensor_copy(m_cur[:, :, :], m_tab[:, bass.ds(j * 2, 2), :]).then_inc(m_staged, 1)
                nc.gpsimd.tensor_copy(qb_cur[:, :], qb_tab[:, bass.ds(j * 2, 2)]).then_inc(m_staged, 1)

            def finish_norm(b, n_batches):
                power(rstd[:, 0:QT], ve[:, 0:QT], b_var, n_batches, b_pow)
                pool.wait_ge(consts_ready, 1)
                pool.wait_ge(b_pow, n_batches)
                for qt in range(QT):
                    last = nc.gpsimd.tensor_scalar(x2_rows[:, qt, :], hrow[:, qt, :], mv[:, qt, 0:1],
                                                   rstd[:, qt:qt + 1], ALU.subtract, ALU.mult)
                last.then_inc(x2_rows_ok, 1)
                pool.wait_ge(x2_rows_ok, n_batches)
                nc.gpsimd.tensor_copy(x_all[:, bass.ds(b * QT, QT), :], x2_rows[:, :, :]).then_inc(x2_ok, 1)

            pool.wait_ge(a_x1T_kept, AB + HELD)
            stage_tokens(0)
            with pool.Fori(0, NJ) as j:
                stage_pair(j, j)
            with pool.Fori(1, B) as b:
                stage_tokens(b)
                stage_pair(b * NJ, 0)
                finish_norm(b - 1, b)
                with pool.Fori(1, NJ) as j:
                    stage_pair(b * NJ + j, j)
            stage_pair(B * NJ, 0)
            finish_norm(B - 1, B)

            with pool.Fori(0, NG) as g:
                pool.wait_ge(x2_ok, B + HELD)
                pool.wait_ge(c_tr, g + HELD)
                nc.gpsimd.tensor_copy(hrow[:, :, :], x_all[:, bass.ds(g * 4, 4), :]).then_inc(c_staged, 1)

            pool.wait_ge(slots_zeroed, 16 * (SLOTS // P + 1))
            pool.wait_ge(c_dest, 1)
            for t in range(NT):
                nc.gpsimd.indirect_dma_start(
                    xe_dram[:, :], bass.IndirectOffsetOnAxis(ap=dest[:, t:t + 1], axis=0), x_all[:, t, :], None,
                    bounds_check=SLOTS - 1, oob_is_err=False).then_inc(c_scatter, 16)
            pool.wait_ge(f_out, 16 * E + HELD)
            for t in range(NT):
                nc.gpsimd.indirect_dma_start(
                    y_all[:, t, :], None, ye_dram[:, :], bass.IndirectOffsetOnAxis(ap=dest[:, t:t + 1], axis=0),
                    bounds_check=SLOTS, oob_is_err=False).then_inc(c_gather, 16)
            with pool.Fori(0, NG) as g:
                power(rstd[:, :], ve[:, :], g_var, g + 1, g_pow)

        @block.scalar
        def _(act):
            for held in (q_f_ok, a_x1T_kept, ring_act, f_relu,):
                act.sem_inc(held, HELD)
            act.sem_inc(exp_ok, HELD_EXP)
            copy = nc.scalar.copy
            act.wait_ge(weights_in, 16 * 15)
            nc.scalar.activation(dec[:, 0:1], decay_c[:, :], ACT.Exp, scale=-1.0).then_inc(decay_exp, 1)
            act.wait_ge(setup_tr, 1)
            copy(w_T[:, 0:3, :], ps[:, 0, 0:3 * P].rearrange("p (m n) -> p m n", m=3)).then_inc(setup_ev_act, 1)
            act.wait_ge(setup_tr, 2)
            copy(wq_T[:, :, :], ps[:, 1:3, :].rearrange("p a (b n) -> p (a b) n", n=P)).then_inc(setup_ev_act, 1)
            act.wait_ge(setup_mm, 1)
            nc.scalar.mul(m_tab[:, :, :], ps[:, 0:4, :].rearrange("p a (b n) -> p (a b) n", n=P), SCALE)\
                .then_inc(tables_act, 1)

            with act.Fori(0, AB) as i:
                act.wait_ge(a_xT_ps, i + 1)
                copy(xT[:, :], ps[:, 0, :]).then_inc(a_xT, 1)
                act.wait_ge(a_rkv, i * 3 + 1)
                nc.scalar.activation(th[:, :], ps[:, 1, :], ACT.Tanh, scale=0.5).then_inc(a_gate, 1)
                act.wait_ge(a_rkv, i * 3 + 2)
                copy(ksb[:, :], ps[:, 2, :]).then_inc(a_gate, 1)
                act.wait_ge(a_y, i + 1)
                nc.scalar.activation(ysq[:, :], y[:, :], ACT.Square).then_inc(a_ysq, 1)
                act.wait_ge(a_x1T_ps, i + 1 + HELD)
                copy(x1Ts[:, :], ps[:, 6, :]).then_inc(a_x1T, 1)
                copy(x1T_all[:, bass.ds(i * AN, AN)], ps[:, 6, :]).then_inc(a_x1T_kept, 1)

            def query_out(n_pairs):
                act.wait_ge(q_ps, n_pairs + HELD)
                nc.scalar.activation(q_f[:, 0, :], ps[:, QBANK, 0:T], ACT.Identity, bias=qb_cur[:, 0:1])
                nc.scalar.activation(q_f[:, 1, :], ps[:, QBANK, T:2 * T], ACT.Identity, bias=qb_cur[:, 1:2])\
                    .then_inc(q_f_ok, 1)

            def query_high(n_pairs):
                act.wait_ge(q_f_ok, n_pairs + HELD)
                copy(q_hi[:, :, :], q_f[:, :, :]).then_inc(q_hi_ok, 1)

            act.wait_ge(m_staged, 2)
            query_out(1)
            query_high(1)

            def context_high(n_batches):
                for c, tiles in enumerate(K_CHUNKS):
                    n = sum(P if k < KT - 1 else KREM for k in tiles)
                    k0 = tiles[0] * P
                    act.wait_ge(ctx_tr, n_batches * NC + c + 1 + HELD)
                    copy(ctx_hi[:, k0:k0 + n], ps[:, RING[c % NRB], 0:n]).then_inc(ctx_hi_ok, 1)
                    copy(ctx_f[:, k0:k0 + n], ps[:, RING[c % NRB], 0:n]).then_inc(ctx_f_ok, 1)

            context_high(0)
            with act.Fori(0, B) as b:
                with act.Fori(0, NJ) as j:
                    pair = b * NJ + j

                    def ring(key):
                        i = AT[key]
                        if OWNER[i] != "act":
                            return
                        kind, u, c = key
                        act.wait_ge(ring_full, pair * RING_FULL + filled(i))
                        src = ps[:, RING[i % NRB], :].rearrange("p (k n) -> p k n", n=P)
                        tiles = K_CHUNKS[c]
                        if kind == "v":
                            copy(v_pair[:, tiles[0]:tiles[-1] + 1, :], src[:, 0:len(tiles), :])\
                                .then_inc(ring_act, 1)
                        else:
                            copy(prob_T[:, u % 2, tiles[0]:tiles[-1] + 1, u // 2 * P:u // 2 * P + P],
                                 src[:, 0:len(tiles), :]).then_inc(ring_act, 1)

                    def exps(u):
                        act.wait_ge(row_max, pair * 4 + u + 1)
                        bias = nbias[:, u % 2:u % 2 + 1]
                        for c in range(4):
                            nc.scalar.activation(prob[:, u % 2, PART[c]:PART[c + 1]],
                                                 ps[:, c, PART[c] - KEY0[c]:PART[c + 1] - KEY0[c]], ACT.Exp,
                                                 bias=bias, accum_out=esum[:, u, c:c + 1]).then_inc(exp_ok, 1)

                    def spread(qt):
                        act.wait_ge(pv_ok, pair * 2 + qt + 1)
                        copy(rdT[:, qt, :], ps[:, 6, 2 * qt * P + P:2 * qt * P + 2 * P]).then_inc(rdT_ok, 1)

                    ring(("v", 0, 0))
                    exps(0)
                    for c in range(NC):
                        ring(("t", 0, c))
                    exps(1)
                    act.wait_ge(q_lo_ok, pair + 1 + HELD)
                    act.wait_ge(m_staged, pair * 2 + 4)
                    query_out(pair + 2)
                    for c in range(NC):
                        ring(("t", 1, c))
                    exps(2)
                    for c in range(NC):
                        ring(("t", 2, c))
                    exps(3)
                    spread(0)
                    for c in range(NC):
                        ring(("t", 3, c))
                    act.wait_ge(scores, pair * 16 + 16)
                    query_high(pair + 2)
                    spread(1)
                context_high(b + 1)

            with act.Fori(0, NG) as g:
                act.wait_ge(c_tr, g + 1 + HELD)
                copy(x1Ts[:, :], ps[:, 0, :]).then_inc(c_xT, 1)
            act.wait_ge(c_lm, 1)
            nc.scalar.activation(ex[:, :, :], lm[:, :, :], ACT.Exp).then_inc(c_exp, 1)
            with act.Fori(0, E // 2) as i:
                for s in range(2):
                    act.wait_ge(f_tr, i * 2 + s + 1)
                    copy(xeT[:, s, :], ps[:, 0 + s, 0:CAP]).then_inc(f_xT, 1)
                    for f in range(FC):
                        act.wait_ge(f_h, i * (2 * FC) + s * FC + f + 1)
                        nc.scalar.activation(hT[:, s, f, :], ps[:, 2 + f, 0:CAP], ACT.Relu).then_inc(f_relu, 1)

        @block.vector
        def _(dve):
            for held in (a_xs_free, q_lo_ok, ring_dve, norm_ok, y_read, c_logit_kept, f_y_sb, a_r,):
                dve.sem_inc(held, HELD)
            own = Chain(dve, dve_own)
            v = nc.vector
            dve.wait_ge(weights_in, 16 * 15)
            own(v.tensor_reduce(w_sum[:, :], w_rows[:, :, :], AX.X, ALU.add, apply_absolute_value=True))
            own(v.tensor_scalar(w_scale[:, :], w_sum[:, :], 1.0 / D, 1e-5, ALU.mult, ALU.max))
            own(v.tensor_scalar(w_half[:, :], w_scale[:, :], 0.5, None, ALU.mult))
            own(v.tensor_scalar(w_nhalf[:, :], w_scale[:, :], -0.5, None, ALU.mult))
            for m in range(4):
                own(v.tensor_scalar(w_tmp[:, m, :], w_rows[:, m, :], w_half[:, m:m + 1], None, ALU.is_gt))
                own(v.scalar_tensor_tensor(w_tern[:, m, :], w_rows[:, m, :], w_nhalf[:, m:m + 1],
                                           w_tmp[:, m, :], ALU.is_lt, ALU.subtract))
                own(v.scalar_tensor_tensor(w_tmp[:, m, :], w_tern[:, m, :], w_scale[:, m:m + 1],
                                           w_rows[:, m, :], ALU.mult, ALU.add))
                v.tensor_tensor(w_tern[:, m, :], w_rows[:, m, :], w_tmp[:, m, :], ALU.subtract)\
                    .then_inc(tern_ready, 1)
            dve.wait_ge(decay_exp, 1)
            own(v.tensor_scalar(dec[:, 1:2], dec[:, 0:1], 1.0, None, ALU.add))
            own(v.reciprocal(dec[:, 2:3], dec[:, 1:2]))
            own(v.tensor_scalar(dec[:, 3:4], dec[:, 2:3], 1e-7, None, ALU.max))
            own(v.memset(carry[:, :, :], 0.0))
            own(v.memset(scale_t[:, :, 0:1], 1.0))
            own(v.tensor_tensor_scan(scale_t[:, 0, 1:T], dec[:, 3:4].broadcast_to([P, T - 1]), carry[:, 0, 1:T],
                                     1.0, ALU.mult, ALU.add))
            own(v.tensor_copy(scale_t[:, 1, :], scale_t[:, 0, :]))
            own(v.tensor_scalar(half_scale[:, :, :], scale_t[:, :, :], 0.5, None, ALU.mult))
            own(v.tensor_scalar(inv_scale[:, :, :], scale_t[:, :, :], 1e-10, None, ALU.max))
            own(v.reciprocal(scale_t[:, :, :], inv_scale[:, :, :]))
            own(v.tensor_copy(inv_scale[:, :, :], scale_t[:, :, :]))
            own(v.memset(carry[:, :, 1:T], 1.0))
            own(v.memset(wk_T[64:P, 0, :, :], 0.0))
            own(v.memset(wk_T[0:64, 1, :, :], 0.0))
            own(v.memset(bk_m[:, :, :], 0.0))
            own(v.memset(ctx_hi[:, KEYS:KPAD].bitcast(F32), 0.0))
            own(v.memset(ctx_lo[:, KEYS:KPAD].bitcast(F32), 0.0))
            own(v.tensor_copy(bk_m[0:64, :, 0], bk_c[0:64, :]))
            own(v.tensor_copy(bk_m[64:P, :, 1], bk_c[64:P, :]))
            dve.wait_ge(setup_tr, 1)
            dve.wait_ge(setup_ev_act, 1)
            v.tensor_scalar(w_T[:, 3, :], ps[:, 0, 3 * P:4 * P], lnw_c[:, :], None, ALU.mult)\
                .then_inc(setup_ev_dve, 1)
            dve.wait_ge(setup_tr, 3)
            v.tensor_copy(wk_T[0:64, 0, :, :], ps[0:64, 3:5, :].rearrange("p a (b n) -> p (a b) n", n=P))\
                .then_inc(setup_ev_dve, 1)
            v.tensor_copy(wk_T[64:P, 1, :, :], ps[64:P, 3:5, :].rearrange("p a (b n) -> p (a b) n", n=P))\
                .then_inc(setup_ev_dve, 1)
            dve.wait_ge(setup_mm, 2)
            v.tensor_scalar(qb_tab[:, :], ps[:, 5, 0:H], SCALE, None, ALU.mult).then_inc(tables_dve, 1)
            v.tensor_scalar(kb_tab[:, :], ps[:, 5, H:2 * H], SCALE, None, ALU.mult).then_inc(tables_dve, 1)
            v.tensor_scalar(kb_const[:, :], ps[:, 5, 2 * H:3 * H], SCALE, None, ALU.mult).then_inc(tables_dve, 1)
            v.tensor_tensor(bo_all[:, :], ps[:, 6, 0:P], bo_b[:, :], ALU.add).then_inc(tables_dve, 1)
            dve.wait_ge(tables_dve, 4)

            def carry_wait():
                v.memset(pad[:, :], 0.0)

            def moments(tiles):
                for t in range(tiles):
                    last = v.bn_stats(stats[:, t, :], hrow[:, t, :])
                own(last)
                carry_wait()
                for t in range(tiles):
                    last = v.bn_aggr(mv[:, t, :], stats[:, t, :])
                own(last)

            flat = lambda a: a[:, :, :].rearrange("p b t -> p (b t)")
            with dve.Fori(0, AB) as i:
                own.enter(i, 3 + 2)
                dve.wait_ge(a_gate, i * 2 + 2)
                dve.wait_ge(a_rkv, i * 3 + 3)
                own(v.tensor_tensor(t1[:, :], ksb[:, :], ps[:, 3, :], ALU.mult))
                own(v.tensor_tensor(t2[:, :], t1[:, :], flat(inv_scale), ALU.mult))
                own(v.tensor_tensor_scan(t1[:, :], flat(carry), t2[:, :], 0.0, ALU.mult, ALU.add))
                v.tensor_tensor(t2[:, :], t1[:, :], flat(half_scale), ALU.mult).then_inc(a_r, 1)
                dve.wait_ge(a_r, i * 3 + 1 + HELD)
                v.scalar_tensor_tensor(y[:, :], th[:, :], 1.0, t2[:, :], ALU.add, ALU.mult).then_inc(a_y, 1)
                dve.wait_ge(a_o, i * 2 + 2)
                v.tensor_scalar(ms[:, :], ps[:, 5, 0:4], 1.0 / D, 1e-6, ALU.mult, ALU.add).then_inc(a_var, 1)
                dve.wait_ge(a_pow, i * 2 + 1)
                for t in range(4):
                    last = v.scalar_tensor_tensor(hrow[:, t, :], ps[:, 4, t * P:t * P + P], rms[:, t:t + 1],
                                                  xs[:, t, :], ALU.mult, ALU.add)
                last.then_inc(a_xs_free, 1)
                dve.wait_ge(a_xs_free, i + 1 + HELD)
                moments(4)
                v.tensor_scalar(ve[:, :], mv[:, :, 1], 1e-5, None, ALU.add).then_inc(a_var, 1)
                dve.wait_ge(a_pow, i * 2 + 2)
                dve.wait_ge(a_x1_kept, i + HELD)
                dve.wait_ge(a_x1T_ps, i + HELD)
                for t in range(4):
                    last = v.tensor_scalar(x1s[:, t, :], hrow[:, t, :], mv[:, t, 0:1], rstd[:, t:t + 1],
                                           ALU.subtract, ALU.mult)
                    last.then_inc(a_x1, 1) if t == 3 else last.then_inc(a_r, 1) if t == 0 else None
                dve.wait_ge(a_r_ps, i + 1)
                for bb in range(2):
                    for qt in range(QT):
                        t = bb * QT + qt
                        last = v.tensor_tensor(r_all[:, bass.ds(i * 2 * NJ + bb * NJ, NJ), 2 * qt:2 * qt + 2],
                                               ps[:, 7, t * H:t * H + H].rearrange("p (j h) -> p j h", h=2),
                                               kb_const[:, :].rearrange("p (j h) -> p j h", h=2), ALU.add)
                last.then_inc(a_r, 1)
            own.leave(AB)
            dve.wait_ge(a_r, AB * 3 + HELD)

            def query_low(n_pairs):
                dve.wait_ge(q_hi_ok, n_pairs)
                v.tensor_tensor(q_lo[:, :, :], q_f[:, :, :], q_hi[:, :, :].bitcast(F32), ALU.subtract)\
                    .then_inc(q_lo_ok, 1)

            query_low(1)
            PAIR_STEPS = 1 + 4 * 2 + 2 * 2

            def context_low(n_batches):
                for c, tiles in enumerate(K_CHUNKS):
                    n = sum(P if k < KT - 1 else KREM for k in tiles)
                    k0 = tiles[0] * P
                    dve.wait_ge(ctx_f_ok, n_batches * NC + c + 1)
                    v.tensor_tensor(ctx_lo[:, k0:k0 + n], ctx_f[:, k0:k0 + n],
                                    ctx_hi[:, k0:k0 + n].bitcast(F32), ALU.subtract).then_inc(ctx_lo_ok, 1)

            def stage_r(pair):
                own(v.tensor_copy(r_cur[:, :, :], r_all[:, bass.ds(pair, 1), :]))

            context_low(0)
            own(v.memset(r_all[:, B * NJ:B * NJ + 1, :], 0.0))
            own(v.tensor_copy(r_cur[:, :, :], r_all[:, 0:1, :]))
            with dve.Fori(0, B) as b:
                start = own.base + own.steps
                EPI = 1 + 2
                with dve.Fori(0, NJ) as j:
                    pair = b * NJ + j
                    own.base, own.steps = start + b * (NJ * PAIR_STEPS + EPI) + j * PAIR_STEPS, 0

                    def ring(key):
                        i = AT[key]
                        if OWNER[i] != "dve":
                            return
                        kind, u, c = key
                        dve.wait_ge(ring_full, pair * RING_FULL + filled(i))
                        src = ps[:, RING[i % NRB], :].rearrange("p (k n) -> p k n", n=P)
                        tiles = K_CHUNKS[c]
                        if kind == "v":
                            rows = KREM if tiles[-1] == KT - 1 else P
                            v.tensor_copy(v_pair[0:rows, tiles[0]:tiles[-1] + 1, :],
                                          src[0:rows, 0:len(tiles), :]).then_inc(ring_dve, 1)
                        else:
                            v.tensor_copy(prob_T[:, u % 2, tiles[0]:tiles[-1] + 1, u // 2 * P:u // 2 * P + P],
                                          src[:, 0:len(tiles), :]).then_inc(ring_dve, 1)

                    def maxima(u):
                        s = u % 2
                        for c in range(4):
                            dve.wait_ge(scores, pair * 16 + 4 * u + c + 1)
                            last = v.tensor_reduce(mx[:, s, c:c + 1], ps[:, c, 0:WID[c]], AX.X, ALU.max)
                        own(last)
                        own(v.tensor_reduce(nmx[:, s:s + 1], mx[:, s, :], AX.X, ALU.max, negate=True))
                        r = r_cur[:, 0, u:u + 1]
                        v.scalar_tensor_tensor(nbias[:, s:s + 1], nmx[:, s:s + 1], r, r, ALU.subtract,
                                               ALU.add).then_inc(row_max, 1)

                    def row_sums(qt):
                        dve.wait_ge(exp_ok, pair * 16 + 8 * qt + 8 + HELD_EXP)
                        own(v.tensor_reduce(den[:, 2 * qt:2 * qt + 2], esum[:, 2 * qt:2 * qt + 2, :], AX.X, ALU.add))
                        own(v.reciprocal(rden[:, 2 * qt:2 * qt + 2], den[:, 2 * qt:2 * qt + 2]))
                        v.tensor_copy(rspread[:, qt, :].rearrange("p (h d) -> p h d", h=2),
                                      rden[:, 2 * qt:2 * qt + 2, None].broadcast_to([P, 2, DH])).then_inc(rden_ok, 1)

                    def normalise(qt):
                        dve.wait_ge(rdT_ok, pair * 2 + qt + 1)
                        v.tensor_tensor(heads_T[:, bass.ds(j, 1), qt * P:qt * P + P],
                                        ps[:, 6, 2 * qt * P:2 * qt * P + P].rearrange("p (a n) -> p a n", a=1),
                                        rdT[:, qt:qt + 1, :], ALU.mult).then_inc(norm_ok, 1)

                    maxima(0)
                    for c in range(NC):
                        ring(("v", 0, c))
                    maxima(1)
                    for c in range(NC):
                        ring(("t", 0, c))
                    maxima(2)
                    for c in range(NC):
                        ring(("t", 1, c))
                    row_sums(0)
                    maxima(3)
                    for c in range(NC):
                        ring(("t", 2, c))
                    row_sums(1)
                    normalise(0)
                    for c in range(NC):
                        ring(("t", 3, c))
                    query_low(pair + 2)
                    dve.wait_ge(row_max, pair * 4 + 4)
                    stage_r(pair + 1)
                    normalise(1)
                assert own.steps == PAIR_STEPS, own.steps
                own.base, own.steps = start + b * (NJ * PAIR_STEPS + EPI) + NJ * PAIR_STEPS, 0
                context_low(b + 1)
                dve.wait_ge(y_ps, b + 1)
                dve.wait_ge(a_x1_kept, AB + HELD)
                dve.wait_ge(x2_ok, b + HELD)
                own(v.tensor_tensor(hrow[:, 0:QT, :], ps[:, 6, 0:QT * P].rearrange("p (t n) -> p t n", n=P),
                                    bo_all[:, None, :].broadcast_to([P, QT, P]), ALU.add))
                v.tensor_tensor(hrow[:, 0:QT, :], hrow[:, 0:QT, :], x_all[:, bass.ds(b * QT, QT), :], ALU.add)\
                    .then_inc(y_read, 1)
                dve.wait_ge(y_read, b + 1 + HELD)
                moments(QT)
                v.tensor_scalar(ve[:, 0:QT], mv[:, 0:QT, 1], 1e-5, None, ALU.add).then_inc(b_var, 1)
                assert own.steps == EPI, own.steps
            own.base, own.steps = start + B * (NJ * PAIR_STEPS + EPI), 0
            dve.wait_ge(x2_ok, B + HELD)

            with dve.Fori(0, NG) as g:
                dve.wait_ge(c_logit, g + 1)
                carry_wait()
                v.tensor_copy(logit[:, bass.ds(g * 4, 4), :],
                              ps[:, 1, 0:4 * E].rearrange("p (t e) -> p t e", e=E)).then_inc(c_logit_kept, 1)
            dve.wait_ge(c_logit_kept, NG + HELD)
            over = lambda a: a[:, :, None].broadcast_to([P, NT, E])
            own(v.tensor_reduce(tmax[:, :], logit[:, :, :], AX.X, ALU.max))
            v.tensor_tensor(lm[:, :, :], logit[:, :, :], over(tmax), ALU.subtract).then_inc(c_lm, 1)
            dve.wait_ge(c_lm, 1)
            own(v.tensor_scalar(rk[:, :, :], lm[:, :, :], 0.0, None, ALU.is_ge))
            own(v.scalar_tensor_tensor(one_hot[:, :, :].rearrange("p t e -> p (t e)"),
                                       rk[:, :, :].rearrange("p t e -> p (t e)"), -float(E),
                                       iota8[:, :, :].rearrange("p t e -> p (t e)"), ALU.mult, ALU.add))
            own(v.tensor_reduce(vmin[:, :], one_hot[:, :, :], AX.X, ALU.min))
            v.tensor_tensor(rk[:, :, :], one_hot[:, :, :], over(vmin), ALU.is_equal).then_inc(c_hot, 1)
            dve.wait_ge(c_exp, 1)
            own(v.tensor_reduce(tden[:, :], ex[:, :, :], AX.X, ALU.add))
            own(v.reciprocal(ptok[:, :], tden[:, :]))
            own(v.memset(cmask[:, :, :], 1.0))
            own(v.memset(cmask[:, :, 0:1], 0.0))
            dve.wait_ge(c_rank_ps, 2)
            own(v.tensor_copy(tot[:, :, :], ps[:, 1, 0:NT * E].rearrange("p (t e) -> p e t", e=E)))
            own(v.tensor_tensor_scan(csum[:, :, :].rearrange("p e t -> p (e t)"),
                                     cmask[:, :, :].rearrange("p e t -> p (e t)"),
                                     tot[:, :, :].rearrange("p e t -> p (e t)"), 0.0, ALU.mult, ALU.add))
            own(v.tensor_tensor(cmask[:, :, :], csum[:, :, :], tot[:, :, :], ALU.subtract))
            own(v.tensor_tensor(lm[:, :, :], ps[:, 0, 0:NT * E].rearrange("p (t e) -> p t e", e=E),
                                cmask[:, :, :].rearrange("p e t -> p t e"), ALU.add))
            own(v.tensor_tensor(ex[:, :, :], lm[:, :, :], rk[:, :, :], ALU.mult))
            own(v.tensor_reduce(rank[:, :], ex[:, :, :], AX.X, ALU.add))
            own(v.tensor_scalar(keep[:, :], rank[:, :], float(CAP), None, ALU.is_lt))
            own(v.scalar_tensor_tensor(slot[:, :], vmin[:, :], float(CAP), rank[:, :], ALU.mult, ALU.add))
            own(v.tensor_scalar(tmax[:, :], slot[:, :], float(E * CAP - SLOTS), None, ALU.add))
            own(v.tensor_tensor(slot[:, :], tmax[:, :], keep[:, :], ALU.mult))
            own(v.tensor_tensor(tden[:, :], ptok[:, :], keep[:, :], ALU.mult))
            v.tensor_scalar(dest[:, :], slot[:, :], float(SLOTS), None, ALU.add).then_inc(c_dest, 1)

            with dve.Fori(0, E // 2) as i:
                for s in range(2):
                    dve.wait_ge(f_y, i * 2 + s + 1 + HELD)
                    dve.wait_ge(f_out, i * 32 + HELD)
                    v.tensor_copy(ye[:, s, :, :], ps[:, 6 + s, 0:ST * P].rearrange("p (t n) -> p t n", n=P))\
                        .then_inc(f_y_sb, 1)

            dve.wait_ge(c_gather, 16 * NT)
            with dve.Fori(0, NG) as g:
                own.enter(g, 1 + 1 + 2)
                for t in range(4):
                    last = (v.tensor_scalar(t1[:, t * P:t * P + P],
                                        y_all[:, bass.ds(g * 4 + t, 1), :].rearrange("p a n -> p (a n)"),
                                        tden[:, bass.ds(g * 4 + t, 1)], None, ALU.mult))
                own(last)
                own(v.tensor_tensor(hrow[:, :, :], t1[:, :].rearrange("p (t n) -> p t n", n=P),
                                    x_all[:, bass.ds(g * 4, 4), :], ALU.add))
                moments(4)
                v.tensor_scalar(ve[:, :], mv[:, :, 1], 1e-5, None, ALU.add).then_inc(g_var, 1)
                dve.wait_ge(g_pow, g + 1)
                dve.wait_ge(g_out, g * 16 + HELD)
                for t in range(4):
                    last = v.tensor_scalar(x1s[:, t, :], hrow[:, t, :], mv[:, t, 0:1], rstd[:, t:t + 1],
                                           ALU.subtract, ALU.mult)
                last.then_inc(g_ready, 1)
            own.leave(NG)

        @block.tensor
        def _(pe):
            for held in (ctx_tr, f_y, q_ps, c_tr, a_x1T_ps,):
                pe.sem_inc(held, HELD)
            mm = nc.tensor.matmul
            tr = nc.tensor.transpose
            pe.wait_ge(masks_ready, 6)
            pe.wait_ge(weights_in, 16 * 15)
            pe.wait_ge(tern_ready, 4)
            for m in range(4):
                last = tr(ps[:, 0, m * P:m * P + P], w_tern[:, m, :], ident[:, :])
            last.then_inc(setup_tr, 1)
            for j in range(NJ):
                last = tr(ps[:, 1 + j // 4, j % 4 * P:j % 4 * P + P], wq_rows[:, j * P:j * P + P], ident[:, :])
            last.then_inc(setup_tr, 1)
            for j in range(NJ):
                last = tr(ps[:, 3 + j // 4, j % 4 * P:j % 4 * P + P], wk_rows[:, j * P:j * P + P], ident[:, :])
            last.then_inc(setup_tr, 1)
            pe.wait_ge(setup_ev_act, 2)
            pe.wait_ge(setup_ev_dve, 3)
            for h in range(H):
                last = mm(ps[:, h // 4, h % 4 * P:h % 4 * P + P], wq_T[:, h // 2, :], wk_T[:, h % 2, h // 2, :],
                          start=True, stop=True)
            last.then_inc(setup_mm, 1)
            for h in range(H):
                mm(ps[:, 5, h:h + 1], wk_T[:, h % 2, h // 2, :], bq_c[:, h // 2:h // 2 + 1], start=True, stop=True)
            for j in range(NJ):
                mm(ps[:, 5, H + 2 * j:H + 2 * j + 2], wq_T[:, j, :], bk_m[:, j, :], start=True, stop=True)
            for j in range(NJ):
                mm(ps[:, 5, 2 * H + 2 * j:2 * H + 2 * j + 2], bq_c[:, j:j + 1].broadcast_to([P, P]), bk_m[:, j, :],
                   start=True, stop=True)
            for j in range(NJ):
                last = mm(ps[:, 6, 0:P], bv_c[:, j:j + 1].broadcast_to([P, P]), wo_rows[:, j, :],
                          start=(j == 0), stop=(j == NJ - 1))
            last.then_inc(setup_mm, 1)
            pe.wait_ge(tables_act, 1)
            pe.wait_ge(tables_dve, 4)

            with pe.Fori(0, AB) as i:
                pe.wait_ge(a_x, i * 16 + 16)
                for t in range(4):
                    last = tr(ps[:, 0, t * P:t * P + P], xs[:, t, :], ident[:, :])
                last.then_inc(a_xT_ps, 1)
                pe.wait_ge(a_xT, i + 1)
                for m in range(3):
                    mm(ps[:, 1 + m, :], w_T[:, m, :], xT[:, :], start=True, stop=True).then_inc(a_rkv, 1)
                pe.wait_ge(a_y, i + 1)
                for t in range(4):
                    last = mm(ps[:, 4, t * P:t * P + P], y[:, t * P:t * P + P], w_T[:, 3, :], start=True, stop=True)
                last.then_inc(a_o, 1)
                pe.wait_ge(a_ysq, i + 1)
                for t in range(4):
                    last = mm(ps[:, 5, t:t + 1], ysq[:, t * P:t * P + P], ones[:, 0:1], start=True, stop=True)
                last.then_inc(a_o, 1)
                pe.wait_ge(a_x1, i + 1)
                pe.wait_ge(a_x1T_kept, i + HELD)
                for t in range(4):
                    last = tr(ps[:, 6, t * P:t * P + P], x1s[:, t, :], ident[:, :])
                last.then_inc(a_x1T_ps, 1)
                pe.wait_ge(a_x1T, i + 1)
                pe.wait_ge(a_r, i * 3 + HELD)
                for t in range(4):
                    last = mm(ps[:, 7, t * H:t * H + H], x1Ts[:, t * P:t * P + P], kb_tab[:, :], start=True, stop=True)
                last.then_inc(a_r_ps, 1)
            pe.wait_ge(a_r, AB * 3 + HELD)
            pe.wait_ge(a_x1T_kept, AB + HELD)

            def queries():
                for h in range(2):
                    last = mm(ps[:, QBANK, h * T:h * T + T], m_cur[:, h, :], x1T_cur[:, :], start=True, stop=True)
                last.then_inc(q_ps, 1)

            pe.wait_ge(x1T_staged, 1)
            pe.wait_ge(m_staged, 2)
            queries()

            def context(n_batches, chunks):
                for c in chunks:
                    if c == 0:
                        pe.wait_ge(ctx_in, n_batches * 32 + 32)
                    if c >= NRB:
                        pe.wait_ge(ctx_f_ok, n_batches * NC + c - NRB + 1)
                    for n, k in enumerate(K_CHUNKS[c]):
                        rows = P if k < KT - 1 else KREM
                        last = tr(ps[:, RING[c % NRB], n * P:n * P + rows], ctx_raw[0:rows, k, :],
                                  ident[0:rows, 0:rows])
                    last.then_inc(ctx_tr, 1)

            pe.wait_ge(q_f_ok, 1 + HELD)
            context(0, range(NC))
            EARLY = 1
            with pe.Fori(0, B) as b:
                with pe.Fori(0, NJ) as j:
                    pair = b * NJ + j

                    def unit_scores(u):
                        h, q0 = u % 2, u // 2 * P
                        for c in range(4):
                            pe.wait_ge(exp_ok, pair * 16 + 4 * (u - 1) + c + 1 + HELD_EXP)
                            o = ps[:, c, 0:WID[c]]
                            k0, k1 = KEY0[c], KEY0[c] + WID[c]
                            mm(o, q_hi[:, h, q0:q0 + P], ctx_hi[:, k0:k1], start=True, stop=False)
                            mm(o, q_hi[:, h, q0:q0 + P], ctx_lo[:, k0:k1], start=False, stop=False)
                            mm(o, q_lo[:, h, q0:q0 + P], ctx_hi[:, k0:k1], start=False, stop=True)\
                                .then_inc(scores, 1)

                    def ring(key):
                        i = AT[key]
                        kind, u, c = key
                        if i >= NRB:
                            na, nd = emptied(i - NRB)
                            if OWNER[i - NRB] == "act":
                                pe.wait_ge(ring_act, pair * RING_ACT + na + HELD)
                            elif OWNER[i - NRB] == "dve":
                                pe.wait_ge(ring_dve, pair * RING_DVE + nd + HELD)
                            else:
                                pe.wait_ge(q_f_ok, pair + 2 + HELD)
                        if kind == "q":
                            pe.wait_ge(m_staged, pair * 2 + 4)
                            queries()
                            return
                        bank = RING[i % NRB]
                        for n, k in enumerate(K_CHUNKS[c]):
                            if kind == "v":
                                rows = P if k < KT - 1 else KREM
                                last = mm(ps[0:rows, bank, n * P:n * P + P], ctx_f[:, k * P:k * P + rows],
                                          wv_rows[:, bass.ds(j * P, P)], start=True, stop=True)
                            else:
                                last = tr(ps[:, bank, n * P:n * P + P], prob[:, u % 2, k * P:k * P + P], ident[:, :])
                        last.then_inc(ring_full, 1)

                    def transposed(u):
                        for c in range(NC):
                            parts = next(n for n in range(1, 5) if PART[n] >= min(KEYS, (K_CHUNKS[c][-1] + 1) * P))
                            pe.wait_ge(exp_ok, pair * 16 + 4 * u + parts + HELD_EXP)
                            if (u, c) == (0, NC - 1):
                                ring(("q", 0, 0))
                            ring(("t", u, c))

                    def values(qt, chunks, last_filled):
                        col = 2 * qt * P
                        for c in chunks:
                            i = AT["t", 2 * qt + 1, c]
                            if i > last_filled - NRB:
                                na, nd = emptied(i)
                                if OWNER[i] == "act":
                                    pe.wait_ge(ring_act, pair * RING_ACT + na + HELD)
                                else:
                                    pe.wait_ge(ring_dve, pair * RING_DVE + nd + HELD)
                            for k, h in ((k, h) for k in K_CHUNKS[c] for h in range(2)):
                                mm(ps[h * DH:h * DH + DH, 6, col:col + P], v_pair[:, k, h * DH:h * DH + DH],
                                   prob_T[:, h, k, qt * P:qt * P + P], start=(k == 0), stop=(k == KT - 1))
                        if c == NC - 1:
                            pe.wait_ge(rden_ok, pair * 2 + qt + 1)
                            tr(ps[:, 6, col + P:col + 2 * P], rspread[:, qt, :], ident[:, :]).then_inc(pv_ok, 1)

                    pe.wait_ge(ctx_f_ok, b * NC + NC)
                    pe.wait_ge(ctx_lo_ok, b * NC + NC)
                    pe.wait_ge(q_lo_ok, pair + 1 + HELD)
                    unit_scores(0)
                    for c in range(NC):
                        ring(("v", 0, c))
                    unit_scores(1)
                    transposed(0)
                    pe.wait_ge(norm_ok, pair * 2 + HELD)
                    pe.wait_ge(y_read, b + HELD)
                    unit_scores(2)
                    transposed(1)
                    values(0, range(0, EARLY), AT["t", 1, NC - 1])
                    unit_scores(3)
                    transposed(2)
                    values(0, range(EARLY, NC), AT["t", 2, NC - 1])
                    transposed(3)
                    pe.wait_ge(norm_ok, pair * 2 + 1 + HELD)
                    values(1, range(NC), AT["t", 3, NC - 1])
                context(b + 1, range(NC - 1))
                pe.wait_ge(norm_ok, b * (2 * NJ) + 2 * NJ + HELD)
                for qt in range(QT):
                    for jj in range(NJ):
                        last = mm(ps[:, 6, qt * P:qt * P + P], heads_T[:, jj, qt * P:qt * P + P],
                                  wo_rows[:, jj, :], start=(jj == 0), stop=(jj == NJ - 1))
                    if qt == 0:
                        context(b + 1, [NC - 1])
                last.then_inc(y_ps, 1)
            pe.wait_ge(y_read, B + HELD)
            pe.wait_ge(q_lo_ok, B * NJ + 1 + HELD)

            with pe.Fori(0, NG) as g:
                pe.wait_ge(c_staged, g + 1)
                for t in range(4):
                    last = tr(ps[:, 0, t * P:t * P + P], hrow[:, t, :], ident[:, :])
                last.then_inc(c_tr, 1)
                pe.wait_ge(c_xT, g + 1)
                pe.wait_ge(c_logit_kept, g + HELD)
                for t in range(4):
                    last = mm(ps[:, 1, t * E:t * E + E], x1Ts[:, t * P:t * P + P], fwr_sb[:, :], start=True, stop=True)
                last.then_inc(c_logit, 1)
            pe.wait_ge(c_hot, 1)
            hot = rk[:, :, :].rearrange("p t e -> p (t e)")
            mm(ps[:, 0, 0:NT * E], tri[:, :], hot, start=True, stop=True).then_inc(c_rank_ps, 1)
            mm(ps[:, 1, 0:NT * E], ones[:, :], hot, start=True, stop=True).then_inc(c_rank_ps, 1)
            pe.wait_ge(c_dest, 1)

            with pe.Fori(0, E // 2) as i:
                for s in range(2):
                    pe.wait_ge(f_in[s], i * 48 + 48)
                    for t in range(ST):
                        last = tr(ps[:, s, t * P:t * P + P], xe[:, s, t, :], ident[:, :])
                    last.then_inc(f_tr, 1)
                    pe.wait_ge(f_xT, i * 2 + s + 1)
                    pe.wait_ge(f_relu, i * (2 * FC) + s * FC + HELD)
                    for f in range(FC):
                        mm(ps[:, 2 + f, 0:CAP], w1_sb[:, s, f * P:f * P + P], xeT[:, s, :], start=True, stop=True)\
                            .then_inc(f_h, 1)
                    pe.wait_ge(f_relu, i * (2 * FC) + s * FC + FC + HELD)
                    pe.wait_ge(f_y_sb, i * 2 + HELD)
                    for t in range(ST):
                        for f in range(FC):
                            last = mm(ps[:, 6 + s, t * P:t * P + P], hT[:, s, f, t * P:t * P + P],
                                      w2_sb[:, s, f, :], start=(f == 0), stop=(f == FC - 1))
                    last.then_inc(f_y, 1)


_INS = ['x', 'ctx_1024', 'L0_attn_Wr', 'L0_attn_Wk', 'L0_attn_Wv', 'L0_attn_Wo', 'L0_attn_decay', 'L0_attn_ln_w',
        'L0_xattn_Wq', 'L0_xattn_bq', 'L0_xattn_Wk', 'L0_xattn_bk', 'L0_xattn_Wv', 'L0_xattn_bv', 'L0_xattn_Wo',
        'L0_xattn_bo', 'L0_ffn_Wr', 'L0_ffn_W1', 'L0_ffn_W2']


def kernel(**inputs):
    import numpy as _np
    import concourse.bacc as _bacc
    from concourse import mybir as _mybir
    from concourse.bass_utils import run_bass_kernel_spmd as _run

    nc = _bacc.Bacc("TRN2", target_bir_lowering=False, num_devices=1)
    arrays, args = {}, []
    for name in _INS:
        a = _np.ascontiguousarray(inputs[name])
        arrays[f"in_{name}_dram"] = a
        args.append(nc.dram_tensor(f"in_{name}_dram", a.shape, _mybir.dt.from_np(a.dtype), kind="ExternalInput").ap())
    shape = inputs["x"].shape
    args.append(nc.dram_tensor("out_0_dram", shape, _mybir.dt.float32, kind="ExternalOutput").ap())
    decoder_layer(nc, *args)
    r = _run(nc, [arrays], core_ids=[0])
    return r.results[0]["out_0_dram"]
```

```python
from contextlib import ExitStack

import concourse.bass as bass
from concourse import mybir

P = 128
F32 = mybir.dt.float32
F32R = mybir.dt.float32r
I32 = mybir.dt.int32
ALU = mybir.AluOpType
ACT = mybir.ActivationFunctionType
AX = mybir.AxisListType


HELD = 1
HELD_EXP = 4


class Chain:

    def __init__(self, eng, sem):
        self.eng, self.sem, self.base, self.steps = eng, sem, 0, 0

    def __call__(self, instruction):
        instruction.then_inc(self.sem, 1)
        self.steps += 1
        self.eng.wait_ge(self.sem, self.base + self.steps)

    def enter(self, turn, per_turn):
        self.start = self.base + self.steps
        self.base, self.steps, self.per_turn = self.start + turn * per_turn, 0, per_turn

    def leave(self, turns):
        assert self.steps == self.per_turn, (self.steps, self.per_turn)
        self.base, self.steps = self.start + turns * self.per_turn, 0


def decoder_layer(nc, x, ctx, Wr, Wk, Wv, Wo, decay, ln_w, xWq, xbq, xWk, xbk, xWv, xbv, xWo, xbo,
                  fWr, fW1, fW2, out):
    B, T, D = x.shape
    KEYS = ctx.shape[1]
    AD = xWq.shape[1]
    DH = 64
    H = AD // DH
    NJ = H // 2
    QT = T // P
    KT = -(-KEYS // P)
    KREM = KEYS - (KT - 1) * P
    NT = B * QT
    E = fWr.shape[1]
    F = fW1.shape[2]
    FC = F // P
    CAP = max(-(-B * T // E), 1)
    ST = CAP // P
    SLOTS = E * CAP
    AB = B // 2
    ATILES = 2 * QT
    AN = 2 * T
    SCALE = DH ** -0.5
    NG = NT // 4
    assert D == P and QT == 2 and H == 16 and CAP % P == 0 and B % 2 == 0 and ATILES == 4
    CH = (KEYS - 1) // 4
    assert 4 * CH + 1 == KEYS and CH % 2 == 0
    KEY0 = [0, CH, 2 * CH, 3 * CH]
    WID = [CH, CH, CH + 2, CH + 2]
    KPAD = KEYS + 1
    PART = [0, CH, 2 * CH, 3 * CH + 1, KEYS]

    xe_dram = nc.dram_tensor("slots_in", [SLOTS, D], F32, kind="Internal").ap()
    ye_dram = nc.dram_tensor("slots_out", [SLOTS + 1, D], F32, kind="Internal").ap()

    with ExitStack() as stack:
        def sb(name, shape, dt=F32):
            return stack.enter_context(nc.sbuf_tensor(name, shape, dt))

        def sem(name):
            return stack.enter_context(nc.semaphore(name))

        ps = stack.enter_context(nc.psum_tensor("ps", [P, 8, 512], F32))

        ident = sb("ident", [P, P])
        ones = sb("ones", [P, P])
        tri = sb("tri", [P, P])
        iota8 = sb("iota8", [P, NT, E])
        minus_half = sb("minus_half", [P, 4])
        w_rows = sb("w_rows", [P, 4, P])
        w_tmp = sb("w_tmp", [P, 4, P])
        w_tern = sb("w_tern", [P, 4, P])
        w_T = sb("w_T", [P, 4, P])
        w_sum = sb("w_sum", [P, 4])
        w_scale = sb("w_scale", [P, 4])
        w_half = sb("w_half", [P, 4])
        w_nhalf = sb("w_nhalf", [P, 4])
        decay_c = sb("decay_c", [P, 1])
        dec = sb("dec", [P, 4])
        lnw_c = sb("lnw_c", [P, 1])
        scale_t = sb("scale_t", [P, 2, T])
        inv_scale = sb("inv_scale", [P, 2, T])
        half_scale = sb("half_scale", [P, 2, T])
        carry = sb("carry", [P, 2, T])
        wv_rows = sb("wv_rows", [P, AD])
        wo_rows = sb("wo_rows", [P, NJ, P])
        wq_T = sb("wq_T", [P, NJ, P])
        wk_T = sb("wk_T", [P, 2, NJ, P])
        bq_c = sb("bq_c", [P, NJ])
        bk_c = sb("bk_c", [P, NJ])
        bv_c = sb("bv_c", [P, NJ])
        bk_m = sb("bk_m", [P, NJ, 2])
        bo_b = sb("bo_b", [P, P])
        bo_all = sb("bo_all", [P, P])
        m_tab = sb("m_tab", [P, H, P])
        qb_tab = sb("qb_tab", [P, H])
        kb_tab = sb("kb_tab", [P, H])
        kb_const = sb("kb_const", [P, H])
        fwr_sb = sb("fwr_sb", [P, E])
        zeros = sb("zeros", [P, P])

        x_all = sb("x_all", [P, NT, P])
        x1T_all = sb("x1T_all", [P, B * T])
        r_all = sb("r_all", [P, B * NJ + 1, 2 * QT])

        prob_T = sb("prob_T", [P, 2, KT, T])
        region = prob_T[:, :, :, :].rearrange("p h k t -> p (h k t)")
        xT, th, ksb, y, ysq, t2 = (region[:, n * AN:(n + 1) * AN] for n in range(6))
        t1 = region[:, NT * P:NT * P + AN] if NT * P > 6 * AN else region[:, 6 * AN:7 * AN]

        wq_rows, wk_rows = region[:, 0:AD], region[:, AD:2 * AD]

        xs = sb("xs", [P, 4, P])
        xres = sb("xres", [P, 4, P])
        hrow = sb("hrow", [P, 4, P])
        x1s = sb("x1s", [P, 4, P])
        x1Ts = sb("x1Ts", [P, AN])
        ms = sb("ms", [P, 4])
        rms = sb("rms", [P, 4])
        stats = sb("stats", [P, 4, 6])
        mv = sb("mv", [P, 4, 2])
        ve = sb("ve", [P, 4])
        rstd = sb("rstd", [P, 4])
        pad = sb("pad", [P, 4])

        ctx_raw = sb("ctx_raw", [P, KT, P])
        ctx_f = sb("ctx_f", [P, KEYS])
        ctx_hi = sb("ctx_hi", [P, KPAD], F32R)
        ctx_lo = sb("ctx_lo", [P, KPAD], F32R)
        x1T_cur = sb("x1T_cur", [P, T])
        m_cur = sb("m_cur", [P, 2, P])
        qb_cur = sb("qb_cur", [P, 2])
        q_f = sb("q_f", [P, 2, T])
        q_hi = sb("q_hi", [P, 2, T], F32R)
        q_lo = sb("q_lo", [P, 2, T], F32R)
        r_cur = sb("r_cur", [P, 1, 2 * QT])
        prob = sb("prob", [P, 2, KT * P])
        v_pair = sb("v_pair", [P, KT, P])
        mx = sb("mx", [P, 2, 4])
        nmx = sb("nmx", [P, 2])
        nbias = sb("nbias", [P, 2])
        esum = sb("esum", [P, 4, 4])
        den = sb("den", [P, 4])
        rden = sb("rden", [P, 4])
        rspread = sb("rspread", [P, QT, P])
        rdT = sb("rdT", [P, QT, P])
        x2_rows = sb("x2_rows", [P, QT, P])
        heads_T = sb("heads_T", [P, NJ, T])

        logit = sb("logit", [P, NT, E])
        lm = sb("lm", [P, NT, E])
        ex = sb("ex", [P, NT, E])
        one_hot = sb("one_hot", [P, NT, E])
        rk = sb("rk", [P, NT, E])
        tot = sb("tot", [P, E, NT])
        cmask = sb("cmask", [P, E, NT])
        csum = sb("csum", [P, E, NT])
        tmax = sb("tmax", [P, NT])
        tden = sb("tden", [P, NT])
        ptok = sb("ptok", [P, NT])
        vmin = sb("vmin", [P, NT])
        rank = sb("rank", [P, NT])
        keep = sb("keep", [P, NT])
        slot = sb("slot", [P, NT])
        dest = sb("dest", [P, NT], I32)
        w1_sb = sb("w1_sb", [P, 2, F])
        w2_sb = sb("w2_sb", [P, 2, FC, P])
        xe = sb("xe", [P, 2, ST, P])
        spare = prob[:, :, :].rearrange("p u k -> p (u k)")
        xeT = spare[:, 0:2 * CAP].rearrange("p (s c) -> p s c", s=2)
        assert B * T == 2 * FC * CAP
        hT = x1T_all[:, :].rearrange("p (s f c) -> p s f c", s=2, f=FC)
        ye = spare[:, 2 * CAP:4 * CAP].rearrange("p (s t n) -> p s t n", s=2, n=P)
        x2s = [hrow[:, :, :], x1s[:, :, :]]
        x2T = [x1Ts[:, :], t2]
        y_all = region[:, 0:NT * P].rearrange(
            "p (n d) -> p n d", n=NT)

        tern_in = sem("tern_in")
        qk_in = sem("qk_in")
        weights_in = sem("weights_in")
        zero_parts = sem("zero_parts")
        consts_ready = sem("consts_ready")
        masks_ready = sem("masks_ready")
        slots_zeroed = sem("slots_zeroed")
        tern_ready = sem("tern_ready")
        decay_exp = sem("decay_exp")
        setup_tr = sem("setup_tr")
        setup_ev_act = sem("setup_ev_act")
        setup_ev_dve = sem("setup_ev_dve")
        setup_mm = sem("setup_mm")
        tables_act = sem("tables_act")
        tables_dve = sem("tables_dve")
        dve_own = sem("dve_own")
        pool_own = sem("pool_own")
        a_x = sem("a_x")
        a_xres = sem("a_xres")
        a_h = sem("a_h")
        a_xT_ps = sem("a_xT_ps")
        a_xT = sem("a_xT")
        a_rkv = sem("a_rkv")
        a_gate = sem("a_gate")
        a_y = sem("a_y")
        a_ysq = sem("a_ysq")
        a_o = sem("a_o")
        a_var = sem("a_var")
        a_pow = sem("a_pow")
        a_x1 = sem("a_x1")
        a_x1_kept = sem("a_x1_kept")
        a_x1T_ps = sem("a_x1T_ps")
        a_x1T = sem("a_x1T")
        a_x1T_kept = sem("a_x1T_kept")
        a_r_ps = sem("a_r_ps")
        a_r = sem("a_r")
        a_state = sem("a_state")
        a_kv = sem("a_kv")
        a_kv2 = sem("a_kv2")
        ctx_in = sem("ctx_in")
        ctx_tr = sem("ctx_tr")
        ctx_hi_ok = sem("ctx_hi_ok")
        ctx_f_ok = sem("ctx_f_ok")
        ctx_lo_ok = sem("ctx_lo_ok")
        x1T_staged = sem("x1T_staged")
        m_staged = sem("m_staged")
        q_ps = sem("q_ps")
        q_f_ok = sem("q_f_ok")
        q_hi_ok = sem("q_hi_ok")
        q_lo_ok = sem("q_lo_ok")
        scores = sem("scores")
        row_max = sem("row_max")
        exp_ok = sem("exp_ok")
        ring_full = sem("ring_full")
        ring_act = sem("ring_act")
        ring_dve = sem("ring_dve")
        rden_ok = sem("rden_ok")
        pv_ok = sem("pv_ok")
        rdT_ok = sem("rdT_ok")
        norm_ok = sem("norm_ok")
        y_ps = sem("y_ps")
        y_read = sem("y_read")
        b_var = sem("b_var")
        b_pow = sem("b_pow")
        x2_rows_ok = sem("x2_rows_ok")
        x2_ok = sem("x2_ok")
        c_staged = sem("c_staged")
        c_tr = sem("c_tr")
        c_xT = sem("c_xT")
        c_logit = sem("c_logit")
        c_logit_kept = sem("c_logit_kept")
        c_lm = sem("c_lm")
        c_exp = sem("c_exp")
        c_hot = sem("c_hot")
        c_rank_ps = sem("c_rank_ps")
        c_dest = sem("c_dest")
        c_scatter = sem("c_scatter")
        f_in = [sem(f"f_in{i}") for i in range(2)]
        f_tr = sem("f_tr")
        f_xT = sem("f_xT")
        f_h = sem("f_h")
        f_relu = sem("f_relu")
        f_y = sem("f_y")
        f_y_sb = sem("f_y_sb")
        g_var = sem("g_var")
        g_pow = sem("g_pow")
        f_out = sem("f_out")
        c_gather = [sem(f"c_gather{i}") for i in range(2)]
        g_ready = sem("g_ready")
        g_out = sem("g_out")

        RING = (4, 5, 7)
        NRB = len(RING)
        K_CHUNKS = [list(range(4 * c, min(4 * c + 4, KT))) for c in range(-(-KT // 4))]
        NC = len(K_CHUNKS)
        assert NC == 4
        CHUNKS = ([("v", 0, c) for c in range(NC)] + [("t", 0, c) for c in range(NC - 1)] + [("q", 0, 0)] +
                  [("t", 0, NC - 1)] + [("t", u, c) for u in (1, 2, 3) for c in range(NC)])
        NRING = len(CHUNKS)
        assert NRING % NRB == 0
        AT = {key: i for i, key in enumerate(CHUNKS)}
        BY_ACT = {("v", 0): 1, ("t", 0): 1, ("t", 1): 2, ("t", 2): 2, ("t", 3): 2}
        OWNER = ["query" if kind == "q" else "act" if c < BY_ACT[kind, u] else "dve" for kind, u, c in CHUNKS]
        RING_ACT = OWNER.count("act")
        RING_DVE = OWNER.count("dve")

        RING_FULL = RING_ACT + RING_DVE

        def filled(i):
            return i + 1 - OWNER[:i + 1].count("query")

        QBANK = RING[AT[("q", 0, 0)] % NRB]

        def emptied(i):
            return OWNER[:i + 1].count("act"), OWNER[:i + 1].count("dve")

        C_IN = ctx.rearrange("b k d -> (b k) d")

        block = stack.enter_context(nc.Block())

        @block.sync
        def _(sp):
            for held in (f_out, g_out,):
                sp.sem_inc(held, HELD)
            def load(dst, src, loaded=weights_in):
                sp.dma_start(dst, src).then_inc(loaded, 16)

            for m, w in enumerate((Wr, Wk, Wv, Wo)):
                load(w_rows[:, m, :], w, tern_in)
            load(decay_c[:, :], decay.rearrange("(d a) -> d a", a=1), tern_in)
            load(lnw_c[:, :], ln_w.rearrange("(d a) -> d a", a=1), tern_in)
            load(wq_rows, xWq, qk_in)
            load(wk_rows, xWk, qk_in)
            load(wv_rows[:, :], xWv)
            load(wo_rows[:, :, :], xWo.rearrange("(j p) n -> p j n", p=P))
            with nc.allow_non_contiguous_dma(reason="biases laid over the partitions, 4 KB each"):
                load(bq_c[:, :], xbq.rearrange("(j p) -> p j", p=P))
                load(bk_c[:, :], xbk.rearrange("(j p) -> p j", p=P))
                load(bv_c[:, :], xbv.rearrange("(j p) -> p j", p=P))
            load(bo_b[:, :], xbo.rearrange("(a n) -> a n", a=1).broadcast_to([P, P]))
            load(fwr_sb[:, :], fWr)
            sp.wait_ge(consts_ready, 1)
            for s in range(SLOTS // P):
                sp.dma_start(xe_dram[s * P:(s + 1) * P, :], zeros[:, :]).then_inc(slots_zeroed, 16)
            sp.dma_start(ye_dram[SLOTS:SLOTS + 1, :], zeros[0:1, :]).then_inc(slots_zeroed, 16)
            def load_tokens(i, dst, loaded):
                sp.dma_start(dst[:, :, :], x[bass.ds(i * 2, 2)].rearrange(
                    "b (t p) d -> p (b t) d", p=P)).then_inc(loaded, 16)

            load_tokens(0, xs, a_x)
            with sp.Fori(0, AB - 1) as i:
                sp.wait_ge(a_xT_ps, i + 1 + HELD)
                load_tokens(i + 1, xs, a_x)
                sp.wait_ge(a_h, i + HELD)
                load_tokens(i, xres, a_xres)
            sp.wait_ge(a_h, AB - 1 + HELD)
            load_tokens(AB - 1, xres, a_xres)
            def load_context(b):
                sp.dma_start(ctx_raw[:, 0:KT - 1, :], C_IN[bass.ds(b * KEYS, (KT - 1) * P)].rearrange(
                    "(t p) d -> p t d", p=P)).then_inc(ctx_in, 16)
                sp.dma_start(ctx_raw[0:KREM, KT - 1, :],
                             C_IN[bass.ds(b * KEYS + (KT - 1) * P, KREM)]).then_inc(ctx_in, 16)

            load_context(0)
            with sp.Fori(1, B) as b:
                sp.wait_ge(ctx_tr, b * NC + HELD)
                load_context(b)
            sp.wait_ge(ctx_tr, B * NC + HELD)
            load_context(0)
            def load_weights(i, s):
                sp.dma_start(w1_sb[:, s, :], fW1[bass.ds(i * 2 + s, 1)].rearrange(
                    "o d f -> (o d) f")).then_inc(f_in[s], 16)
                sp.dma_start(w2_sb[:, s, :, :], fW2[bass.ds(i * 2 + s, 1)].rearrange(
                    "o (c p) d -> p (o c) d", p=P)).then_inc(f_in[s], 16)

            def load_slots(i, s):
                sp.dma_start(xe[:, s, :, :], xe_dram[bass.ds(i * (2 * CAP) + s * CAP, CAP)].rearrange(
                    "(t p) d -> p t d", p=P)).then_inc(f_in[s], 16)

            def store_outputs(i, s):
                sp.wait_ge(f_y_sb, i * 2 + s + 1 + HELD)
                sp.dma_start(ye_dram[bass.ds(i * (2 * CAP) + s * CAP, CAP)].rearrange(
                    "(t p) d -> p t d", p=P), ye[:, s, :, :]).then_inc(f_out, 16)

            load_weights(0, 0)
            load_weights(0, 1)
            sp.wait_ge(c_scatter, 16 * NT)
            load_slots(0, 0)
            load_slots(0, 1)
            with sp.Fori(0, E // 2 - 1) as i:
                for s in range(2):
                    sp.wait_ge(f_y, i * 2 + s + 1 + HELD)
                    load_slots(i + 1, s)
                    load_weights(i + 1, s)
                for s in range(2):
                    store_outputs(i, s)
            store_outputs(E // 2 - 1, 0)
            store_outputs(E // 2 - 1, 1)
            with sp.Fori(0, NG) as g:
                sp.wait_ge(g_ready, g + 1)
                sp.dma_start(out[bass.ds(g * 2, 2)].rearrange("b (t p) d -> p (b t) d", p=P),
                             x1s[:, :, :]).then_inc(g_out, 16)
            sp.wait_ge(g_out, 16 * NG + HELD)

        @block.gpsimd
        def _(pool):
            for held in (a_x1_kept, x2_ok,):
                pool.sem_inc(held, HELD)
            own = Chain(pool, pool_own)
            nc.gpsimd.memset(zeros[:, :], 0.0).then_inc(consts_ready, 1)
            own(nc.gpsimd.memset(ident[:, :], 0.0))
            nc.gpsimd.affine_select(out=ident[:, :], in_=ident[:, :], compare_op=ALU.not_equal, fill=1.0,
                                    base=0, pattern=[[-1, P]], channel_multiplier=1).then_inc(masks_ready, 1)
            own(nc.gpsimd.memset(tri[:, :], 0.0))
            nc.gpsimd.affine_select(out=tri[:, :], in_=tri[:, :], compare_op=ALU.is_ge, fill=1.0,
                                    base=0, pattern=[[-1, P]], channel_multiplier=1).then_inc(masks_ready, 1)
            nc.gpsimd.memset(ones[:, :], 1.0).then_inc(masks_ready, 1)
            nc.gpsimd.memset(minus_half[:, :], -0.5).then_inc(masks_ready, 1)
            nc.gpsimd.iota(iota8[:, :, :], pattern=[[0, NT], [1, E]], base=0, channel_multiplier=0,
                           allow_small_or_imprecise_dtypes=True).then_inc(masks_ready, 1)
            nc.gpsimd.memset(wk_T[:, :, :, :], 0.0).then_inc(zero_parts, 1)
            own(nc.gpsimd.memset(v_pair[:, KT - 1, :], 0.0))
            own(nc.gpsimd.memset(prob[:, 0, :], 0.0))
            nc.gpsimd.memset(prob[:, 1, :], 0.0).then_inc(masks_ready, 1)
            pool.wait_ge(masks_ready, 4)

            def power(dst, src, ready, count, done):
                pool.wait_ge(ready, count)
                nc.gpsimd.tensor_tensor(dst, src, minus_half[:, 0:src.shape[-1]], ALU.pow).then_inc(done, 1)

            with pool.Fori(0, AB) as i:
                power(rms[:, :], ms[:, :], a_var, i * 2 + 1, a_pow)
                power(rstd[:, :], ve[:, :], a_var, i * 2 + 2, a_pow)
                pool.wait_ge(a_x1, i + 1)
                nc.gpsimd.tensor_copy(x_all[:, bass.ds(i * 4, 4), :], x1s[:, :, :]).then_inc(a_x1_kept, 1)

            def stage_tokens(b):
                pool.wait_ge(q_ps, b * NJ + HELD)
                nc.gpsimd.tensor_copy(x1T_cur[:, :], x1T_all[:, bass.ds(b * T, T)]).then_inc(x1T_staged, 1)

            def stage_pair(pair, j):
                pool.wait_ge(consts_ready, 1)
                pool.wait_ge(q_ps, pair + HELD)
                pool.wait_ge(q_f_ok, pair + HELD)
                nc.gpsimd.tensor_copy(m_cur[:, :, :], m_tab[:, bass.ds(j * 2, 2), :]).then_inc(m_staged, 1)
                nc.gpsimd.tensor_copy(qb_cur[:, :], qb_tab[:, bass.ds(j * 2, 2)]).then_inc(m_staged, 1)

            def finish_norm(b, n_batches):
                power(rstd[:, 0:QT], ve[:, 0:QT], b_var, n_batches, b_pow)
                pool.wait_ge(consts_ready, 1)
                pool.wait_ge(b_pow, n_batches)
                for qt in range(QT):
                    last = nc.gpsimd.tensor_scalar(x2_rows[:, qt, :], hrow[:, qt, :], mv[:, qt, 0:1],
                                                   rstd[:, qt:qt + 1], ALU.subtract, ALU.mult)
                last.then_inc(x2_rows_ok, 1)
                pool.wait_ge(x2_rows_ok, n_batches)
                nc.gpsimd.tensor_copy(x_all[:, bass.ds(b * QT, QT), :], x2_rows[:, :, :]).then_inc(x2_ok, 1)

            pool.wait_ge(a_x1T_kept, AB + HELD)
            stage_tokens(0)
            with pool.Fori(0, NJ) as j:
                stage_pair(j, j)
            with pool.Fori(1, B) as b:
                stage_tokens(b)
                stage_pair(b * NJ, 0)
                finish_norm(b - 1, b)
                with pool.Fori(1, NJ) as j:
                    stage_pair(b * NJ + j, j)
            stage_pair(B * NJ, 0)
            finish_norm(B - 1, B)

            pool.wait_ge(slots_zeroed, 16 * (SLOTS // P + 1))
            pool.wait_ge(c_dest, 1)
            for t in range(NT):
                nc.gpsimd.indirect_dma_start(
                    xe_dram[:, :], bass.IndirectOffsetOnAxis(ap=dest[:, t:t + 1], axis=0), x_all[:, t, :], None,
                    bounds_check=SLOTS - 1, oob_is_err=False).then_inc(c_scatter, 16)
            pool.wait_ge(f_out, 16 * E + HELD)
            for g in range(NG):
                if g >= 2:
                    pool.wait_ge(c_gather[g % 2], 64 * (g // 2))
                for t in range(4 * g, 4 * g + 4):
                    nc.gpsimd.indirect_dma_start(
                        y_all[:, t, :], None, ye_dram[:, :], bass.IndirectOffsetOnAxis(ap=dest[:, t:t + 1], axis=0),
                        bounds_check=SLOTS, oob_is_err=False).then_inc(c_gather[g % 2], 16)
                if g >= 1:
                    power(rstd[:, :], ve[:, :], g_var, g, g_pow)
            power(rstd[:, :], ve[:, :], g_var, NG, g_pow)

        @block.scalar
        def _(act):
            for held in (q_f_ok, a_x1T_kept, ring_act, f_relu,):
                act.sem_inc(held, HELD)
            act.sem_inc(exp_ok, HELD_EXP)
            copy = nc.scalar.copy
            act.wait_ge(tern_in, 16 * 6)
            nc.scalar.activation(dec[:, 0:1], decay_c[:, :], ACT.Exp, scale=-1.0).then_inc(decay_exp, 1)
            act.wait_ge(setup_tr, 1)
            copy(wq_T[:, :, :], ps[:, 1:3, :].rearrange("p a (b n) -> p (a b) n", n=P)).then_inc(setup_ev_act, 1)
            act.wait_ge(setup_tr, 3)
            copy(w_T[:, 0:3, :], ps[:, 0, 0:3 * P].rearrange("p (m n) -> p m n", m=3)).then_inc(setup_ev_act, 1)
            act.wait_ge(setup_mm, 1)
            nc.scalar.mul(m_tab[:, :, :], ps[:, 0:4, :].rearrange("p a (b n) -> p (a b) n", n=P), SCALE)\
                .then_inc(tables_act, 1)

            def tokens(i):
                act.wait_ge(a_xT_ps, i + 1 + HELD)
                copy(xT[:, :], ps[:, 0, :]).then_inc(a_xT, 1)

            def keys(i):
                act.wait_ge(a_rkv, i * 3 + 2)
                copy(ksb[:, :], ps[:, 2, :]).then_inc(a_gate, 1)

            def gate(i):
                act.wait_ge(a_rkv, i * 3 + 1)
                nc.scalar.activation(th[:, :], ps[:, 1, :], ACT.Tanh, scale=0.5).then_inc(a_gate, 1)

            def squares(i):
                act.wait_ge(a_y, i + 1)
                act.wait_ge(a_o, i * 2 + HELD)
                nc.scalar.activation(ysq[:, :], y[:, :], ACT.Square).then_inc(a_ysq, 1)

            def keep_x1T(i):
                act.wait_ge(a_x1T_ps, i + 1 + HELD)
                copy(x1Ts[:, :], ps[:, 6, :]).then_inc(a_x1T, 1)
                copy(x1T_all[:, bass.ds(i * AN, AN)], ps[:, 6, :]).then_inc(a_x1T_kept, 1)

            def step(i, first):
                tokens(i)
                act.wait_ge(a_kv, i)
                keys(i)
                squares(i - 1)
                gate(i)
                if not first:
                    keep_x1T(i - 2)

            tokens(0)
            keys(0)
            gate(0)
            step(1, True)
            with act.Fori(2, AB) as i:
                step(i, False)
            squares(AB - 1)
            keep_x1T(AB - 2)
            keep_x1T(AB - 1)

            def query_out(n_pairs):
                act.wait_ge(q_ps, n_pairs + HELD)
                nc.scalar.activation(q_f[:, 0, :], ps[:, QBANK, 0:T], ACT.Identity, bias=qb_cur[:, 0:1])
                nc.scalar.activation(q_f[:, 1, :], ps[:, QBANK, T:2 * T], ACT.Identity, bias=qb_cur[:, 1:2])\
                    .then_inc(q_f_ok, 1)

            def query_high(n_pairs):
                act.wait_ge(q_f_ok, n_pairs + HELD)
                copy(q_hi[:, :, :], q_f[:, :, :]).then_inc(q_hi_ok, 1)

            act.wait_ge(m_staged, 2)
            query_out(1)
            query_high(1)

            def context_high(n_batches):
                for c, tiles in enumerate(K_CHUNKS):
                    n = sum(P if k < KT - 1 else KREM for k in tiles)
                    k0 = tiles[0] * P
                    act.wait_ge(ctx_tr, n_batches * NC + c + 1 + HELD)
                    copy(ctx_hi[:, k0:k0 + n], ps[:, RING[c % NRB], 0:n]).then_inc(ctx_hi_ok, 1)
                    copy(ctx_f[:, k0:k0 + n], ps[:, RING[c % NRB], 0:n]).then_inc(ctx_f_ok, 1)

            context_high(0)
            with act.Fori(0, B) as b:
                with act.Fori(0, NJ) as j:
                    pair = b * NJ + j

                    def ring(key):
                        i = AT[key]
                        if OWNER[i] != "act":
                            return
                        kind, u, c = key
                        act.wait_ge(ring_full, pair * RING_FULL + filled(i))
                        src = ps[:, RING[i % NRB], :].rearrange("p (k n) -> p k n", n=P)
                        tiles = K_CHUNKS[c]
                        if kind == "v":
                            copy(v_pair[:, tiles[0]:tiles[-1] + 1, :], src[:, 0:len(tiles), :])\
                                .then_inc(ring_act, 1)
                        else:
                            copy(prob_T[:, u % 2, tiles[0]:tiles[-1] + 1, u // 2 * P:u // 2 * P + P],
                                 src[:, 0:len(tiles), :]).then_inc(ring_act, 1)

                    def exps(u):
                        act.wait_ge(row_max, pair * 4 + u + 1)
                        bias = nbias[:, u % 2:u % 2 + 1]
                        for c in range(4):
                            nc.scalar.activation(prob[:, u % 2, PART[c]:PART[c + 1]],
                                                 ps[:, c, PART[c] - KEY0[c]:PART[c + 1] - KEY0[c]], ACT.Exp,
                                                 bias=bias, accum_out=esum[:, u, c:c + 1]).then_inc(exp_ok, 1)

                    def spread(qt):
                        act.wait_ge(pv_ok, pair * 2 + qt + 1)
                        copy(rdT[:, qt, :], ps[:, 6, 2 * qt * P + P:2 * qt * P + 2 * P]).then_inc(rdT_ok, 1)

                    ring(("v", 0, 0))
                    exps(0)
                    for c in range(NC):
                        ring(("t", 0, c))
                    exps(1)
                    act.wait_ge(q_lo_ok, pair + 1 + HELD)
                    act.wait_ge(m_staged, pair * 2 + 4)
                    query_out(pair + 2)
                    for c in range(NC):
                        ring(("t", 1, c))
                    exps(2)
                    for c in range(NC):
                        ring(("t", 2, c))
                    exps(3)
                    spread(0)
                    for c in range(NC):
                        ring(("t", 3, c))
                    act.wait_ge(scores, pair * 16 + 16)
                    query_high(pair + 2)
                    spread(1)
                context_high(b + 1)

            with act.Fori(0, NG // 2) as i:
                for s in range(2):
                    act.wait_ge(c_tr, i * 2 + s + 1 + HELD)
                    copy(x2T[s], ps[:, s, :]).then_inc(c_xT, 1)
            act.wait_ge(c_lm, 1)
            nc.scalar.activation(ex[:, :, :], lm[:, :, :], ACT.Exp).then_inc(c_exp, 1)
            with act.Fori(0, E // 2) as i:
                for s in range(2):
                    act.wait_ge(f_tr, i * 2 + s + 1)
                    copy(xeT[:, s, :], ps[:, 0 + s, 0:CAP]).then_inc(f_xT, 1)
                    for f in range(FC):
                        act.wait_ge(f_h, i * (2 * FC) + s * FC + f + 1)
                        nc.scalar.activation(hT[:, s, f, :], ps[:, 2 + f, 0:CAP], ACT.Relu).then_inc(f_relu, 1)

        @block.vector
        def _(dve):
            for held in (a_h, q_lo_ok, ring_dve, norm_ok, y_read, c_logit_kept, f_y_sb, a_r,):
                dve.sem_inc(held, HELD)
            own = Chain(dve, dve_own)
            v = nc.vector
            dve.wait_ge(tern_in, 16 * 6)
            own(v.tensor_reduce(w_sum[:, :], w_rows[:, :, :], AX.X, ALU.add, apply_absolute_value=True))
            own(v.tensor_scalar(w_scale[:, :], w_sum[:, :], 1.0 / D, 1e-5, ALU.mult, ALU.max))
            own(v.tensor_scalar(w_half[:, :], w_scale[:, :], 0.5, None, ALU.mult))
            own(v.tensor_scalar(w_nhalf[:, :], w_scale[:, :], -0.5, None, ALU.mult))
            for m in range(4):
                own(v.tensor_scalar(w_tmp[:, m, :], w_rows[:, m, :], w_half[:, m:m + 1], None, ALU.is_gt))
                own(v.scalar_tensor_tensor(w_tern[:, m, :], w_rows[:, m, :], w_nhalf[:, m:m + 1],
                                           w_tmp[:, m, :], ALU.is_lt, ALU.subtract))
                own(v.scalar_tensor_tensor(w_tmp[:, m, :], w_tern[:, m, :], w_scale[:, m:m + 1],
                                           w_rows[:, m, :], ALU.mult, ALU.add))
                v.tensor_tensor(w_tern[:, m, :], w_rows[:, m, :], w_tmp[:, m, :], ALU.subtract)\
                    .then_inc(tern_ready, 1)
            dve.wait_ge(zero_parts, 1)
            dve.wait_ge(setup_tr, 2)
            v.tensor_copy(wk_T[0:64, 0, :, :], ps[0:64, 3:5, :].rearrange("p a (b n) -> p (a b) n", n=P))\
                .then_inc(setup_ev_dve, 1)
            v.tensor_copy(wk_T[64:P, 1, :, :], ps[64:P, 3:5, :].rearrange("p a (b n) -> p (a b) n", n=P))\
                .then_inc(setup_ev_dve, 1)
            dve.wait_ge(setup_tr, 3)
            dve.wait_ge(setup_ev_act, 2)
            v.tensor_scalar(w_T[:, 3, :], ps[:, 0, 3 * P:4 * P], lnw_c[:, :], None, ALU.mult)\
                .then_inc(setup_ev_dve, 1)
            own(v.memset(bk_m[:, :, :], 0.0))
            dve.wait_ge(weights_in, 16 * 7)
            v.tensor_copy(bk_m[0:64, :, 0], bk_c[0:64, :])
            v.tensor_copy(bk_m[64:P, :, 1], bk_c[64:P, :]).then_inc(setup_ev_dve, 1)
            dve.wait_ge(decay_exp, 1)
            own(v.tensor_scalar(dec[:, 1:2], dec[:, 0:1], 1.0, None, ALU.add))
            own(v.reciprocal(dec[:, 2:3], dec[:, 1:2]))
            own(v.tensor_scalar(dec[:, 3:4], dec[:, 2:3], 1e-7, None, ALU.max))
            own(v.memset(carry[:, :, :], 0.0))
            own(v.memset(scale_t[:, :, 0:1], 1.0))
            own(v.tensor_tensor_scan(scale_t[:, 0, 1:T], dec[:, 3:4].broadcast_to([P, T - 1]), carry[:, 0, 1:T],
                                     1.0, ALU.mult, ALU.add))
            own(v.tensor_copy(scale_t[:, 1, :], scale_t[:, 0, :]))
            own(v.tensor_scalar(half_scale[:, :, :], scale_t[:, :, :], 0.5, None, ALU.mult))
            own(v.tensor_scalar(inv_scale[:, :, :], scale_t[:, :, :], 1e-10, None, ALU.max))
            own(v.reciprocal(scale_t[:, :, :], inv_scale[:, :, :]))
            own(v.tensor_copy(inv_scale[:, :, :], scale_t[:, :, :]))
            own(v.memset(carry[:, :, 1:T], 1.0))
            own(v.memset(ctx_hi[:, KEYS:KPAD].bitcast(F32), 0.0))
            own(v.memset(ctx_lo[:, KEYS:KPAD].bitcast(F32), 0.0))
            dve.wait_ge(setup_mm, 2)
            v.tensor_scalar(qb_tab[:, :], ps[:, 5, 0:H], SCALE, None, ALU.mult).then_inc(tables_dve, 1)
            v.tensor_scalar(kb_tab[:, :], ps[:, 5, H:2 * H], SCALE, None, ALU.mult).then_inc(tables_dve, 1)
            v.tensor_scalar(kb_const[:, :], ps[:, 5, 2 * H:3 * H], SCALE, None, ALU.mult).then_inc(tables_dve, 1)
            v.tensor_tensor(bo_all[:, :], ps[:, 6, 0:P], bo_b[:, :], ALU.add).then_inc(tables_dve, 1)
            dve.wait_ge(tables_dve, 4)

            def carry_wait(n=0):
                v.memset(pad[:, n:n + 1], 0.0)

            def moments(tiles):
                for t in range(tiles):
                    last = v.bn_stats(stats[:, t, :], hrow[:, t, :])
                own(last)
                carry_wait()
                for t in range(tiles):
                    last = v.bn_aggr(mv[:, t, :], stats[:, t, :])
                own(last)

            flat = lambda a: a[:, :, :].rearrange("p b t -> p (b t)")

            def key_value(i):
                dve.wait_ge(a_gate, i * 2 + 1)
                dve.wait_ge(a_rkv, i * 3 + 3)
                v.tensor_tensor(t1[:, :], ksb[:, :], ps[:, 3, :], ALU.mult).then_inc(a_kv, 1)
                dve.wait_ge(a_kv, i + 1)
                v.tensor_tensor(t2[:, :], t1[:, :], flat(inv_scale), ALU.mult).then_inc(a_kv2, 1)

            def state(i):
                dve.wait_ge(a_kv2, i + 1)
                own(v.tensor_tensor_scan(t1[:, :], flat(carry), t2[:, :], 0.0, ALU.mult, ALU.add))
                v.tensor_tensor(t2[:, :], t1[:, :], flat(half_scale), ALU.mult).then_inc(a_state, 1)

            def gated(i):
                dve.wait_ge(a_gate, i * 2 + 2)
                dve.wait_ge(a_state, i + 1)
                v.scalar_tensor_tensor(y[:, :], th[:, :], 1.0, t2[:, :], ALU.add, ALU.mult).then_inc(a_y, 1)

            def mean_square(i):
                dve.wait_ge(a_o, i * 2 + 2 + HELD)
                v.tensor_scalar(ms[:, :], ps[:, 5, 0:4], 1.0 / D, 1e-6, ALU.mult, ALU.add).then_inc(a_var, 1)

            def residual(i):
                dve.wait_ge(a_xres, i * 16 + 16)
                dve.wait_ge(a_pow, i * 2 + 1)
                for t in range(4):
                    last = v.scalar_tensor_tensor(hrow[:, t, :], ps[:, 4, t * P:t * P + P], rms[:, t:t + 1],
                                                  xres[:, t, :], ALU.mult, ALU.add)
                last.then_inc(a_h, 1)
                dve.wait_ge(a_h, i + 1 + HELD)
                moments(4)
                v.tensor_scalar(ve[:, :], mv[:, :, 1], 1e-5, None, ALU.add).then_inc(a_var, 1)

            def normed(i):
                dve.wait_ge(a_pow, i * 2 + 2)
                dve.wait_ge(a_x1_kept, i + HELD)
                dve.wait_ge(a_x1T_ps, i + HELD)
                for t in range(4):
                    last = v.tensor_scalar(x1s[:, t, :], hrow[:, t, :], mv[:, t, 0:1], rstd[:, t:t + 1],
                                           ALU.subtract, ALU.mult)
                last.then_inc(a_x1, 1)

            def row_parts(i):
                dve.wait_ge(a_r_ps, i + 1)
                for bb in range(2):
                    for qt in range(QT):
                        t = bb * QT + qt
                        last = v.tensor_tensor(r_all[:, bass.ds(i * 2 * NJ + bb * NJ, NJ), 2 * qt:2 * qt + 2],
                                               ps[:, 7, t * H:t * H + H].rearrange("p (j h) -> p j h", h=2),
                                               kb_const[:, :].rearrange("p (j h) -> p j h", h=2), ALU.add)
                last.then_inc(a_r, 1)

            key_value(0)
            state(0)
            gated(0)

            def step(i, first):
                key_value(i)
                mean_square(i - 1)
                state(i)
                residual(i - 1)
                gated(i)
                if not first:
                    row_parts(i - 2)
                normed(i - 1)

            step(1, True)
            with dve.Fori(2, AB) as i:
                own.enter(i - 2, 1 + 2)
                step(i, False)
            own.leave(AB - 2)
            mean_square(AB - 1)
            residual(AB - 1)
            row_parts(AB - 2)
            normed(AB - 1)
            row_parts(AB - 1)
            dve.wait_ge(a_r, AB + HELD)

            def query_low(n_pairs):
                dve.wait_ge(q_hi_ok, n_pairs)
                v.tensor_tensor(q_lo[:, :, :], q_f[:, :, :], q_hi[:, :, :].bitcast(F32), ALU.subtract)\
                    .then_inc(q_lo_ok, 1)

            query_low(1)
            PAIR_STEPS = 1 + 4 * 2 + 2 * 2

            def context_low(n_batches):
                for c, tiles in enumerate(K_CHUNKS):
                    n = sum(P if k < KT - 1 else KREM for k in tiles)
                    k0 = tiles[0] * P
                    dve.wait_ge(ctx_f_ok, n_batches * NC + c + 1)
                    v.tensor_tensor(ctx_lo[:, k0:k0 + n], ctx_f[:, k0:k0 + n],
                                    ctx_hi[:, k0:k0 + n].bitcast(F32), ALU.subtract).then_inc(ctx_lo_ok, 1)

            def stage_r(pair):
                own(v.tensor_copy(r_cur[:, :, :], r_all[:, bass.ds(pair, 1), :]))

            context_low(0)
            own(v.memset(r_all[:, B * NJ:B * NJ + 1, :], 0.0))
            own(v.tensor_copy(r_cur[:, :, :], r_all[:, 0:1, :]))
            with dve.Fori(0, B) as b:
                start = own.base + own.steps
                EPI = 1 + 2
                with dve.Fori(0, NJ) as j:
                    pair = b * NJ + j
                    own.base, own.steps = start + b * (NJ * PAIR_STEPS + EPI) + j * PAIR_STEPS, 0

                    def ring(key):
                        i = AT[key]
                        if OWNER[i] != "dve":
                            return
                        kind, u, c = key
                        dve.wait_ge(ring_full, pair * RING_FULL + filled(i))
                        src = ps[:, RING[i % NRB], :].rearrange("p (k n) -> p k n", n=P)
                        tiles = K_CHUNKS[c]
                        if kind == "v":
                            rows = KREM if tiles[-1] == KT - 1 else P
                            v.tensor_copy(v_pair[0:rows, tiles[0]:tiles[-1] + 1, :],
                                          src[0:rows, 0:len(tiles), :]).then_inc(ring_dve, 1)
                        else:
                            v.tensor_copy(prob_T[:, u % 2, tiles[0]:tiles[-1] + 1, u // 2 * P:u // 2 * P + P],
                                          src[:, 0:len(tiles), :]).then_inc(ring_dve, 1)

                    def maxima(u):
                        s = u % 2
                        for c in range(4):
                            dve.wait_ge(scores, pair * 16 + 4 * u + c + 1)
                            last = v.tensor_reduce(mx[:, s, c:c + 1], ps[:, c, 0:WID[c]], AX.X, ALU.max)
                        own(last)
                        own(v.tensor_reduce(nmx[:, s:s + 1], mx[:, s, :], AX.X, ALU.max, negate=True))
                        r = r_cur[:, 0, u:u + 1]
                        v.scalar_tensor_tensor(nbias[:, s:s + 1], nmx[:, s:s + 1], r, r, ALU.subtract,
                                               ALU.add).then_inc(row_max, 1)

                    def row_sums(qt):
                        dve.wait_ge(exp_ok, pair * 16 + 8 * qt + 8 + HELD_EXP)
                        own(v.tensor_reduce(den[:, 2 * qt:2 * qt + 2], esum[:, 2 * qt:2 * qt + 2, :], AX.X, ALU.add))
                        own(v.reciprocal(rden[:, 2 * qt:2 * qt + 2], den[:, 2 * qt:2 * qt + 2]))
                        v.tensor_copy(rspread[:, qt, :].rearrange("p (h d) -> p h d", h=2),
                                      rden[:, 2 * qt:2 * qt + 2, None].broadcast_to([P, 2, DH])).then_inc(rden_ok, 1)

                    def normalise(qt):
                        dve.wait_ge(rdT_ok, pair * 2 + qt + 1)
                        v.tensor_tensor(heads_T[:, bass.ds(j, 1), qt * P:qt * P + P],
                                        ps[:, 6, 2 * qt * P:2 * qt * P + P].rearrange("p (a n) -> p a n", a=1),
                                        rdT[:, qt:qt + 1, :], ALU.mult).then_inc(norm_ok, 1)

                    maxima(0)
                    for c in range(NC):
                        ring(("v", 0, c))
                    maxima(1)
                    for c in range(NC):
                        ring(("t", 0, c))
                    maxima(2)
                    for c in range(NC):
                        ring(("t", 1, c))
                    row_sums(0)
                    maxima(3)
                    for c in range(NC):
                        ring(("t", 2, c))
                    row_sums(1)
                    normalise(0)
                    for c in range(NC):
                        ring(("t", 3, c))
                    query_low(pair + 2)
                    dve.wait_ge(row_max, pair * 4 + 4)
                    stage_r(pair + 1)
                    normalise(1)
                assert own.steps == PAIR_STEPS, own.steps
                own.base, own.steps = start + b * (NJ * PAIR_STEPS + EPI) + NJ * PAIR_STEPS, 0
                context_low(b + 1)
                dve.wait_ge(a_x1_kept, AB + HELD)
                dve.wait_ge(x2_ok, b + HELD)
                own(v.tensor_tensor(hrow[:, 0:QT, :], x_all[:, bass.ds(b * QT, QT), :],
                                    bo_all[:, None, :].broadcast_to([P, QT, P]), ALU.add))
                dve.wait_ge(y_ps, b + 1)
                v.tensor_tensor(hrow[:, 0:QT, :], ps[:, 6, 0:QT * P].rearrange("p (t n) -> p t n", n=P),
                                hrow[:, 0:QT, :], ALU.add)\
                    .then_inc(y_read, 1)
                dve.wait_ge(y_read, b + 1 + HELD)
                moments(QT)
                v.tensor_scalar(ve[:, 0:QT], mv[:, 0:QT, 1], 1e-5, None, ALU.add).then_inc(b_var, 1)
                assert own.steps == EPI, own.steps
            own.base, own.steps = start + B * (NJ * PAIR_STEPS + EPI), 0
            dve.wait_ge(x2_ok, B + HELD)

            with dve.Fori(0, NG // 2) as i:
                dve.wait_ge(c_tr, i * 2 + HELD)
                carry_wait()
                for s in range(2):
                    v.tensor_copy(x2s[s], x_all[:, bass.ds(i * 8 + 4 * s, 4), :]).then_inc(c_staged, 1)
                for s in range(2):
                    dve.wait_ge(c_logit, i * 2 + s + 1)
                    carry_wait(1 + s)
                    v.tensor_copy(logit[:, bass.ds(i * 8 + 4 * s, 4), :],
                                  ps[:, 2 + s, 0:4 * E].rearrange("p (t e) -> p t e", e=E)).then_inc(c_logit_kept, 1)
            dve.wait_ge(c_logit_kept, NG + HELD)
            over = lambda a: a[:, :, None].broadcast_to([P, NT, E])
            own(v.tensor_reduce(tmax[:, :], logit[:, :, :], AX.X, ALU.max))
            v.tensor_tensor(lm[:, :, :], logit[:, :, :], over(tmax), ALU.subtract).then_inc(c_lm, 1)
            dve.wait_ge(c_lm, 1)
            own(v.tensor_scalar(rk[:, :, :], lm[:, :, :], 0.0, None, ALU.is_ge))
            own(v.scalar_tensor_tensor(one_hot[:, :, :].rearrange("p t e -> p (t e)"),
                                       rk[:, :, :].rearrange("p t e -> p (t e)"), -float(E),
                                       iota8[:, :, :].rearrange("p t e -> p (t e)"), ALU.mult, ALU.add))
            own(v.tensor_reduce(vmin[:, :], one_hot[:, :, :], AX.X, ALU.min))
            v.tensor_tensor(rk[:, :, :], one_hot[:, :, :], over(vmin), ALU.is_equal).then_inc(c_hot, 1)
            dve.wait_ge(c_exp, 1)
            own(v.tensor_reduce(tden[:, :], ex[:, :, :], AX.X, ALU.add))
            own(v.reciprocal(ptok[:, :], tden[:, :]))
            own(v.memset(cmask[:, :, :], 1.0))
            own(v.memset(cmask[:, :, 0:1], 0.0))
            dve.wait_ge(c_rank_ps, 2)
            own(v.tensor_copy(tot[:, :, :], ps[:, 1, 0:NT * E].rearrange("p (t e) -> p e t", e=E)))
            own(v.tensor_tensor_scan(csum[:, :, :].rearrange("p e t -> p (e t)"),
                                     cmask[:, :, :].rearrange("p e t -> p (e t)"),
                                     tot[:, :, :].rearrange("p e t -> p (e t)"), 0.0, ALU.mult, ALU.add))
            own(v.tensor_tensor(cmask[:, :, :], csum[:, :, :], tot[:, :, :], ALU.subtract))
            own(v.tensor_tensor(lm[:, :, :], ps[:, 0, 0:NT * E].rearrange("p (t e) -> p t e", e=E),
                                cmask[:, :, :].rearrange("p e t -> p t e"), ALU.add))
            own(v.tensor_tensor(ex[:, :, :], lm[:, :, :], rk[:, :, :], ALU.mult))
            own(v.tensor_reduce(rank[:, :], ex[:, :, :], AX.X, ALU.add))
            own(v.tensor_scalar(keep[:, :], rank[:, :], float(CAP), None, ALU.is_lt))
            own(v.scalar_tensor_tensor(slot[:, :], vmin[:, :], float(CAP), rank[:, :], ALU.mult, ALU.add))
            own(v.tensor_scalar(tmax[:, :], slot[:, :], float(E * CAP - SLOTS), None, ALU.add))
            own(v.tensor_tensor(slot[:, :], tmax[:, :], keep[:, :], ALU.mult))
            own(v.tensor_tensor(tden[:, :], ptok[:, :], keep[:, :], ALU.mult))
            v.tensor_scalar(dest[:, :], slot[:, :], float(SLOTS), None, ALU.add).then_inc(c_dest, 1)

            with dve.Fori(0, E // 2) as i:
                for s in range(2):
                    dve.wait_ge(f_y, i * 2 + s + 1 + HELD)
                    dve.wait_ge(f_out, i * 32 + HELD)
                    v.tensor_copy(ye[:, s, :, :], ps[:, 6 + s, 0:ST * P].rearrange("p (t n) -> p t n", n=P))\
                        .then_inc(f_y_sb, 1)

            with dve.Fori(0, NG // 2) as i:
                own.enter(i, 2 * (1 + 1 + 2))
                for s in range(2):
                    n0 = i * 8 + 4 * s
                    dve.wait_ge(c_gather[s], i * 64 + 64)
                    carry_wait(1 + s)
                    for t in range(4):
                        last = v.tensor_scalar(t1[:, t * P:t * P + P],
                                               y_all[:, bass.ds(n0 + t, 1), :].rearrange("p a n -> p (a n)"),
                                               tden[:, bass.ds(n0 + t, 1)], None, ALU.mult)
                    own(last)
                    own(v.tensor_tensor(hrow[:, :, :], t1[:, :].rearrange("p (t n) -> p t n", n=P),
                                        x_all[:, bass.ds(n0, 4), :], ALU.add))
                    moments(4)
                    v.tensor_scalar(ve[:, :], mv[:, :, 1], 1e-5, None, ALU.add).then_inc(g_var, 1)
                    dve.wait_ge(g_pow, i * 2 + s + 1)
                    dve.wait_ge(g_out, (i * 2 + s) * 16 + HELD)
                    for t in range(4):
                        last = v.tensor_scalar(x1s[:, t, :], hrow[:, t, :], mv[:, t, 0:1], rstd[:, t:t + 1],
                                               ALU.subtract, ALU.mult)
                    last.then_inc(g_ready, 1)
            own.leave(NG // 2)

        @block.tensor
        def _(pe):
            for held in (ctx_tr, q_ps, c_tr, a_x1T_ps, a_xT_ps, a_o, f_y,):
                pe.sem_inc(held, HELD)
            mm = nc.tensor.matmul
            tr = nc.tensor.transpose
            pe.wait_ge(masks_ready, 6)
            pe.wait_ge(qk_in, 16 * 2)
            for j in range(NJ):
                last = tr(ps[:, 1 + j // 4, j % 4 * P:j % 4 * P + P], wq_rows[:, j * P:j * P + P], ident[:, :])
            last.then_inc(setup_tr, 1)
            for j in range(NJ):
                last = tr(ps[:, 3 + j // 4, j % 4 * P:j % 4 * P + P], wk_rows[:, j * P:j * P + P], ident[:, :])
            last.then_inc(setup_tr, 1)
            pe.wait_ge(tern_ready, 4)
            for m in range(4):
                last = tr(ps[:, 0, m * P:m * P + P], w_tern[:, m, :], ident[:, :])
            last.then_inc(setup_tr, 1)
            pe.wait_ge(setup_ev_act, 2)
            pe.wait_ge(setup_ev_dve, 3)
            for h in range(H):
                last = mm(ps[:, h // 4, h % 4 * P:h % 4 * P + P], wq_T[:, h // 2, :], wk_T[:, h % 2, h // 2, :],
                          start=True, stop=True)
            last.then_inc(setup_mm, 1)
            pe.wait_ge(weights_in, 16 * 7)
            pe.wait_ge(setup_ev_dve, 4)
            for h in range(H):
                mm(ps[:, 5, h:h + 1], wk_T[:, h % 2, h // 2, :], bq_c[:, h // 2:h // 2 + 1], start=True, stop=True)
            for j in range(NJ):
                mm(ps[:, 5, H + 2 * j:H + 2 * j + 2], wq_T[:, j, :], bk_m[:, j, :], start=True, stop=True)
            for j in range(NJ):
                mm(ps[:, 5, 2 * H + 2 * j:2 * H + 2 * j + 2], bq_c[:, j:j + 1].broadcast_to([P, P]), bk_m[:, j, :],
                   start=True, stop=True)
            for j in range(NJ):
                last = mm(ps[:, 6, 0:P], bv_c[:, j:j + 1].broadcast_to([P, P]), wo_rows[:, j, :],
                          start=(j == 0), stop=(j == NJ - 1))
            last.then_inc(setup_mm, 1)
            pe.wait_ge(tables_act, 1)
            pe.wait_ge(tables_dve, 4)

            def token_transposes(i):
                pe.wait_ge(a_x, i * 16 + 16)
                for t in range(4):
                    last = tr(ps[:, 0, t * P:t * P + P], xs[:, t, :], ident[:, :])
                last.then_inc(a_xT_ps, 1)

            def rkv(i):
                pe.wait_ge(a_xT, i + 1)
                for m in range(3):
                    mm(ps[:, 1 + m, :], w_T[:, m, :], xT[:, :], start=True, stop=True).then_inc(a_rkv, 1)

            def out_product(i):
                pe.wait_ge(a_y, i + 1)
                for t in range(4):
                    last = mm(ps[:, 4, t * P:t * P + P], y[:, t * P:t * P + P], w_T[:, 3, :], start=True, stop=True)
                last.then_inc(a_o, 1)
                pe.wait_ge(a_ysq, i + 1)
                for t in range(4):
                    last = mm(ps[:, 5, t:t + 1], ysq[:, t * P:t * P + P], ones[:, 0:1], start=True, stop=True)
                last.then_inc(a_o, 1)

            def x1_products(i):
                pe.wait_ge(a_x1, i + 1)
                pe.wait_ge(a_x1T_kept, i + HELD)
                for t in range(4):
                    last = tr(ps[:, 6, t * P:t * P + P], x1s[:, t, :], ident[:, :])
                last.then_inc(a_x1T_ps, 1)
                pe.wait_ge(a_x1T, i + 1)
                pe.wait_ge(a_r, i + HELD)
                for t in range(4):
                    last = mm(ps[:, 7, t * H:t * H + H], x1Ts[:, t * P:t * P + P], kb_tab[:, :], start=True, stop=True)
                last.then_inc(a_r_ps, 1)

            def step(i, first):
                token_transposes(i)
                pe.wait_ge(a_gate, i * 2)
                pe.wait_ge(a_kv, i)
                rkv(i)
                out_product(i - 1)
                if not first:
                    x1_products(i - 2)

            token_transposes(0)
            rkv(0)
            step(1, True)
            with pe.Fori(2, AB) as i:
                step(i, False)
            out_product(AB - 1)
            x1_products(AB - 2)
            x1_products(AB - 1)
            pe.wait_ge(a_r, AB + HELD)
            pe.wait_ge(a_x1T_kept, AB + HELD)

            def queries():
                for h in range(2):
                    last = mm(ps[:, QBANK, h * T:h * T + T], m_cur[:, h, :], x1T_cur[:, :], start=True, stop=True)
                last.then_inc(q_ps, 1)

            pe.wait_ge(x1T_staged, 1)
            pe.wait_ge(m_staged, 2)
            queries()

            def context(n_batches, chunks):
                for c in chunks:
                    if c == 0:
                        pe.wait_ge(ctx_in, n_batches * 32 + 32)
                    if c >= NRB:
                        pe.wait_ge(ctx_f_ok, n_batches * NC + c - NRB + 1)
                    for n, k in enumerate(K_CHUNKS[c]):
                        rows = P if k < KT - 1 else KREM
                        last = tr(ps[:, RING[c % NRB], n * P:n * P + rows], ctx_raw[0:rows, k, :],
                                  ident[0:rows, 0:rows])
                    last.then_inc(ctx_tr, 1)

            pe.wait_ge(q_f_ok, 1 + HELD)
            context(0, range(NC))
            EARLY = 1
            with pe.Fori(0, B) as b:
                with pe.Fori(0, NJ) as j:
                    pair = b * NJ + j

                    def unit_scores(u):
                        h, q0 = u % 2, u // 2 * P
                        for c in range(4):
                            pe.wait_ge(exp_ok, pair * 16 + 4 * (u - 1) + c + 1 + HELD_EXP)
                            o = ps[:, c, 0:WID[c]]
                            k0, k1 = KEY0[c], KEY0[c] + WID[c]
                            mm(o, q_hi[:, h, q0:q0 + P], ctx_hi[:, k0:k1], start=True, stop=False)
                            mm(o, q_hi[:, h, q0:q0 + P], ctx_lo[:, k0:k1], start=False, stop=False)
                            mm(o, q_lo[:, h, q0:q0 + P], ctx_hi[:, k0:k1], start=False, stop=True)\
                                .then_inc(scores, 1)

                    def ring(key):
                        i = AT[key]
                        kind, u, c = key
                        if i >= NRB:
                            na, nd = emptied(i - NRB)
                            if OWNER[i - NRB] == "act":
                                pe.wait_ge(ring_act, pair * RING_ACT + na + HELD)
                            elif OWNER[i - NRB] == "dve":
                                pe.wait_ge(ring_dve, pair * RING_DVE + nd + HELD)
                            else:
                                pe.wait_ge(q_f_ok, pair + 2 + HELD)
                        if kind == "q":
                            pe.wait_ge(m_staged, pair * 2 + 4)
                            queries()
                            return
                        bank = RING[i % NRB]
                        for n, k in enumerate(K_CHUNKS[c]):
                            if kind == "v":
                                rows = P if k < KT - 1 else KREM
                                last = mm(ps[0:rows, bank, n * P:n * P + P], ctx_f[:, k * P:k * P + rows],
                                          wv_rows[:, bass.ds(j * P, P)], start=True, stop=True)
                            else:
                                last = tr(ps[:, bank, n * P:n * P + P], prob[:, u % 2, k * P:k * P + P], ident[:, :])
                        last.then_inc(ring_full, 1)

                    def transposed(u):
                        for c in range(NC):
                            parts = next(n for n in range(1, 5) if PART[n] >= min(KEYS, (K_CHUNKS[c][-1] + 1) * P))
                            pe.wait_ge(exp_ok, pair * 16 + 4 * u + parts + HELD_EXP)
                            if (u, c) == (0, NC - 1):
                                ring(("q", 0, 0))
                            ring(("t", u, c))

                    def values(qt, chunks, last_filled):
                        col = 2 * qt * P
                        for c in chunks:
                            i = AT["t", 2 * qt + 1, c]
                            if i > last_filled - NRB:
                                na, nd = emptied(i)
                                if OWNER[i] == "act":
                                    pe.wait_ge(ring_act, pair * RING_ACT + na + HELD)
                                else:
                                    pe.wait_ge(ring_dve, pair * RING_DVE + nd + HELD)
                            for k, h in ((k, h) for k in K_CHUNKS[c] for h in range(2)):
                                mm(ps[h * DH:h * DH + DH, 6, col:col + P], v_pair[:, k, h * DH:h * DH + DH],
                                   prob_T[:, h, k, qt * P:qt * P + P], start=(k == 0), stop=(k == KT - 1))
                        if c == NC - 1:
                            pe.wait_ge(rden_ok, pair * 2 + qt + 1)
                            tr(ps[:, 6, col + P:col + 2 * P], rspread[:, qt, :], ident[:, :]).then_inc(pv_ok, 1)

                    pe.wait_ge(ctx_f_ok, b * NC + NC)
                    pe.wait_ge(ctx_lo_ok, b * NC + NC)
                    pe.wait_ge(q_lo_ok, pair + 1 + HELD)
                    unit_scores(0)
                    for c in range(NC):
                        ring(("v", 0, c))
                    unit_scores(1)
                    transposed(0)
                    pe.wait_ge(norm_ok, pair * 2 + HELD)
                    pe.wait_ge(y_read, b + HELD)
                    unit_scores(2)
                    transposed(1)
                    values(0, range(0, EARLY), AT["t", 1, NC - 1])
                    unit_scores(3)
                    transposed(2)
                    values(0, range(EARLY, NC), AT["t", 2, NC - 1])
                    transposed(3)
                    pe.wait_ge(norm_ok, pair * 2 + 1 + HELD)
                    values(1, range(NC), AT["t", 3, NC - 1])
                context(b + 1, range(NC - 1))
                pe.wait_ge(norm_ok, b * (2 * NJ) + 2 * NJ + HELD)
                for qt in range(QT):
                    for jj in range(NJ):
                        last = mm(ps[:, 6, qt * P:qt * P + P], heads_T[:, jj, qt * P:qt * P + P],
                                  wo_rows[:, jj, :], start=(jj == 0), stop=(jj == NJ - 1))
                    if qt == 0:
                        context(b + 1, [NC - 1])
                last.then_inc(y_ps, 1)
            pe.wait_ge(y_read, B + HELD)
            pe.wait_ge(q_lo_ok, B * NJ + 1 + HELD)

            with pe.Fori(0, NG // 2) as i:
                for s in range(2):
                    pe.wait_ge(c_staged, i * 2 + s + 1)
                    for t in range(4):
                        last = tr(ps[:, s, t * P:t * P + P], x2s[s][:, t, :], ident[:, :])
                    last.then_inc(c_tr, 1)
                for s in range(2):
                    pe.wait_ge(c_xT, i * 2 + s + 1)
                    pe.wait_ge(c_logit_kept, i * 2 + HELD)
                    for t in range(4):
                        last = mm(ps[:, 2 + s, t * E:t * E + E], x2T[s][:, t * P:t * P + P], fwr_sb[:, :],
                                  start=True, stop=True)
                    last.then_inc(c_logit, 1)
            pe.wait_ge(c_hot, 1)
            hot = rk[:, :, :].rearrange("p t e -> p (t e)")
            mm(ps[:, 0, 0:NT * E], tri[:, :], hot, start=True, stop=True).then_inc(c_rank_ps, 1)
            mm(ps[:, 1, 0:NT * E], ones[:, :], hot, start=True, stop=True).then_inc(c_rank_ps, 1)
            pe.wait_ge(c_dest, 1)

            with pe.Fori(0, E // 2) as i:
                for s in range(2):
                    pe.wait_ge(f_in[s], i * 48 + 48)
                    for t in range(ST):
                        last = tr(ps[:, s, t * P:t * P + P], xe[:, s, t, :], ident[:, :])
                    last.then_inc(f_tr, 1)
                    pe.wait_ge(f_xT, i * 2 + s + 1)
                    pe.wait_ge(f_relu, i * (2 * FC) + s * FC + HELD)
                    for f in range(FC):
                        mm(ps[:, 2 + f, 0:CAP], w1_sb[:, s, f * P:f * P + P], xeT[:, s, :], start=True, stop=True)\
                            .then_inc(f_h, 1)
                    pe.wait_ge(f_relu, i * (2 * FC) + s * FC + FC + HELD)
                    pe.wait_ge(f_y_sb, i * 2 + HELD)
                    for t in range(ST):
                        for f in range(FC):
                            last = mm(ps[:, 6 + s, t * P:t * P + P], hT[:, s, f, t * P:t * P + P],
                                      w2_sb[:, s, f, :], start=(f == 0), stop=(f == FC - 1))
                    last.then_inc(f_y, 1)


_INS = ['x', 'ctx_1024', 'L0_attn_Wr', 'L0_attn_Wk', 'L0_attn_Wv', 'L0_attn_Wo', 'L0_attn_decay', 'L0_attn_ln_w',
        'L0_xattn_Wq', 'L0_xattn_bq', 'L0_xattn_Wk', 'L0_xattn_bk', 'L0_xattn_Wv', 'L0_xattn_bv', 'L0_xattn_Wo',
        'L0_xattn_bo', 'L0_ffn_Wr', 'L0_ffn_W1', 'L0_ffn_W2']


def kernel(**inputs):
    import numpy as _np
    import concourse.bacc as _bacc
    from concourse import mybir as _mybir
    from concourse.bass_utils import run_bass_kernel_spmd as _run

    nc = _bacc.Bacc("TRN2", target_bir_lowering=False, num_devices=1)
    arrays, args = {}, []
    for name in _INS:
        a = _np.ascontiguousarray(inputs[name])
        arrays[f"in_{name}_dram"] = a
        args.append(nc.dram_tensor(f"in_{name}_dram", a.shape, _mybir.dt.from_np(a.dtype), kind="ExternalInput").ap())
    shape = inputs["x"].shape
    args.append(nc.dram_tensor("out_0_dram", shape, _mybir.dt.float32, kind="ExternalOutput").ap())
    decoder_layer(nc, *args)
    r = _run(nc, [arrays], core_ids=[0])
    return r.results[0]["out_0_dram"]
```
